# Optimizing a Trainium2 kernel written in Bass

```python
import numpy as np
import jax
import jax.numpy as jnp

def _softmax(x, axis=-1):
    return jax.nn.softmax(x, axis=axis)

def _gelu(x):
    return jax.nn.gelu(x, approximate=True)

def _silu(x):
    return jax.nn.silu(x)

def _sigmoid(x):
    return jax.nn.sigmoid(x)

def _layernorm(x, axis=-1, eps=1e-05):
    m = jnp.mean(x, axis=axis, keepdims=True)
    v = jnp.var(x, axis=axis, keepdims=True)
    return (x - m) / jnp.sqrt(v + eps)

def _scatter_add(tgt, idx, src, axis=0):
    return tgt.at[idx].add(src)

def _segment_sum(src, seg, n):
    return jax.ops.segment_sum(src, seg, n)
kernel_name = 'mk_adaln_d1_jaxref_r8_fc2da2'

def setup_inputs(seed: int=0):
    np.random.seed(seed)
    _w = jnp.asarray

    def _L0_attn_setup():
        import math
        import jax, jax.numpy as jnp
        import numpy as np
        N_HEADS = 16
        LOCAL_HEADS = 8
        GLOBAL_HEADS = N_HEADS - LOCAL_HEADS
        WINDOW = 32
        NEG_INF = -1e+30
        key = jax.random.key(seed)
        ks = jax.random.split(key, 6)
        B, S, E = (1, 512, 128)
        inp = {'hidden_states': jax.random.normal(ks[0], (B, S, E), dtype=jnp.float32), 'Wq': jax.random.normal(ks[1], (E, E), dtype=jnp.float32) * (1.0 / math.sqrt(E)), 'Wk': jax.random.normal(ks[2], (E, E), dtype=jnp.float32) * (1.0 / math.sqrt(E)), 'Wv': jax.random.normal(ks[3], (E, E), dtype=jnp.float32) * (1.0 / math.sqrt(E)), 'Wo': jax.random.normal(ks[4], (E, E), dtype=jnp.float32) * (1.0 / math.sqrt(E)), 'bo': jnp.zeros((E,), dtype=jnp.float32)}
        return inp
    _L0_attn_in = _L0_attn_setup()

    def _L0_ffn_setup():
        import jax, jax.numpy as jnp
        import numpy as np
        E = 16
        H = 128
        F = 256
        TOP_K = 1
        B, S = (2, 128)
        key = jax.random.key(seed)
        ks = jax.random.split(key, 7)
        s = 0.02
        return {'hidden_states': jax.random.normal(ks[0], (B, S, H), jnp.float32), 'w_router': jax.random.normal(ks[1], (E, H), jnp.float32) * s, 'gate_up_proj': jax.random.normal(ks[2], (E, H, 2 * F), jnp.float32) * s, 'down_proj': jax.random.normal(ks[3], (E, F, H), jnp.float32) * s, 'w_gate': jax.random.normal(ks[4], (F, H), jnp.float32) * s, 'w_up': jax.random.normal(ks[5], (F, H), jnp.float32) * s, 'w_down': jax.random.normal(ks[6], (H, F), jnp.float32) * s}
    _L0_ffn_in = _L0_ffn_setup()
    _L0_c = _w((lambda *s: np.random.randn(*s).astype(np.float32) * 0.05)(4, 128))
    _L0_wmod = _w((lambda *s: np.random.randn(*s).astype(np.float32) * 0.05)(128, 6 * 128) * 128 ** (-0.5))
    _d = {'L0_attn_hidden_states': _L0_attn_in['hidden_states'], 'L0_attn_Wq': _L0_attn_in['Wq'], 'L0_attn_Wk': _L0_attn_in['Wk'], 'L0_attn_Wv': _L0_attn_in['Wv'], 'L0_attn_Wo': _L0_attn_in['Wo'], 'L0_attn_bo': _L0_attn_in['bo'], 'L0_ffn_w_router': _L0_ffn_in['w_router'], 'L0_ffn_gate_up_proj': _L0_ffn_in['gate_up_proj'], 'L0_ffn_down_proj': _L0_ffn_in['down_proj'], 'L0_ffn_w_gate': _L0_ffn_in['w_gate'], 'L0_ffn_w_up': _L0_ffn_in['w_up'], 'L0_ffn_w_down': _L0_ffn_in['w_down'], 'L0_c': _L0_c, 'L0_wmod': _L0_wmod}
    _x0 = _d['L0_attn_hidden_states']
    _d['L0_attn_hidden_states'] = jax.random.normal(jax.random.fold_in(jax.random.key(seed), 1), (4, 1024, 128), dtype=_x0.dtype)
    del _x0
    return _d

def reference(L0_attn_hidden_states, L0_attn_Wq, L0_attn_Wk, L0_attn_Wv, L0_attn_Wo, L0_attn_bo, L0_ffn_w_router, L0_ffn_gate_up_proj, L0_ffn_down_proj, L0_ffn_w_gate, L0_ffn_w_up, L0_ffn_w_down, L0_c, L0_wmod):

    def _L0_attn_ref(hidden_states, Wq, Wk, Wv, Wo, bo):
        import math
        import jax, jax.numpy as jnp
        import numpy as np
        N_HEADS = 16
        LOCAL_HEADS = 8
        GLOBAL_HEADS = N_HEADS - LOCAL_HEADS
        WINDOW = 32
        NEG_INF = -1e+30
        B, S, E = hidden_states.shape
        H, D = (N_HEADS, E // N_HEADS)
        scale = 1.0 / math.sqrt(D)

        def proj(W):
            y = jnp.einsum('bse,fe->bsf', hidden_states, W)
            return y.reshape(B, S, H, D).transpose(0, 2, 1, 3)
        q = proj(Wq) * scale
        k = proj(Wk)
        v = proj(Wv)
        i = jnp.arange(S)[:, None]
        j = jnp.arange(S)[None, :]
        causal = j <= i
        local = causal & (j >= i - WINDOW)

        def attend(qh, kh, vh, mask):
            scores = jnp.einsum('bhsd,bhtd->bhst', qh, kh)
            scores = jnp.where(mask, scores, NEG_INF)
            w = jax.nn.softmax(scores, axis=-1)
            return jnp.einsum('bhst,bhtd->bhsd', w, vh)
        out_g = attend(q[:, :GLOBAL_HEADS], k[:, :GLOBAL_HEADS], v[:, :GLOBAL_HEADS], causal)
        out_l = attend(q[:, GLOBAL_HEADS:], k[:, GLOBAL_HEADS:], v[:, GLOBAL_HEADS:], local)
        attn = jnp.concatenate([out_g, out_l], axis=1)
        attn = attn.transpose(0, 2, 1, 3).reshape(B, S, E)
        return jnp.einsum('bse,fe->bsf', attn, Wo) + bo

    def _L0_ffn_ref(hidden_states, w_router, gate_up_proj, down_proj, w_gate, w_up, w_down):
        import jax, jax.numpy as jnp
        import numpy as np
        E = 16
        H = 128
        F = 256
        TOP_K = 1
        B, S = (2, 128)
        b, s, h = hidden_states.shape
        x = hidden_states.reshape(-1, h)
        logits = x @ w_router.T
        _, top_idx = jax.lax.top_k(logits, TOP_K)
        mask = jax.nn.one_hot(top_idx, E, dtype=logits.dtype).sum(axis=1)
        scores = jax.nn.sigmoid(logits) * mask
        masked_inputs = scores.T[:, :, None] * x[None, :, :]
        gate_up = jnp.einsum('eth,ehf->etf', masked_inputs, gate_up_proj)
        gate, up = jnp.split(gate_up, 2, axis=-1)
        expert_out = jnp.einsum('etf,efh->eth', up * jax.nn.silu(gate), down_proj)
        shared = jax.nn.silu(x @ w_gate.T) * (x @ w_up.T) @ w_down.T
        out = shared + expert_out.sum(axis=0)
        return out.reshape(b, s, h)
    x = L0_attn_hidden_states
    mod = (_silu(L0_c) @ L0_wmod).reshape(L0_c.shape[0], 6, 1, -1)
    sa, ca, ga, sb, cb, gb = (mod[:, 0], mod[:, 1], mod[:, 2], mod[:, 3], mod[:, 4], mod[:, 5])
    ga = (2 * (ga >= 0) - 1) * jnp.maximum(jnp.abs(ga), 0.25)
    gb = (2 * (gb >= 0) - 1) * jnp.maximum(jnp.abs(gb), 0.25)
    h = _layernorm(x, axis=-1) * (1 + ca) + sa
    x = x + ga * _L0_attn_ref(h, L0_attn_Wq, L0_attn_Wk, L0_attn_Wv, L0_attn_Wo, L0_attn_bo)
    h = _layernorm(x, axis=-1) * (1 + cb) + sb
    x = x + gb * _L0_ffn_ref(h, L0_ffn_w_router, L0_ffn_gate_up_proj, L0_ffn_down_proj, L0_ffn_w_gate, L0_ffn_w_up, L0_ffn_w_down)
    return x

_drawn_inputs = setup_inputs


def setup_inputs(seed=0):
    import zlib

    import numpy as np

    out = dict(_drawn_inputs(seed))
    spreads = {'L0_attn_bo': (0.0, 0.324)}
    factors = {'L0_ffn_w_router': 8.0,
     'L0_ffn_gate_up_proj': 8.0,
     'L0_ffn_down_proj': 8.0,
     'L0_ffn_w_gate': 8.0,
     'L0_ffn_w_up': 8.0,
     'L0_ffn_w_down': 8.0}
    for name, (base, spread) in spreads.items():
        noise = np.random.default_rng([zlib.crc32(name.encode()), seed]).standard_normal(out[name].shape)
        drawn = base * np.exp(spread * noise) if base else spread * noise
        out[name] = jnp.asarray(drawn.astype(out[name].dtype))
    for name, factor in factors.items():
        out[name] = (out[name] * factor).astype(out[name].dtype)
    return out
```

```python
from contextlib import ExitStack

import concourse.bass as bass
from concourse import mybir

F32 = mybir.dt.float32
BF16 = mybir.dt.bfloat16
I32 = mybir.dt.int32
ALU = mybir.AluOpType
ACT = mybir.ActivationFunctionType
AX = mybir.AxisListType

P = 128
B, S, E = 4, 1024, 128
TPB = S // P
NT = B * TPB
H, D, WINDOW = 16, 8, 32
SCALE = D ** -0.5
NEG = -1e30
EPS = 1e-5
NE, F = 16, 256
NPART = 3
KS = NPART * NPART * D
KM = KS + NPART
VW = D + 1
UH = 8
NU = 2
BAND = P + WINDOW
ET = NT + NE
HALF = 512


def adaln_kernel(nc, x, wqT, wkT, wvT, woT, bo, wrT, gate_up, down, wgT, wuT, wdT, cT, wmod, out):
    ctx = ExitStack()
    with ctx:
        def sb(name, shape, dt=F32):
            return ctx.enter_context(nc.sbuf_tensor(name, shape, dt))

        def sem(name):
            return ctx.enter_context(nc.semaphore(name))

        psum = ctx.enter_context(nc.psum_tensor("psum", [P, 8, HALF], F32))
        q_parts_d = nc.dram_tensor("q_parts_d", [H, NPART, D, B * S], BF16, kind="Internal").ap()
        k_parts_d = nc.dram_tensor("k_parts_d", [H, NPART, D, B * S], BF16, kind="Internal").ap()
        v_d = nc.dram_tensor("v_d", [B, P, TPB * H * VW], F32, kind="Internal").ap()

        x_sb = sb("x_sb", [P, NT, E])
        ident = sb("ident", [P, P])
        identb = sb("identb", [P, P], BF16)
        mask_qk = sb("mask_qk", [P, P], BF16)
        mask_kq = sb("mask_kq", [P, P], BF16)
        mask_lq = sb("mask_lq", [P, TPB, 2 * WINDOW], BF16)
        mask_lk = sb("mask_lk", [P, 2, BAND], BF16)
        mod_cols = sb("mod_cols", [P, 4, B])
        mod_rows = sb("mod_rows", [P, B, 4, E])
        attn_sb = sb("attn_sb", [P, NT, E])
        work = sb("work", [P, 29000])

        setup(nc, sem, psum, work, x, x_sb, wqT, wkT, wvT, bo, cT, wmod, ident, identb, mask_qk, mask_kq,
              mask_lq, mask_lk, mod_cols, mod_rows, q_parts_d, k_parts_d, v_d)
        attention(nc, sem, psum, work, attn_sb, ident, identb, mask_qk, mask_kq, mask_lq, mask_lk, q_parts_d,
                  k_parts_d, v_d)
        sorted_d = nc.dram_tensor("sorted_d", [ET * P, E], F32, kind="Internal").ap()
        expert_d = nc.dram_tensor("expert_d", [ET * P, E], F32, kind="Internal").ap()
        feed_forward(nc, sem, psum, work, x_sb, attn_sb, ident, mod_cols, mod_rows, woT, wrT, gate_up, down, wgT,
                     wuT, wdT, sorted_d, expert_d, out)


def setup(nc, sem, psum, work, x, x_sb, wqT, wkT, wvT, bo, cT, wmod, ident, identb, mask_qk, mask_kq,
          mask_lq, mask_lk, mod_cols, mod_rows, q_parts_d, k_parts_d, v_d):
    at = [0]

    def part(n, dt=F32):
        a = work[:, at[0]:at[0] + n]
        at[0] += n
        return a

    wq_sb, wk_sb, wv_sb = part(E), part(E), part(E)
    wmod_sb = part(6 * E)
    bo_sb = part(E)
    c_sb, c_exp, c_silu = part(B), part(B), part(B)
    c_bc = part(B * P).rearrange("p (b m) -> p b m", b=B)
    sign = part(B * E).rearrange("p (b m) -> p b m", b=B)
    size = part(B * E).rearrange("p (b m) -> p b m", b=B)
    stats = part(TPB * 6).rearrange("p (t s) -> p t s", t=TPB)
    mv = part(TPB * 2).rearrange("p (t s) -> p t s", t=TPB)
    half_neg = part(TPB)
    ve = part(TPB)
    rstd = part(TPB)
    xn = part(TPB * E).rearrange("p (t e) -> p t e", t=TPB)
    hT = part(S)
    mod_b = part(2)
    rest = part(2 * S).rearrange("p (w s) -> p w s", w=2)
    q_parts = part(2 * NPART * S // 2).bitcast(BF16).rearrange("p (w i s) -> p w i s", w=2, i=NPART)
    v_sb = part(TPB * H * VW).rearrange("p (t h w) -> p t h w", t=TPB, h=H)

    s_wm, s_w, s_x, s_bo = sem("modulation_weights_in"), sem("projection_weights_in"), sem("x_in"), sem("bo_in")
    s_const, s_zero = sem("constants_made"), sem("constants_zeroed")
    s_cexp, s_c, s_cols, s_rows, s_rowsb = (sem("c_exp_done"), sem("c_steps"), sem("mod_cols_summed"),
                                            sem("mod_rows_summed"), sem("mod_rows_copied"))
    s_mod, s_gate = sem("mod_steps"), sem("gates_done")
    s_bo_added = sem("bo_added")
    s_ln, s_stat, s_ve, s_rstd, s_xn = sem("ln_steps"), sem("stats_done"), sem("ve_done"), sem("rstd_done"), sem("xn_done")
    s_xT, s_hT, s_modb = sem("x_transposed"), sem("hT_done"), sem("mod_b_copied")
    s_proj, s_p1, s_rest, s_p2, s_parts = (sem("projected"), sem("first_part_done"), sem("rest_done"),
                                           sem("second_part_done"), sem("parts_done"))
    s_vproj, s_v = sem("v_projected"), sem("v_copied")
    s_stored = sem("parts_stored")
    s_half = sem("constants_half")

    STORES = 16 * (2 * NPART + 1)

    with nc.Block() as block:
        @block.sync
        def _(sp):
            sp.sem_inc(s_stored, 16)
            sp.dma_start(c_sb, cT).then_inc(s_wm, 16)
            sp.dma_start(wmod_sb, wmod).then_inc(s_wm, 16)
            xv = x.rearrange("b (t p) e -> b p t e", p=P)
            for b in range(B):
                sp.dma_start(x_sb[:, b * TPB:(b + 1) * TPB, :], xv[b]).then_inc(s_x, 16)
            with sp.Fori(0, B) as b:
                sp.wait_ge(s_parts, b * 4 + 4)
                cols = bass.ds(b * S, S)
                for i in range(NPART):
                    sp.dma_start(q_parts_d[:, i, :, cols], q_parts[:, 0, i]).then_inc(s_stored, 16)
                    sp.dma_start(k_parts_d[:, i, :, cols], q_parts[:, 1, i]).then_inc(s_stored, 16)
                sp.wait_ge(s_v, b * 2 + 4)
                sp.dma_start(v_d[bass.ds(b, 1)].rearrange("o p n -> (o p) n"),
                             v_sb.rearrange("p t h w -> p (t h w)")).then_inc(s_stored, 16)
            sp.wait_ge(s_stored, B * STORES + 16)

        @block.gpsimd
        def _(pool):
            pool.dma_start(bo_sb, bo.partition_broadcast(P)).then_inc(s_bo, 16)
            pool.memset(ident[:, :], 0.0).then_inc(s_zero, 1)
            pool.memset(identb[:, :], 0.0).then_inc(s_zero, 1)
            pool.memset(mask_qk[:, :], 0.0).then_inc(s_zero, 1)
            pool.memset(mask_kq[:, :], 0.0).then_inc(s_zero, 1)
            pool.memset(mask_lq[:, :, :], 0.0).then_inc(s_zero, 1)
            pool.memset(mask_lk[:, :, :], 0.0).then_inc(s_zero, 1)
            pool.memset(half_neg, -0.5).then_inc(s_half, 1)
            pool.wait_ge(s_zero, 6)
            for m in (ident, identb):
                pool.affine_select(out=m[:, :], in_=m[:, :], compare_op=ALU.not_equal, fill=1.0, base=0,
                                   pattern=[[-1, P]], channel_multiplier=1).then_inc(s_const, 1)
            pool.affine_select(out=mask_qk[:, :], in_=mask_qk[:, :], compare_op=ALU.is_ge, fill=NEG, base=0,
                               pattern=[[-1, P]], channel_multiplier=1).then_inc(s_const, 1)
            pool.affine_select(out=mask_kq[:, :], in_=mask_kq[:, :], compare_op=ALU.is_ge, fill=NEG, base=0,
                               pattern=[[1, P]], channel_multiplier=-1).then_inc(s_const, 1)
            pool.wait_ge(s_const, 4)
            for j in range(P // WINDOW):
                rows = mask_lq[j * WINDOW:(j + 1) * WINDOW]
                pool.affine_select(out=rows, in_=rows, compare_op=ALU.is_ge, fill=NEG, base=0,
                                   pattern=[[0, TPB], [1, 2 * WINDOW]], channel_multiplier=-1).then_inc(s_const, 1)
                pool.wait_ge(s_const, 5 + 2 * j)
                pool.affine_select(out=rows, in_=rows, compare_op=ALU.is_ge, fill=NEG, base=WINDOW,
                                   pattern=[[0, TPB], [-1, 2 * WINDOW]], channel_multiplier=1).then_inc(s_const, 1)
                pool.wait_ge(s_const, 6 + 2 * j)
            pool.affine_select(out=mask_lk[:, :, :], in_=mask_lk[:, :, :], compare_op=ALU.is_ge, fill=NEG, base=0,
                               pattern=[[0, 2], [1, BAND]], channel_multiplier=-1).then_inc(s_const, 1)
            pool.wait_ge(s_const, 13)
            pool.affine_select(out=mask_lk[:, :, :], in_=mask_lk[:, :, :], compare_op=ALU.is_ge, fill=NEG, base=WINDOW,
                               pattern=[[0, 2], [-1, BAND]], channel_multiplier=1).then_inc(s_const, 1)
            pool.memset(mask_lq[0:WINDOW, 0, 0:WINDOW], NEG).then_inc(s_const, 1)
            pool.wait_ge(s_half, 1)
            with pool.Fori(0, B) as b:
                pool.wait_ge(s_ve, b + 1)
                pool.tensor_tensor(rstd, ve, half_neg, ALU.pow).then_inc(s_rstd, 1)
            pool.wait_ge(s_bo, 16)
            pool.wait_ge(s_gate, 2)
            pool.wait_ge(s_xn, B)
            for b in range(B):
                pool.tensor_tensor(size[:, b, :], mod_rows[:, b, 0, :], bo_sb, ALU.mult).then_inc(s_bo_added, 1)
            pool.wait_ge(s_bo_added, B)
            for b in range(B):
                xb = x_sb[:, b * TPB:(b + 1) * TPB, :]
                pool.tensor_tensor(xb, xb, size[:, b, :].unsqueeze(1).broadcast_to([P, TPB, E]),
                                   ALU.add).then_inc(s_bo_added, 1)

        @block.scalar
        def _(act):
            act.sem_inc(s_hT, 2)
            act.sem_inc(s_v, 2)
            act.dma_start(wq_sb, wqT).then_inc(s_w, 16)
            act.dma_start(wk_sb, wkT).then_inc(s_w, 16)
            act.dma_start(wv_sb, wvT).then_inc(s_w, 16)
            act.wait_ge(s_wm, 32)
            act.activation(c_exp, c_sb, ACT.Exp, scale=-1.0).then_inc(s_cexp, 1)
            for b in range(B):
                act.wait_ge(s_rows, b + 1)
                act.activation(mod_rows[:, b], psum[:, b, :].rearrange("p (j e) -> p j e", j=4),
                               ACT.Copy).then_inc(s_rowsb, 1)
            with act.Fori(0, B) as b:
                act.wait_ge(s_modb, b + 1)
                for c in range(2):
                    act.wait_ge(s_xT, b * 2 + c + 1)
                    if c == 0:
                        act.wait_ge(s_vproj, b * 2 + 2)
                    act.activation(hT[:, c * HALF:(c + 1) * HALF], psum[:, c, :], ACT.Identity,
                                   scale=mod_b[:, 1:2], bias=mod_b[:, 0:1]).then_inc(s_hT, 1)
                for w in range(2):
                    if w == 0:
                        act.wait_ge(s_stored, b * STORES + 16)
                    for c in range(2):
                        act.wait_ge(s_proj, b * 4 + w * 2 + c + 1)
                        act.activation(q_parts[:, w, 0, c * HALF:(c + 1) * HALF], psum[:, 2 + 2 * w + c, :], ACT.Copy,
                                       scale=SCALE if w == 0 else 1.0).then_inc(s_p1, 1)
                for c in range(2):
                    act.wait_ge(s_vproj, b * 2 + c + 3)
                    act.activation(v_sb[:, c * 4:(c + 1) * 4, :, 0:D],
                                   psum[:, 6 + c, :].rearrange("p (t h d) -> p t h d", t=4, h=H),
                                   ACT.Copy).then_inc(s_v, 1)

        @block.vector
        def _(dve):
            dve.sem_inc(s_rest, 4)
            dve.memset(v_sb, 1.0).then_inc(s_c, 1)
            dve.wait_ge(s_cexp, 1)
            dve.tensor_scalar(c_exp, c_exp, 1.0, None, ALU.add).then_inc(s_c, 1)
            dve.wait_ge(s_c, 2)
            dve.reciprocal(c_exp, c_exp).then_inc(s_c, 1)
            dve.wait_ge(s_c, 3)
            dve.tensor_tensor(c_silu, c_exp, c_sb, ALU.mult).then_inc(s_c, 1)
            dve.wait_ge(s_c, 4)
            dve.tensor_copy(c_bc, c_silu.unsqueeze(2).broadcast_to([P, B, P])).then_inc(s_c, 1)
            dve.wait_ge(s_cols, 1)
            dve.tensor_copy(mod_cols[:, :, :], psum[:, 4, 0:4 * B].rearrange("p (j b) -> p j b", j=4)).then_inc(s_mod, 1)
            dve.wait_ge(s_mod, 1)
            for j in (1, 3):
                dve.tensor_scalar(mod_cols[:, j, :], mod_cols[:, j, :], 1.0, None, ALU.add).then_inc(s_mod, 1)
            dve.wait_ge(s_rowsb, B)
            dve.tensor_scalar(mod_rows[:, :, 2, :], mod_rows[:, :, 2, :], 1.0, None, ALU.add).then_inc(s_mod, 1)
            n = 4
            for j in (0, 3):
                g = mod_rows[:, :, j, :]
                dve.tensor_scalar(sign, g, 0.0, 2.0, ALU.is_ge, ALU.mult).then_inc(s_mod, 1)
                dve.wait_ge(s_mod, n + 1)
                dve.tensor_scalar(sign, sign, 1.0, None, ALU.subtract).then_inc(s_mod, 1)
                dve.wait_ge(s_mod, n + 2)
                dve.tensor_tensor(size, g, sign, ALU.mult).then_inc(s_mod, 1)
                dve.wait_ge(s_mod, n + 3)
                n += 3
                dve.scalar_tensor_tensor(out=g, in0=size, scalar=0.25, in1=sign, op0=ALU.max,
                                         op1=ALU.mult).then_inc(s_gate, 1)
                dve.wait_ge(s_gate, 1 if j == 0 else 2)
            with dve.Fori(0, B) as b:
                dve.wait_ge(s_x, B * 16)
                for t in range(TPB):
                    dve.bn_stats(stats[:, t, :], x_sb[:, bass.ds(b * TPB + t, 1), :].rearrange("p o e -> p (o e)")).then_inc(s_stat, 1)
                dve.wait_ge(s_hT, b * 2 + 2)
                dve.wait_ge(s_stat, b * TPB + TPB)
                dve.tensor_copy(mod_b, mod_cols[:, 0:2, bass.ds(b, 1)].rearrange("p j o -> p (j o)")).then_inc(s_modb, 1)
                for t in range(TPB):
                    dve.bn_aggr(mv[:, t, :], stats[:, t, :]).then_inc(s_ln, 1)
                dve.wait_ge(s_ln, b * TPB + TPB)
                dve.tensor_scalar(ve, mv[:, :, 1], EPS, None, ALU.add).then_inc(s_ve, 1)
                dve.wait_ge(s_rstd, b + 1)
                for t in range(TPB):
                    n = dve.tensor_scalar(xn[:, t, :], x_sb[:, bass.ds(b * TPB + t, 1), :].rearrange("p o e -> p (o e)"),
                                          mv[:, t, 0:1], rstd[:, t:t + 1], ALU.subtract, ALU.mult)
                n.then_inc(s_xn, 1)
                for w in range(2):
                    for c in range(2):
                        n = w * 2 + c
                        cols = slice(c * HALF, (c + 1) * HALF)
                        dve.wait_ge(s_p1, b * 4 + n + 1)
                        dve.scalar_tensor_tensor(out=rest[:, w, cols], in0=psum[:, 2 + n, :],
                                                 scalar=SCALE if w == 0 else 1.0, in1=q_parts[:, w, 0, cols],
                                                 op0=ALU.mult, op1=ALU.subtract).then_inc(s_rest, 1)
                        dve.wait_ge(s_rest, b * 4 + n + 5)
                        dve.tensor_copy(q_parts[:, w, 1, cols], rest[:, w, cols]).then_inc(s_p2, 1)
                        dve.wait_ge(s_p2, b * 4 + n + 1)
                        dve.tensor_tensor(q_parts[:, w, 2, cols], rest[:, w, cols], q_parts[:, w, 1, cols],
                                          ALU.subtract).then_inc(s_parts, 1)

        @block.tensor
        def _(pe):
            pe.sem_inc(s_vproj, 2)
            pe.wait_ge(s_wm, 32)
            pe.wait_ge(s_c, 4)
            for n, j in enumerate((0, 1, 3, 4)):
                mm = pe.matmul(psum[:, 4, n * B:(n + 1) * B], wmod_sb[:, j * E:(j + 1) * E], c_silu, start=True, stop=True)
            mm.then_inc(s_cols, 1)
            pe.wait_ge(s_c, 5)
            for b in range(B):
                pe.matmul(psum[:, b, :], c_bc[:, b, :], wmod_sb[:, 2 * E:6 * E], start=True, stop=True).then_inc(s_rows, 1)
            pe.wait_ge(s_const, 1)
            pe.wait_ge(s_w, 48)
            pe.wait_ge(s_rowsb, B)
            pe.wait_ge(s_mod, 1)
            with pe.Fori(0, B) as b:
                pe.wait_ge(s_xn, b + 1)
                for c in range(2):
                    for t in range(4):
                        mm = pe.transpose(psum[:, c, t * P:(t + 1) * P], xn[:, c * 4 + t, :], ident[:, :])
                    mm.then_inc(s_xT, 1)
                for w, wt in enumerate((wq_sb, wk_sb)):
                    for c in range(2):
                        if w == 0:
                            pe.wait_ge(s_hT, b * 2 + c + 3)
                        pe.wait_ge(s_rest, b * 4 + 4)
                        pe.matmul(psum[:, 2 + 2 * w + c, :], wt, hT[:, c * HALF:(c + 1) * HALF],
                                  start=True, stop=True).then_inc(s_proj, 1)
                pe.wait_ge(s_v, b * 2 + 2)
                for c in range(2):
                    for t in range(4):
                        mm = pe.matmul(psum[:, 6 + c, t * P:(t + 1) * P], hT[:, (c * 4 + t) * P:(c * 4 + t + 1) * P],
                                       wv_sb, start=True, stop=True)
                    mm.then_inc(s_vproj, 1)



MAX_BANKS = [
    ([(0, 0, 128, 0), (4, 512, 128, 128)], (0, 8, 2)),
    ([(1, 0, 256, 0), (5, 512, 256, 256)], (1, 8, 2)),
    ([(2, 0, 384, 0)], (2, 1, 1)),
    ([(3, 0, 512, 0)], (3, 1, 1)),
    ([(4, 0, 512, 0)], (4, 1, 1)),
    ([(5, 0, 512, 0)], (5, 1, 1)),
    ([(6, 0, 512, 0)], (6, 1, 1)),
    ([(7, 0, 512, 0)], (7, 1, 1)),
    ([(6, 512, 384, 0)], (10, 1, 1)),
    ([(7, 512, 512, 0)], (11, 1, 1)),
]
G, L = 0, 1
STEPS = 2 * TPB
SCORES = 4 * 4 + 4 * 2 + TPB
RING_A = 4 * len(MAX_BANKS) + 4 + 2
RING_B = 4
RING = RING_A + RING_B


def max_steps():
    return ([("max_g", h, n) for h in range(4) for n in range(len(MAX_BANKS))] + [("turn_m", G)],
            [("max_l", h) for h in range(4)] + [("turn_m", L)])


def slot_steps(with_next):
    ahead, of_l = max_steps() if with_next else ([], [])
    turn_g = ahead[-1:]
    ahead = ahead[:-1]
    steps = []

    def more(n):
        steps.extend(ahead[:n])
        del ahead[:n]

    for kb in range(TPB):
        parts = 4 if kb < 4 else 2
        share = [8, 7, 6, 5, 4, 3, 2, 1][kb]
        for part in range(parts):
            steps.append(("score_g", kb, part))
            more(share * (part + 1) // parts - share * part // parts)
            if part == 1 and kb:
                steps.append(("weigh_g", kb - 1))
    for kt in range(TPB):
        steps.append(("score_l", kt))
        if kt == 0:
            steps += [("weigh_g", TPB - 1), ("out", G)]
        else:
            steps.append(("weigh_l", kt - 1))
        more(1)
        if kt == 2:
            steps += [("turn_o", G, 0), ("turn_o", G, 1)]
        if kt == 4:
            steps += turn_g
        if kt >= 5:
            steps += of_l[:1]
            del of_l[:1]
    steps += [("weigh_l", TPB - 1), ("out", L)]
    steps += of_l
    steps += [("turn_o", L, 0), ("turn_o", L, 1)]
    assert not ahead
    return steps


def attention(nc, sem, psum, work, attn_sb, ident, identb, mask_qk, mask_kq, mask_lq, mask_lk, q_parts_d,
              k_parts_d, v_d):
    at = [0]

    def part(n, dt=F32):
        a = work[:, at[0]:at[0] + n]
        at[0] += n
        return a

    q_rep, k_rep, v_u = [], [], []
    for u in range(NU):
        q_rep.append(part(UH * S // 2).bitcast(BF16).rearrange("p (h s) -> p h s", h=UH))
        k_rep.append(part(UH * S // 2).bitcast(BF16).rearrange("p (h s) -> p h s", h=UH))
        v_u.append(part(TPB * UH * VW).rearrange("p (t h w) -> p t h w", t=TPB, h=UH))
    probs = [part(4 * S).rearrange("p (h s) -> p h s", h=4) for _ in range(2)]
    o_sb = part(S)
    maxima = [part(4 * 12).rearrange("p (h n) -> p h n", h=4) for _ in (G, L)]
    left = [part(4 * TPB).rearrange("p (h t) -> p h t", h=4) for _ in (G, L)]
    m_parts = [part(NPART * 4 * TPB // 2).bitcast(BF16).rearrange("p (i h t) -> p i h t", i=NPART, h=4) for _ in (G, L)]
    zero = part(4 * TPB).rearrange("p (h t) -> p h t", h=4)
    m_rows = [part(P // 2).bitcast(BF16) for _ in (G, L)]
    inv = [part(16).rearrange("p (t h) -> p t h", t=4) for _ in range(2)]

    s_init = sem("attention_memory_set")
    s_load = [[sem(f"unit{u}_global_heads_in"), sem(f"unit{u}_local_heads_in")] for u in range(NU)]
    s_score, s_exp = sem("scores_ready"), sem("score_buffers_free")
    s_ring, s_ring_free = sem("ring_filled"), sem("ring_banks_free")
    s_weigh = sem("weighed")
    s_out_free = sem("outputs_copied")
    s_max = [sem("global_maxima_ready"), sem("local_maxima_ready")]
    s_pairs = sem("maxima_paired")
    s_zero = sem("zeros_made")
    s_split = sem("maxima_split_steps")
    s_mparts = [sem("global_maxima_split"), sem("local_maxima_split")]
    s_mrows = [sem("global_max_rows_ready"), sem("local_max_rows_ready")]
    s_m = [sem("global_max_rows_in"), sem("local_max_rows_in")]
    s_inv, s_attn = sem("sums_inverted"), sem("attention_written")
    LOADS = 16 * 9
    ROWS = 16 * NPART

    def over_slots(eng, slot):
        with eng.Fori(0, B - 1) as b:
            for u in range(NU):
                slot(b, u, b * NU + u, True)
        for u in range(NU):
            slot(B - 1, u, (B - 1) * NU + u, u < NU - 1)

    with nc.Block() as block:
        @block.sync
        def _(sp):
            def load(b, u, quad):
                h0, to = 4 * (u + NU * quad), slice(4 * quad, 4 * quad + 4)
                cols = bass.ds(b * S, S)

                def parts(of, i0, i1):
                    return of[h0:h0 + 4, i0:i1, :, cols].rearrange("h i d s -> (i d) h s")

                for r in range(NPART):
                    row = r * NPART * D
                    sp.dma_start(q_rep[u][row:row + NPART * D, to, :], parts(q_parts_d, 0, NPART)).then_inc(s_load[u][quad], 16)
                    cut = row + (NPART - r) * D
                    sp.dma_start(k_rep[u][row:cut, to, :], parts(k_parts_d, r, NPART)).then_inc(s_load[u][quad], 16)
                    if r:
                        sp.dma_start(k_rep[u][cut:row + NPART * D, to, :], parts(k_parts_d, 0, r)).then_inc(s_load[u][quad], 16)
                vals = v_d[bass.ds(b, 1)].rearrange("o p (t h w) -> (o p) t h w", t=TPB, h=H)
                sp.dma_start(v_u[u][:, :, to, :], vals[:, :, h0:h0 + 4, :]).then_inc(s_load[u][quad], 16)

            def rows(u, quad, unit):
                sp.wait_ge(s_mrows[quad], unit + 1)
                for i in range(NPART):
                    sp.dma_start(q_rep[u][KS + i:KS + i + 1, 4 * quad:4 * quad + 4, :],
                                 m_rows[quad][i * 4 * TPB:(i + 1) * 4 * TPB, :]).then_inc(s_m[quad], 16)

            sp.wait_ge(s_init, 3)
            for u in range(NU):
                for quad in (G, L):
                    load(0, u, quad)
            for quad in (G, L):
                rows(0, quad, 0)

            def slot(b, u, s, more):
                if not isinstance(b, int):
                    sp.wait_ge(s_weigh, s * STEPS + TPB + 2)
                    load(b + 1, u, G)
                if more:
                    rows(1 - u, G, s + 1)
                if not isinstance(b, int):
                    sp.wait_ge(s_weigh, s * STEPS + STEPS + 2)
                    load(b + 1, u, L)
                if more:
                    rows(1 - u, L, s + 1)

            over_slots(sp, slot)
            for quad in (G, L):
                sp.wait_ge(s_m[quad], B * NU * ROWS)

        @block.gpsimd
        def _(pool):
            def split(quad, unit):
                pool.wait_ge(s_max[quad], unit + 1)
                m = maxima[quad][:, :, 0:TPB]
                n = unit * 8 + quad * 4
                pool.tensor_tensor(m_parts[quad][:, 0], zero, m, ALU.subtract).then_inc(s_split, 1)
                pool.wait_ge(s_split, n + 1)
                pool.tensor_tensor(left[quad], m, m_parts[quad][:, 0], ALU.add).then_inc(s_split, 1)
                pool.wait_ge(s_split, n + 2)
                pool.tensor_tensor(m_parts[quad][:, 1], zero, left[quad], ALU.subtract).then_inc(s_split, 1)
                pool.wait_ge(s_split, n + 3)
                pool.tensor_tensor(left[quad], left[quad], m_parts[quad][:, 1], ALU.add).then_inc(s_split, 1)
                pool.wait_ge(s_split, n + 4)
                pool.tensor_tensor(m_parts[quad][:, 2], zero, left[quad], ALU.subtract).then_inc(s_mparts[quad], 1)

            pool.memset(zero, 0.0).then_inc(s_zero, 1)
            pool.wait_ge(s_zero, 1)
            with pool.Fori(0, B * NU) as unit:
                split(G, unit)
                split(L, unit)

        @block.scalar
        def _(act):
            act.sem_inc(s_exp, 2)
            act.sem_inc(s_out_free, 1)

            def slot(b, u, s, more):
                n = r = turned = 0
                for step in slot_steps(more):
                    if step[0] in ("max_g", "max_l", "turn_m", "turn_o"):
                        r += 1
                        turned = r if step[0] == "turn_o" else turned
                    elif step[0] in ("score_g", "score_l"):
                        kt = step[1] + (TPB if step[0] == "score_l" else 0)
                        to = probs[kt % 2]
                        bank = 2 * (n % 2)
                        act.wait_ge(s_score, s * SCORES + n + 1)
                        first = step[0] == "score_l" or step[2] == 0
                        if first:
                            act.wait_ge(s_weigh, s * STEPS + kt + 1)
                        if step[0] == "score_l":
                            dst = to[:, :, 0:BAND].rearrange("p (a c) q -> p a c q", a=2)
                            src = psum[:, bank:bank + 2, 0:2 * BAND].rearrange("p a (c q) -> p a c q", c=2)
                        elif step[1] < 4:
                            cols = S - step[1] * P
                            dst = to[:, step[2], 0:cols]
                            src = psum[:, bank:bank + 2, :].rearrange("p a q -> p (a q)")[:, 0:cols]
                        else:
                            cols = S - step[1] * P
                            dst = to[:, 2 * step[2]:2 * step[2] + 2, 0:cols]
                            src = psum[:, bank:bank + 2, 0:cols]
                        act.activation(dst, src, ACT.Exp).then_inc(s_exp, 1)
                        n += 1
                    elif step[0] == "out":
                        act.wait_ge(s_weigh, s * STEPS + (step[1] + 1) * TPB + 2)
                        act.wait_ge(s_ring, RING_A + s * RING + turned)
                        act.activation(o_sb, psum[:, 6:8, :].rearrange("p a q -> p (a q)"), ACT.Copy).then_inc(s_out_free, 1)

            over_slots(act, slot)

        @block.vector
        def _(dve):
            dve.memset(psum[:, 6:8, :], 0.0).then_inc(s_init, 1)
            for u in range(NU):
                dve.memset(k_rep[u][64:96, :, :], 1.0).then_inc(s_init, 1)
            dve.sem_inc(s_ring_free, 2)

            def run(step, u, s, n, pair):
                kind = step[0]
                bank = psum[:, 4 + pair]
                dve.wait_ge(s_ring, n + 1)
                if kind == "max_g":
                    _, h, i = step
                    pieces, (first, by, count) = MAX_BANKS[i]
                    cols = pieces[0][2]
                    dve.tensor_reduce(maxima[G][:, h, first:first + by * (count - 1) + 1:by],
                                      bank[:, 0:count * cols].rearrange("p (c k) -> p c k", c=count), AX.X,
                                      ALU.max).then_inc(s_ring_free, 1)
                elif kind == "max_l":
                    _, h = step
                    dve.tensor_reduce(maxima[L][:, h, 0:TPB], bank.rearrange("p (t k) -> p t k", t=TPB), AX.X,
                                      ALU.max).then_inc(s_ring_free, 1)
                elif kind == "turn_m":
                    quad = step[1]
                    if s is not None:
                        dve.wait_ge(s_m[quad], (s + 1) * ROWS)
                    dve.tensor_copy(m_rows[quad][0:96, :], bank.bitcast(BF16)[0:96, 0:P]).then_inc(s_mrows[quad], 1)
                    dve.wait_ge(s_mrows[quad], 1 if s is None else s + 2)
                    dve.sem_inc(s_ring_free, 1)
            def after(step, s, n):
                if step == ("max_g", 3, len(MAX_BANKS) - 1):
                    dve.wait_ge(s_ring_free, n + 3)
                    m = maxima[G]
                    dve.tensor_tensor(m[:, :, 4:8], m[:, :, 4:8], m[:, :, 8:12], ALU.max).then_inc(s_max[G], 1)
                elif step == ("max_l", 3):
                    dve.wait_ge(s_ring_free, n + 3)
                    dve.sem_inc(s_max[L], 1)

            n = 0
            for step in sum(max_steps(), []):
                run(step, None, None, n, n % 2)
                after(step, None, n)
                n += 1

            def slot(b, u, s, more):
                n = 0
                for step in slot_steps(more):
                    if step[0] in ("max_g", "max_l", "turn_m"):
                        run(step, u, s, RING_A + s * RING + n, n % 2)
                        after(step, s, RING_A + s * RING + n)
                        n += 1
                    elif step[0] == "turn_o":
                        _, quad, c = step
                        h0 = 4 * (u + NU * quad)
                        bank = psum[:, 4 + n % 2].rearrange("p (t h w) -> p t h w", t=4, h=4)
                        k = s * 4 + quad * 2 + c
                        dve.wait_ge(s_ring, RING_A + s * RING + n + 1)
                        dve.reciprocal(inv[c], bank[:, :, :, D]).then_inc(s_inv, 1)
                        dve.wait_ge(s_inv, k + 1)
                        dve.tensor_tensor(
                            attn_sb[:, bass.ds(b * TPB + 4 * c, 4), h0 * D:(h0 + 4) * D].rearrange("p t (h d) -> p t h d", h=4),
                            bank[:, :, :, 0:D], inv[c].unsqueeze(3).broadcast_to([P, 4, 4, D]),
                            ALU.mult).then_inc(s_ring_free, 1)
                        n += 1

            over_slots(dve, slot)

        @block.tensor
        def _(pe):
            def ring_bank(n, pair):
                pe.wait_ge(s_ring_free, n + 1)
                return psum[:, 4 + pair]

            def run(step, u, batch, unit, n, pair):
                kind = step[0]
                if step == ("max_g", 0, 0):
                    pe.wait_ge(s_load[u][G], (batch + 1) * LOADS)
                if step == ("max_l", 0):
                    pe.wait_ge(s_load[u][L], (batch + 1) * LOADS)
                if kind == "turn_m":
                    quad = step[1]
                    pe.wait_ge(s_mparts[quad], unit + 1)
                    bank = ring_bank(n, pair)
                    pe.transpose(bank.bitcast(BF16)[0:96, 0:P], m_parts[quad].rearrange("p i h t -> p (i h t)"),
                                 identb[:, :]).then_inc(s_ring, 1)
                    return
                bank = ring_bank(n, pair)
                if kind == "max_g":
                    _, h, i = step
                    for qt, k0, cols, to in MAX_BANKS[i][0]:
                        last = k0 + cols == (qt + 1) * P
                        mm = pe.matmul(bank[:, to:to + cols], q_rep[u][0:KS, h, qt * P:(qt + 1) * P],
                                       k_rep[u][0:KS, h, k0:k0 + cols], start=True, stop=not last)
                        if last:
                            mm = pe.matmul(bank[:, to + cols - P:to + cols], identb[:, :], mask_qk[:, :],
                                           start=False, stop=True)
                else:
                    _, h = step
                    pe.matmul(bank, identb[:, :], mask_lq[:, :, :].rearrange("p t k -> p (t k)"), start=True, stop=False,
                              skip_group_check=True)
                    for t in range(TPB):
                        for j in range(P // WINDOW):
                            q0 = t * P + j * WINDOW
                            k0 = max(q0 - WINDOW, 0)
                            c0 = t * 2 * WINDOW + k0 - (q0 - WINDOW)
                            cols = q0 + WINDOW - k0
                            mm = pe.matmul(bank[j * WINDOW:(j + 1) * WINDOW, c0:c0 + cols],
                                           q_rep[u][0:KS, 4 + h, q0:q0 + WINDOW], k_rep[u][0:KS, 4 + h, k0:k0 + cols],
                                           start=False, stop=True, skip_group_check=True)
                mm.then_inc(s_ring, 1)

            pe.sem_inc(s_weigh, 2)
            pe.wait_ge(s_init, 3)
            n = 0
            for step in sum(max_steps(), []):
                run(step, 0, 0, 0, n, n % 2)
                n += 1

            def slot(b, u, s, more):
                n = r = 0
                for step in slot_steps(more):
                    kind = step[0]
                    if kind == "score_g":
                        _, kb, i = step
                        if kb == 0 and i == 0:
                            pe.wait_ge(s_m[G], (s + 1) * ROWS)
                        pe.wait_ge(s_exp, s * SCORES + n + 1)
                        cols = S - kb * P
                        for h in ([i] if kb < 4 else [2 * i, 2 * i + 1]):
                            for c0 in range(0, cols, HALF):
                                bank = 2 * (n % 2) + (c0 // HALF if kb < 4 else h % 2)
                                w = min(HALF, cols - c0)
                                mm = pe.matmul(psum[:, bank, 0:w], k_rep[u][0:KM, h, kb * P:(kb + 1) * P],
                                               q_rep[u][0:KM, h, kb * P + c0:kb * P + c0 + w],
                                               start=True, stop=c0 > 0)
                                if c0 == 0:
                                    mm = pe.matmul(psum[:, bank, 0:P], identb[:, :], mask_kq[:, :], start=False, stop=True)
                        mm.then_inc(s_score, 1)
                        n += 1
                    elif kind == "score_l":
                        kt = step[1]
                        if kt == 0:
                            pe.wait_ge(s_m[L], (s + 1) * ROWS)
                        pe.wait_ge(s_exp, s * SCORES + n + 1)
                        w = min(BAND, S - kt * P)
                        for a in range(2):
                            bank = 2 * (n % 2) + a
                            pe.matmul(psum[:, bank, 0:2 * BAND], identb[:, :],
                                      mask_lk[:, :, :].rearrange("p c q -> p (c q)"), start=True, stop=False,
                                      skip_group_check=True)
                            for c in range(2):
                                h = 4 + 2 * a + c
                                mm = pe.matmul(psum[:, bank, c * BAND:c * BAND + w], k_rep[u][0:KM, h, kt * P:(kt + 1) * P],
                                               q_rep[u][0:KM, h, kt * P:kt * P + w], start=False, stop=True,
                                               skip_group_check=True)
                        mm.then_inc(s_score, 1)
                        n += 1
                    elif kind == "weigh_g":
                        kb = step[1]
                        done = (4 * (kb + 1) if kb < 4 else 16 + 2 * (kb - 3))
                        pe.wait_ge(s_exp, s * SCORES + done + 2)
                        if kb == 0:
                            pe.wait_ge(s_out_free, s * 2 + 1)
                        for half in range(2):
                            q0 = max(kb * P, half * HALF)
                            w = (half + 1) * HALF - q0
                            if w <= 0:
                                continue
                            for h in range(4):
                                mm = pe.matmul(psum[32 * h:32 * h + VW, 6 + half, q0 - half * HALF:HALF], v_u[u][:, kb, h, :],
                                               probs[kb % 2][:, h, q0 - kb * P:q0 - kb * P + w], start=kb == 0,
                                               stop=kb == (3 if half == 0 else 7), skip_group_check=True)
                        mm.then_inc(s_weigh, 1)
                    elif kind == "weigh_l":
                        kt = step[1]
                        pe.wait_ge(s_exp, s * SCORES + 24 + kt + 1 + 2)
                        if kt == 0:
                            pe.wait_ge(s_out_free, s * 2 + 2)
                        end = min(kt * P + BAND, S)
                        for half in range(2):
                            q0, q1 = max(kt * P, half * HALF), min(end, (half + 1) * HALF)
                            if q1 <= q0:
                                continue
                            first = kt == 0 or (half == 1 and kt == 3)
                            for h in range(4):
                                mm = pe.matmul(psum[32 * h:32 * h + VW, 6 + half, q0 - half * HALF:q1 - half * HALF],
                                               v_u[u][:, kt, 4 + h, :], probs[kt % 2][:, h, q0 - kt * P:q1 - kt * P],
                                               start=first, stop=True, skip_group_check=True)
                        mm.then_inc(s_weigh, 1)
                    elif kind == "turn_o":
                        _, quad, c = step
                        pe.wait_ge(s_out_free, s * 2 + quad + 2)
                        bank = ring_bank(RING_A + s * RING + r, r % 2)
                        for t in range(4):
                            mm = pe.transpose(bank[:, t * P:(t + 1) * P], o_sb[:, (4 * c + t) * P:(4 * c + t + 1) * P], ident[:, :])
                        mm.then_inc(s_ring, 1)
                        r += 1
                    elif kind in ("max_g", "max_l", "turn_m"):
                        run(step, 1 - u, b + u, s + 1, RING_A + s * RING + r, r % 2)
                        r += 1

            over_slots(pe, slot)



def feed_forward(nc, sem, psum, work, x_sb, attn_sb, ident, mod_cols, mod_rows, woT, wrT, gate_up, down, wgT,
                 wuT, wdT, sorted_d, expert_d, out):
    at = [0]

    def part(n, dt=F32):
        a = work[:, at[0]:at[0] + n]
        at[0] += n
        return a

    wo_sb, wr_sb = part(E), part(NE)
    wg_sb, wu_sb = part(F), part(F)
    wd_sb = part(2 * E).rearrange("p (c e) -> p c e", c=2)
    gu_sb = part(NE * 2 * F)
    dn_sb = part(NE * 2 * E)
    stage, attnT, xn, h2T, tmp = part(HALF), part(HALF), part(HALF), part(HALF), part(HALF)
    silu = part(2 * HALF).rearrange("p (c s) -> p c s", c=2)
    act_s = part(2 * HALF).rearrange("p (c s) -> p c s", c=2)
    stats = part(4 * 6).rearrange("p (t s) -> p t s", t=4)
    mv = part(4 * 2).rearrange("p (t s) -> p t s", t=4)
    half_neg, ve, rstd, mod_b = part(4), part(4), part(4), part(2)
    x2 = part(HALF).rearrange("p (t e) -> p t e", t=4)
    h2m, cb_row = part(HALF), part(E)
    logits = part(NT * NE).rearrange("p (t e) -> p t e", t=NT)
    zeros = part(8 * E)
    top, gate_of, best, pos_f, pos = part(NT), part(NT), part(NT), part(NT), part(NT).bitcast(I32)
    pick = part(NT * NE).rearrange("p (t e) -> p t e", t=NT)
    pick_b = part(NT * NE // 2).bitcast(BF16).rearrange("p (t e) -> p t e", t=NT)
    lower = part(NE)
    steps_of = part(NT)
    tri16 = part(NE * NE).rearrange("p (e f) -> p e f", e=NE)
    before = part(P // 2).bitcast(BF16)
    ones = part(P // 2).bitcast(BF16)
    slots = part(ET)
    count, tiles, ends, starts = part(NE), part(NE), part(NE), part(NE)
    cmp = part(ET * NE)
    expert_f = part(ET)
    expert = part(ET).bitcast(I32)
    h_in = [part(P) for _ in range(2)]
    h_inT = [part(P) for _ in range(2)]
    w_gu = [part(2 * F) for _ in range(2)]
    w_dn = [part(2 * E) for _ in range(2)]
    silu_e = [part(2 * P) for _ in range(2)]
    act_e = [part(2 * P) for _ in range(2)]
    y_out = [part(P) for _ in range(2)]

    dense(nc, sem, psum, x_sb, attn_sb, ident, mod_cols, mod_rows, woT, wrT, gate_up, down, wgT, wuT, wdT, sorted_d,
          wo_sb, wr_sb, wg_sb, wu_sb, wd_sb, gu_sb, dn_sb, stage, attnT, xn, h2T, tmp, silu, act_s, stats, mv,
          half_neg, ve, rstd, mod_b, logits, zeros, x2, h2m, cb_row)
    route(nc, sem, psum, attn_sb, sorted_d, logits, top, gate_of, best, pos_f, pos, pick, pick_b, lower, steps_of,
          tri16, before, ones, slots, count, tiles, ends, starts, cmp, expert_f, expert)
    experts(nc, sem, psum, ident, sorted_d, expert_d, gu_sb, dn_sb, expert, h_in, h_inT, w_gu, w_dn, silu_e, act_e, y_out)
    combine(nc, sem, x_sb, attn_sb, mod_rows, pos, expert_d, out)


def dense(nc, sem, psum, x_sb, attn_sb, ident, mod_cols, mod_rows, woT, wrT, gate_up, down, wgT, wuT, wdT, sorted_d,
          wo_sb, wr_sb, wg_sb, wu_sb, wd_sb, gu_sb, dn_sb, stage, attnT, xn, h2T, tmp, silu, act_s, stats, mv,
          half_neg, ve, rstd, mod_b, logits, zeros, x2, h2m, cb_row):
    s_w, s_ew = sem("dense_weights_in"), sem("expert_weights_in")
    s_zero, s_zeroed = sem("dense_zeros_made"), sem("sorted_rows_zeroed")
    s_stage, s_aT, s_attnT, s_y = sem("attn_staged"), sem("attn_turned"), sem("attnT_ready"), sem("attn_projected")
    s_gated, s_x2 = sem("attn_gated"), sem("x2_ready")
    s_stat, s_aggr, s_ve, s_rstd, s_xn = (sem("stats2_done"), sem("aggr2_done"), sem("ve2_done"), sem("rstd2_done"),
                                          sem("xn2_done"))
    s_modb = sem("mod2_copied")
    s_xT, s_h2T, s_h2m, s_h2 = sem("xn2_turned"), sem("h2T_ready"), sem("h2_scaled"), sem("h2_ready")
    s_log, s_logs = sem("logits_summed"), sem("logits_copied")
    s_gate, s_up, s_silu, s_act = sem("gate_ready"), sem("up_ready"), sem("silu_ready"), sem("act_ready")
    s_dn, s_dng, s_x3 = sem("shared_ready"), sem("shared_gated"), sem("x3_ready")

    with nc.Block() as block:
        @block.sync
        def _(sp):
            sp.dma_start(wo_sb, woT).then_inc(s_w, 16)
            sp.dma_start(wr_sb, wrT).then_inc(s_w, 16)
            sp.dma_start(wg_sb, wgT).then_inc(s_w, 16)
            sp.dma_start(wu_sb, wuT).then_inc(s_w, 16)
            sp.dma_start(wd_sb, wdT.rearrange("(c p) e -> p c e", p=P)).then_inc(s_w, 16)
            sp.dma_start(gu_sb.rearrange("p (e f) -> p e f", e=NE), gate_up.rearrange("e h f -> h e f")).then_inc(s_ew, 16)
            sp.dma_start(dn_sb.rearrange("p (e c h) -> p e c h", e=NE, c=2),
                         down.rearrange("e (c p) h -> p e c h", p=P)).then_inc(s_ew, 16)
            sp.wait_ge(s_zero, 2)
            for n in range(ET // 8):
                sp.dma_start(sorted_d[n * 8 * P:(n + 1) * 8 * P, :].rearrange("(p r) e -> p (r e)", p=P),
                             zeros).then_inc(s_zeroed, 16)
            sp.wait_ge(s_ew, 32)
            sp.wait_ge(s_zeroed, 16 * (ET // 8))

        @block.gpsimd
        def _(pool):
            pool.memset(zeros, 0.0).then_inc(s_zero, 1)
            pool.memset(half_neg, -0.5).then_inc(s_zero, 1)
            pool.wait_ge(s_zero, 2)
            with pool.Fori(0, B) as b:
                for c in range(2):
                    n = b * 2 + c
                    pool.wait_ge(s_ve, n + 1)
                    pool.tensor_tensor(rstd, ve, half_neg, ALU.pow).then_inc(s_rstd, 1)
                    pool.wait_ge(s_xn, n + 1)
                    pool.tensor_tensor(h2m.rearrange("p (t e) -> p t e", t=4), xn.rearrange("p (t e) -> p t e", t=4),
                                       cb_row.unsqueeze(1).broadcast_to([P, 4, E]), ALU.mult).then_inc(s_h2m, 1)

        @block.scalar
        def _(act):
            act.sem_inc(s_h2T, 1)
            with act.Fori(0, B) as b:
                for c in range(2):
                    n = b * 2 + c
                    act.activation(stage.rearrange("p (t e) -> p t e", t=4), attn_sb[:, bass.ds(b * TPB + 4 * c, 4), :],
                                   ACT.Copy).then_inc(s_stage, 1)
                    act.wait_ge(s_aT, n + 1)
                    act.activation(attnT, psum[:, 0, :], ACT.Copy).then_inc(s_attnT, 1)
                    act.wait_ge(s_xT, n + 1)
                    act.wait_ge(s_modb, b * 2 + 1)
                    act.activation(h2T, psum[:, 2, :], ACT.Identity, scale=mod_b[:, 1:2], bias=mod_b[:, 0:1])\
                        .then_inc(s_h2T, 1)
                    act.wait_ge(s_gate, n + 1)
                    act.wait_ge(s_act, n + 1)
                    act.activation(silu, psum[:, 4:6, :], ACT.Silu).then_inc(s_silu, 1)

        @block.vector
        def _(dve):
            dve.sem_inc(s_act, 1)
            dve.sem_inc(s_dng, 1)
            with dve.Fori(0, B) as b:
                for c in range(2):
                    n = b * 2 + c
                    x4 = x_sb[:, bass.ds(b * TPB + 4 * c, 4), :]
                    tmp4 = tmp.rearrange("p (t e) -> p t e", t=4)

                    def row(j):
                        return mod_rows[:, bass.ds(b, 1), j, :].broadcast_to([P, 4, E])

                    if c == 0:
                        dve.wait_ge(s_h2T, n + 1)
                        dve.tensor_copy(mod_b, mod_cols[:, 2:4, bass.ds(b, 1)].rearrange("p j o -> p (j o)")).then_inc(s_modb, 1)
                        dve.tensor_copy(cb_row, mod_rows[:, bass.ds(b, 1), 2, :].rearrange("p o e -> p (o e)")).then_inc(s_modb, 1)
                    dve.wait_ge(s_y, n + 1)
                    dve.tensor_tensor(tmp4, psum[:, 1, :].rearrange("p (t e) -> p t e", t=4), row(0), ALU.mult).then_inc(s_gated, 1)
                    dve.wait_ge(s_gated, n + 1)
                    dve.tensor_tensor(x2, x4, tmp4, ALU.add).then_inc(s_x2, 1)
                    dve.wait_ge(s_x2, n + 1)
                    for t in range(4):
                        dve.bn_stats(stats[:, t, :], x2[:, t, :]).then_inc(s_stat, 1)
                    dve.wait_ge(s_stat, n * 4 + 4)
                    dve.tensor_copy(ve, stats[:, :, 0]).then_inc(s_aggr, 1)
                    for t in range(4):
                        dve.bn_aggr(mv[:, t, :], stats[:, t, :]).then_inc(s_aggr, 1)
                    dve.wait_ge(s_aggr, n * 5 + 5)
                    dve.tensor_scalar(ve, mv[:, :, 1], EPS, None, ALU.add).then_inc(s_ve, 1)
                    dve.wait_ge(s_rstd, n + 1)
                    for t in range(4):
                        st = dve.tensor_scalar(xn[:, t * E:(t + 1) * E],
                                               x2[:, t, :], mv[:, t, 0:1], rstd[:, t:t + 1], ALU.subtract, ALU.mult)
                    st.then_inc(s_xn, 1)
                    dve.wait_ge(s_h2m, n + 1)
                    dve.tensor_tensor(attn_sb[:, bass.ds(b * TPB + 4 * c, 4), :], h2m.rearrange("p (t e) -> p t e", t=4),
                                      row(1), ALU.add).then_inc(s_h2, 1)
                    dve.wait_ge(s_log, n + 1)
                    dve.tensor_copy(logits[:, bass.ds(b * TPB + 4 * c, 4), :],
                                    psum[:, 3, 0:4 * NE].rearrange("p (t e) -> p t e", t=4)).then_inc(s_logs, 1)
                    dve.wait_ge(s_up, n + 1)
                    dve.wait_ge(s_silu, n + 1)
                    dve.tensor_tensor(act_s, psum[:, 6:8, :], silu, ALU.mult).then_inc(s_act, 1)
                    dve.wait_ge(s_dn, n + 1)
                    dve.tensor_tensor(tmp4, psum[:, 0, :].rearrange("p (t e) -> p t e", t=4), row(3), ALU.mult).then_inc(s_dng, 1)
                    dve.wait_ge(s_dng, n + 2)
                    dve.tensor_tensor(x4, x2, tmp4, ALU.add).then_inc(s_x3, 1)
                    dve.wait_ge(s_x3, n + 1)

        @block.tensor
        def _(pe):
            pe.wait_ge(s_w, 80)
            with pe.Fori(0, B) as b:
                for c in range(2):
                    n = b * 2 + c
                    tile = [slice(t * P, (t + 1) * P) for t in range(4)]
                    pe.wait_ge(s_stage, n + 1)
                    pe.wait_ge(s_dng, n + 1)
                    for t in range(4):
                        mm = pe.transpose(psum[:, 0, tile[t]], stage[:, tile[t]], ident[:, :])
                    mm.then_inc(s_aT, 1)
                    pe.wait_ge(s_attnT, n + 1)
                    for t in range(4):
                        mm = pe.matmul(psum[:, 1, tile[t]], attnT[:, tile[t]], wo_sb, start=True, stop=True)
                    mm.then_inc(s_y, 1)
                    pe.wait_ge(s_xn, n + 1)
                    for t in range(4):
                        mm = pe.transpose(psum[:, 2, tile[t]], xn[:, tile[t]], ident[:, :])
                    mm.then_inc(s_xT, 1)
                    pe.wait_ge(s_h2T, n + 2)
                    for t in range(4):
                        mm = pe.matmul(psum[:, 3, t * NE:(t + 1) * NE], h2T[:, tile[t]], wr_sb, start=True, stop=True)
                    mm.then_inc(s_log, 1)
                    for f in range(2):
                        mm = pe.matmul(psum[:, 4 + f, :], wg_sb[:, f * P:(f + 1) * P], h2T, start=True, stop=True)
                    mm.then_inc(s_gate, 1)
                    for f in range(2):
                        mm = pe.matmul(psum[:, 6 + f, :], wu_sb[:, f * P:(f + 1) * P], h2T, start=True, stop=True)
                    mm.then_inc(s_up, 1)
                    pe.wait_ge(s_act, n + 2)
                    for t in range(4):
                        for f in range(2):
                            mm = pe.matmul(psum[:, 0, tile[t]], act_s[:, f, tile[t]], wd_sb[:, f, :], start=f == 0, stop=f == 1)
                    mm.then_inc(s_dn, 1)


def route(nc, sem, psum, attn_sb, sorted_d, logits, top, gate_of, best, pos_f, pos, pick, pick_b, lower, steps_of,
          tri16, before, ones, slots, count, tiles, ends, starts, cmp, expert_f, expert):
    s_c, s_v = sem("route_constants"), sem("route_steps")
    s_top, s_sig, s_pick = sem("top_logit_ready"), sem("gates_ready"), sem("pick_ready")
    s_places, s_counts = sem("places_summed"), sem("counts_summed")
    s_scaled, s_pos, s_scat = sem("rows_scaled"), sem("places_ready"), sem("rows_sorted")

    with nc.Block() as block:
        @block.gpsimd
        def _(pool):
            small = dict(allow_small_or_imprecise_dtypes=True)
            pool.iota(lower, pattern=[[-1, NE]], base=NE, channel_multiplier=0, **small).then_inc(s_c, 1)
            pool.iota(steps_of, pattern=[[P, NT]], base=0, channel_multiplier=0, **small).then_inc(s_c, 1)
            pool.iota(slots, pattern=[[1, ET]], base=0, channel_multiplier=0, **small).then_inc(s_c, 1)
            pool.memset(tri16, 1.0).then_inc(s_c, 1)
            pool.memset(before, 1.0).then_inc(s_c, 1)
            pool.memset(ones, 1.0).then_inc(s_c, 1)
            pool.wait_ge(s_c, 6)
            pool.affine_select(out=tri16, in_=tri16, compare_op=ALU.is_ge, fill=0.0, base=0,
                               pattern=[[1, NE], [-1, NE]], channel_multiplier=0).then_inc(s_c, 1)
            pool.affine_select(out=before, in_=before, compare_op=ALU.is_gt, fill=0.0, base=0,
                               pattern=[[1, P]], channel_multiplier=-1).then_inc(s_c, 1)
            pool.wait_ge(s_pos, 1)
            for t in range(NT):
                if t % TPB == 0:
                    pool.wait_ge(s_scaled, t // TPB + 1)
                pool.indirect_dma_start(sorted_d[:, :], bass.IndirectOffsetOnAxis(ap=pos[:, t:t + 1], axis=0),
                                        attn_sb[:, t, :], None).then_inc(s_scat, 16)
            pool.wait_ge(s_scat, 16 * NT)

        @block.scalar
        def _(act):
            act.wait_ge(s_top, 1)
            act.activation(gate_of, top, ACT.Sigmoid).then_inc(s_sig, 1)

        @block.vector
        def _(dve):
            done = [0]

            def then(ins):
                done[0] += 1
                ins.then_inc(s_v, 1)
                dve.wait_ge(s_v, done[0])

            shape = [P, NT, NE]
            dve.tensor_reduce(top, logits, AX.X, ALU.max).then_inc(s_top, 1)
            dve.wait_ge(s_top, 1)
            then(dve.tensor_tensor(pick, logits, top.unsqueeze(2).broadcast_to(shape), ALU.is_equal))
            dve.wait_ge(s_c, 8)
            then(dve.tensor_tensor(pick, pick, lower.unsqueeze(1).broadcast_to(shape), ALU.mult))
            then(dve.tensor_reduce(best, pick, AX.X, ALU.max))
            then(dve.tensor_tensor(pick, lower.unsqueeze(1).broadcast_to(shape), best.unsqueeze(2).broadcast_to(shape),
                                   ALU.is_equal))
            dve.tensor_copy(pick_b, pick).then_inc(s_pick, 1)
            dve.wait_ge(s_sig, 1)
            for b in range(B):
                rows = attn_sb[:, b * TPB:(b + 1) * TPB, :]
                dve.tensor_tensor(rows, rows, gate_of[:, b * TPB:(b + 1) * TPB].unsqueeze(2).broadcast_to([P, TPB, E]),
                                  ALU.mult).then_inc(s_scaled, 1)
            dve.wait_ge(s_counts, 1)
            then(dve.tensor_reduce(count, psum[:, 1, :].rearrange("p (t e) -> p e t", t=NT), AX.X, ALU.add))
            cmp_n = cmp[:, 0:NE * NT].rearrange("p (e n) -> p e n", e=NE)
            then(dve.tensor_tensor(cmp_n, count.unsqueeze(2).broadcast_to([P, NE, NT]),
                                   steps_of.unsqueeze(1).broadcast_to([P, NE, NT]), ALU.is_gt))
            then(dve.tensor_reduce(tiles, cmp_n, AX.X, ALU.add))
            cmp_e = cmp[:, 0:NE * NE].rearrange("p (e f) -> p e f", e=NE)
            then(dve.tensor_tensor(cmp_e, tri16, tiles.unsqueeze(1).broadcast_to([P, NE, NE]), ALU.mult))
            then(dve.tensor_reduce(ends, cmp_e, AX.X, ALU.add))
            then(dve.tensor_tensor(starts, ends, tiles, ALU.subtract))
            then(dve.tensor_scalar(starts, starts, float(P), None, ALU.mult))
            dve.wait_ge(s_places, 1)
            placed = cmp[:, 0:NT * NE].rearrange("p (t e) -> p t e", t=NT)
            then(dve.tensor_tensor(placed, psum[:, 0, :].rearrange("p (t e) -> p t e", t=NT),
                                   starts.unsqueeze(1).broadcast_to(shape), ALU.add))
            then(dve.tensor_tensor(placed, placed, pick, ALU.mult))
            then(dve.tensor_reduce(pos_f, placed, AX.X, ALU.add))
            dve.tensor_copy(pos, pos_f).then_inc(s_pos, 1)
            cmp_s = cmp.rearrange("p (s e) -> p s e", s=ET)
            then(dve.tensor_tensor(cmp_s, slots.unsqueeze(2).broadcast_to([P, ET, NE]),
                                   ends.unsqueeze(1).broadcast_to([P, ET, NE]), ALU.is_ge))
            then(dve.tensor_reduce(expert_f, cmp_s, AX.X, ALU.add))
            then(dve.tensor_scalar(expert_f, expert_f, float(NE - 1), None, ALU.min))
            then(dve.tensor_copy(expert, expert_f))

        @block.tensor
        def _(pe):
            pe.wait_ge(s_c, 8)
            pe.wait_ge(s_pick, 1)
            flat = pick_b.rearrange("p t e -> p (t e)")
            pe.matmul(psum[:, 1, :], ones, flat, start=True, stop=True).then_inc(s_counts, 1)
            pe.matmul(psum[:, 0, :], before, flat, start=True, stop=False)
            for t in range(NT - 1):
                mm = pe.matmul(psum[:, 0, (t + 1) * NE:], ones, pick_b[:, t:t + 1, :].broadcast_to([P, NT - 1 - t, NE]),
                               start=False, stop=t == NT - 2)
            mm.then_inc(s_places, 1)


def experts(nc, sem, psum, ident, sorted_d, expert_d, gu_sb, dn_sb, expert, h_in, h_inT, w_gu, w_dn, silu_e, act_e, y_out):
    s_in = [sem("even_rows_in"), sem("odd_rows_in")]
    s_turn, s_hT = sem("rows_turned"), sem("rowsT_ready")
    s_wgu, s_wdn = sem("gate_up_copied"), sem("down_copied")
    s_gu, s_silu, s_act = sem("expert_gate_up_ready"), sem("expert_silu_ready"), sem("expert_act_ready")
    s_y, s_yout, s_st = sem("expert_rows_ready"), sem("expert_rows_copied"), sem("expert_rows_stored")

    with nc.Block() as block:
        @block.sync
        def _(sp):
            sp.sem_inc(s_st, 16)

            def load(n, p):
                sp.wait_ge(s_turn, n + 1)
                sp.dma_start(h_in[p], sorted_d[bass.ds(n * P, P), :]).then_inc(s_in[p], 16)

            def store(n, p):
                sp.wait_ge(s_yout, n + 3)
                sp.dma_start(expert_d[bass.ds(n * P, P), :], y_out[p]).then_inc(s_st, 16)

            load(0, 0)
            load(1, 1)
            with sp.Fori(0, ET // 2 - 1) as i:
                for p in range(2):
                    load(i * 2 + p + 2, p)
                    store(i * 2 + p, p)
            store(ET - 2, 0)
            store(ET - 1, 1)
            sp.wait_ge(s_st, 16 * ET + 16)

        @block.scalar
        def _(act):
            act.sem_inc(s_wdn, 1)
            act.sem_inc(s_yout, 2)

            def copy_weights(n, p):
                e = act.value_load(expert[0:1, bass.ds(n, 1)], min_val=0, max_val=NE - 1)
                act.wait_ge(s_y, n + 1)
                act.activation(w_dn[p], dn_sb[:, bass.ds(e * 2 * E, 2 * E)], ACT.Copy).then_inc(s_wdn, 1)

            def turn(n, p):
                act.wait_ge(s_turn, n + 3)
                act.wait_ge(s_gu, n + 1)
                act.activation(h_inT[p], psum[:, p, 0:P], ACT.Copy).then_inc(s_hT, 1)

            def silu(n, p):
                act.wait_ge(s_gu, n + 3)
                act.wait_ge(s_act, n + 1)
                act.activation(silu_e[p], psum[:, 2 + p, 0:2 * P], ACT.Silu).then_inc(s_silu, 1)

            def copy_out(n, p):
                act.wait_ge(s_y, n + 3)
                act.wait_ge(s_st, n * 16 + 16)
                act.activation(y_out[p], psum[:, 4 + p, 0:P], ACT.Copy).then_inc(s_yout, 1)

            turn(0, 0)
            turn(1, 1)
            copy_weights(0, 0)
            silu(0, 0)
            with act.Fori(0, ET // 2 - 1) as i:
                for p in range(2):
                    n = i * 2 + p
                    turn(n + 2, p)
                    copy_weights(n + 1, 1 - p)
                    silu(n + 1, 1 - p)
                    copy_out(n, p)
            copy_weights(ET - 1, 1)
            silu(ET - 1, 1)
            copy_out(ET - 2, 0)
            copy_out(ET - 1, 1)

        @block.vector
        def _(dve):
            dve.sem_inc(s_act, 2)

            def copy_weights(n, p):
                e = dve.value_load(expert[0:1, bass.ds(n, 1)], min_val=0, max_val=NE - 1)
                dve.wait_ge(s_gu, n + 1)
                dve.tensor_copy(w_gu[p], gu_sb[:, bass.ds(e * 2 * F, 2 * F)]).then_inc(s_wgu, 1)

            def mult(n, p):
                dve.wait_ge(s_silu, n + 1)
                dve.wait_ge(s_y, n + 1)
                dve.tensor_tensor(act_e[p], psum[:, 2 + p, 2 * P:4 * P], silu_e[p], ALU.mult).then_inc(s_act, 1)

            copy_weights(0, 0)
            copy_weights(1, 1)
            mult(0, 0)
            with dve.Fori(0, ET // 2 - 1) as i:
                for p in range(2):
                    n = i * 2 + p
                    copy_weights(n + 2, p)
                    mult(n + 1, 1 - p)
            mult(ET - 1, 1)

        @block.tensor
        def _(pe):
            pe.sem_inc(s_gu, 2)
            pe.sem_inc(s_y, 2)
            pe.sem_inc(s_turn, 2)

            def turn(n, p):
                pe.wait_ge(s_in[p], (n - p) * 8 + 16)
                pe.transpose(psum[:, p, 0:P], h_in[p], ident[:, :]).then_inc(s_turn, 1)

            def gate_up(n, p):
                pe.wait_ge(s_hT, n + 1)
                pe.wait_ge(s_wgu, n + 1)
                pe.wait_ge(s_act, n + 1)
                for f in range(4):
                    mm = pe.matmul(psum[:, 2 + p, f * P:(f + 1) * P], w_gu[p][:, f * P:(f + 1) * P], h_inT[p], start=True, stop=True)
                mm.then_inc(s_gu, 1)

            def down(n, p):
                pe.wait_ge(s_act, n + 3)
                pe.wait_ge(s_wdn, n + 2)
                pe.wait_ge(s_yout, n + 1)
                for f in range(2):
                    mm = pe.matmul(psum[:, 4 + p, 0:P], act_e[p][:, f * P:(f + 1) * P], w_dn[p][:, f * P:(f + 1) * P],
                                   start=f == 0, stop=f == 1)
                mm.then_inc(s_y, 1)

            turn(0, 0)
            turn(1, 1)
            gate_up(0, 0)
            with pe.Fori(0, ET // 2 - 1) as i:
                for p in range(2):
                    n = i * 2 + p
                    turn(n + 2, p)
                    gate_up(n + 1, 1 - p)
                    down(n, p)
            gate_up(ET - 1, 1)
            down(ET - 2, 0)
            down(ET - 1, 1)


def combine(nc, sem, x_sb, attn_sb, mod_rows, pos, expert_d, out):
    s_got, s_gated, s_sum, s_out = sem("expert_rows_back"), sem("expert_rows_gated"), sem("result_ready"), sem("result_out")
    out_v = out.rearrange("b (t p) e -> p (b t) e", p=P)

    with nc.Block() as block:
        @block.gpsimd
        def _(pool):
            for t in range(NT):
                pool.indirect_dma_start(attn_sb[:, t, :], None, expert_d[:, :],
                                        bass.IndirectOffsetOnAxis(ap=pos[:, t:t + 1], axis=0)).then_inc(s_got, 16)
                if t % 4 == 3:
                    pool.wait_ge(s_got, 16 * (t + 1))

        @block.vector
        def _(dve):
            for g in range(NT // 4):
                y = attn_sb[:, 4 * g:4 * g + 4, :]
                x4 = x_sb[:, 4 * g:4 * g + 4, :]
                dve.wait_ge(s_got, 64 * (g + 1))
                dve.tensor_tensor(y, y, mod_rows[:, g // 2:g // 2 + 1, 3, :].broadcast_to([P, 4, E]), ALU.mult).then_inc(s_gated, 1)
                dve.wait_ge(s_gated, g + 1)
                dve.tensor_tensor(x4, x4, y, ALU.add).then_inc(s_sum, 1)

        @block.sync
        def _(sp):
            for g in range(NT // 4):
                sp.wait_ge(s_sum, g + 1)
                sp.dma_start(out_v[:, 4 * g:4 * g + 4, :], x_sb[:, 4 * g:4 * g + 4, :]).then_inc(s_out, 16)
            sp.wait_ge(s_out, 16 * (NT // 4))


def kernel(L0_attn_hidden_states, L0_attn_Wq, L0_attn_Wk, L0_attn_Wv, L0_attn_Wo, L0_attn_bo, L0_ffn_w_router,
           L0_ffn_gate_up_proj, L0_ffn_down_proj, L0_ffn_w_gate, L0_ffn_w_up, L0_ffn_w_down, L0_c, L0_wmod):
    import numpy as np
    import concourse.bacc as bacc
    from concourse import mybir as mb
    from concourse.bass_utils import run_bass_kernel_spmd as run

    given = [
        ("x", L0_attn_hidden_states), ("wqT", np.transpose(L0_attn_Wq)), ("wkT", np.transpose(L0_attn_Wk)),
        ("wvT", np.transpose(L0_attn_Wv)), ("woT", np.transpose(L0_attn_Wo)), ("bo", L0_attn_bo),
        ("wrT", np.transpose(L0_ffn_w_router)), ("gate_up", L0_ffn_gate_up_proj), ("down", L0_ffn_down_proj),
        ("wgT", np.transpose(L0_ffn_w_gate)), ("wuT", np.transpose(L0_ffn_w_up)), ("wdT", np.transpose(L0_ffn_w_down)),
        ("cT", np.transpose(L0_c)), ("wmod", L0_wmod),
    ]
    nc = bacc.Bacc("TRN2", target_bir_lowering=False, num_devices=1)
    arrays, args = {}, []
    for name, a in given:
        a = np.ascontiguousarray(a)
        arrays[f"{name}_dram"] = a
        args.append(nc.dram_tensor(f"{name}_dram", a.shape, mb.dt.from_np(a.dtype), kind="ExternalInput").ap())
    out = nc.dram_tensor("out_dram", (B, S, E), F32, kind="ExternalOutput").ap()
    adaln_kernel(nc, *args, out)
    r = run(nc, [arrays], core_ids=[0])
    return r.results[0]["out_dram"]
```

```python
from contextlib import ExitStack

import concourse.bass as bass
from concourse import mybir

F32 = mybir.dt.float32
BF16 = mybir.dt.bfloat16
I32 = mybir.dt.int32
ALU = mybir.AluOpType
ACT = mybir.ActivationFunctionType
AX = mybir.AxisListType

P = 128
B, S, E = 4, 1024, 128
TPB = S // P
NT = B * TPB
H, D, WINDOW = 16, 8, 32
SCALE = D ** -0.5
NEG = -1e30
EPS = 1e-5
NE, F = 16, 256
NPART = 3
KS = NPART * NPART * D
KM = KS + NPART
VW = D + 1
UH = 8
NU = 2
BAND = P + WINDOW
ET = NT + NE
WE = 2 * F + 2 * E
RW = E + 1
HALF = 512


def adaln_kernel(nc, x, wqT, wkT, wvT, woT, bo, wrT, gate_up, down, wgT, wuT, wdT, cT, wmod, out):
    ctx = ExitStack()
    with ctx:
        def sb(name, shape, dt=F32):
            return ctx.enter_context(nc.sbuf_tensor(name, shape, dt))

        def sem(name):
            return ctx.enter_context(nc.semaphore(name))

        psum = ctx.enter_context(nc.psum_tensor("psum", [P, 8, HALF], F32))
        q_parts_d = nc.dram_tensor("q_parts_d", [H, NPART, D, B * S], BF16, kind="Internal").ap()
        k_parts_d = nc.dram_tensor("k_parts_d", [H, NPART, D, B * S], BF16, kind="Internal").ap()
        v_d = nc.dram_tensor("v_d", [B, P, TPB * H * VW], F32, kind="Internal").ap()

        x_sb = sb("x_sb", [P, NT, E])
        ident = sb("ident", [P, P])
        identb = sb("identb", [P, P], BF16)
        mask_qk = sb("mask_qk", [P, P], BF16)
        mask_kq = sb("mask_kq", [P, P], BF16)
        mask_lq = sb("mask_lq", [P, TPB, 2 * WINDOW], BF16)
        mask_lk = sb("mask_lk", [P, 2, BAND], BF16)
        mod_cols = sb("mod_cols", [P, 4, B])
        mod_rows = sb("mod_rows", [P, B, 4, E])
        attn_sb = sb("attn_sb", [P, NT, E])
        work = sb("work", [P, 36000])

        setup(nc, sem, psum, work, x, x_sb, wqT, wkT, wvT, bo, cT, wmod, ident, identb, mask_qk, mask_kq,
              mask_lq, mask_lk, mod_cols, mod_rows, q_parts_d, k_parts_d, v_d)
        attention(nc, sem, psum, work, attn_sb, ident, identb, mask_qk, mask_kq, mask_lq, mask_lk, q_parts_d,
                  k_parts_d, v_d)
        sorted_d = nc.dram_tensor("sorted_d", [ET * P, RW], F32, kind="Internal").ap()
        expert_d = nc.dram_tensor("expert_d", [(NT + ET) * P, E], F32, kind="Internal").ap()
        feed_forward(nc, sem, psum, work, x_sb, attn_sb, ident, mod_cols, mod_rows, woT, wrT, gate_up, down, wgT,
                     wuT, wdT, sorted_d, expert_d, out)


def setup(nc, sem, psum, work, x, x_sb, wqT, wkT, wvT, bo, cT, wmod, ident, identb, mask_qk, mask_kq,
          mask_lq, mask_lk, mod_cols, mod_rows, q_parts_d, k_parts_d, v_d):
    at = [0]

    def part(n, dt=F32):
        a = work[:, at[0]:at[0] + n]
        at[0] += n
        return a

    wq_sb, wk_sb, wv_sb = part(E), part(E), part(E)
    wmod_sb = part(6 * E)
    bo_sb = part(E)
    c_sb, c_exp, c_silu = part(B), part(B), part(B)
    c_bc = part(B * P).rearrange("p (b m) -> p b m", b=B)
    sign = part(B * E).rearrange("p (b m) -> p b m", b=B)
    size = part(B * E).rearrange("p (b m) -> p b m", b=B)
    stats = part(TPB * 6).rearrange("p (t s) -> p t s", t=TPB)
    mv = part(TPB * 2).rearrange("p (t s) -> p t s", t=TPB)
    half_neg = part(TPB)
    ve = part(TPB)
    rstd = part(TPB)
    xn = part(TPB * E).rearrange("p (t e) -> p t e", t=TPB)
    hT = part(S)
    mod_b = part(2)
    rest = part(2 * S).rearrange("p (w s) -> p w s", w=2)
    q_parts = part(2 * NPART * S // 2).bitcast(BF16).rearrange("p (w i s) -> p w i s", w=2, i=NPART)
    v_sb = part(TPB * H * VW).rearrange("p (t h w) -> p t h w", t=TPB, h=H)

    s_wm, s_w, s_x, s_bo = sem("modulation_weights_in"), sem("projection_weights_in"), sem("x_in"), sem("bo_in")
    s_const, s_zero = sem("constants_made"), sem("constants_zeroed")
    s_cexp, s_c, s_cols, s_rows, s_rowsb = (sem("c_exp_done"), sem("c_steps"), sem("mod_cols_summed"),
                                            sem("mod_rows_summed"), sem("mod_rows_copied"))
    s_mod, s_gate = sem("mod_steps"), sem("gates_done")
    s_bo_added = sem("bo_added")
    s_ln, s_stat, s_ve, s_rstd, s_xn = sem("ln_steps"), sem("stats_done"), sem("ve_done"), sem("rstd_done"), sem("xn_done")
    s_xT, s_hT, s_modb = sem("x_transposed"), sem("hT_done"), sem("mod_b_copied")
    s_proj, s_p1, s_rest, s_p2, s_parts = (sem("projected"), sem("first_part_done"), sem("rest_done"),
                                           sem("second_part_done"), sem("parts_done"))
    s_vproj, s_v = sem("v_projected"), sem("v_copied")
    s_stored = sem("parts_stored")
    s_half = sem("constants_half")

    STORES = 16 * (2 * NPART + 1)

    with nc.Block() as block:
        @block.sync
        def _(sp):
            sp.sem_inc(s_stored, 16)
            sp.dma_start(c_sb, cT).then_inc(s_wm, 16)
            sp.dma_start(wmod_sb, wmod).then_inc(s_wm, 16)
            xv = x.rearrange("b (t p) e -> b p t e", p=P)
            for b in range(B):
                sp.dma_start(x_sb[:, b * TPB:(b + 1) * TPB, :], xv[b]).then_inc(s_x, 16)
            with sp.Fori(0, B) as b:
                sp.wait_ge(s_parts, b * 4 + 4)
                cols = bass.ds(b * S, S)
                for i in range(NPART):
                    sp.dma_start(q_parts_d[:, i, :, cols], q_parts[:, 0, i]).then_inc(s_stored, 16)
                    sp.dma_start(k_parts_d[:, i, :, cols], q_parts[:, 1, i]).then_inc(s_stored, 16)
                sp.wait_ge(s_v, b * 2 + 4)
                sp.dma_start(v_d[bass.ds(b, 1)].rearrange("o p n -> (o p) n"),
                             v_sb.rearrange("p t h w -> p (t h w)")).then_inc(s_stored, 16)
            sp.wait_ge(s_stored, B * STORES + 16)

        @block.gpsimd
        def _(pool):
            pool.dma_start(bo_sb, bo.partition_broadcast(P)).then_inc(s_bo, 16)
            pool.memset(ident[:, :], 0.0).then_inc(s_zero, 1)
            pool.memset(identb[:, :], 0.0).then_inc(s_zero, 1)
            pool.memset(mask_qk[:, :], 0.0).then_inc(s_zero, 1)
            pool.memset(mask_kq[:, :], 0.0).then_inc(s_zero, 1)
            pool.memset(mask_lq[:, :, :], 0.0).then_inc(s_zero, 1)
            pool.memset(mask_lk[:, :, :], 0.0).then_inc(s_zero, 1)
            pool.memset(half_neg, -0.5).then_inc(s_half, 1)
            pool.wait_ge(s_zero, 6)
            for m in (ident, identb):
                pool.affine_select(out=m[:, :], in_=m[:, :], compare_op=ALU.not_equal, fill=1.0, base=0,
                                   pattern=[[-1, P]], channel_multiplier=1).then_inc(s_const, 1)
            pool.affine_select(out=mask_qk[:, :], in_=mask_qk[:, :], compare_op=ALU.is_ge, fill=NEG, base=0,
                               pattern=[[-1, P]], channel_multiplier=1).then_inc(s_const, 1)
            pool.affine_select(out=mask_kq[:, :], in_=mask_kq[:, :], compare_op=ALU.is_ge, fill=NEG, base=0,
                               pattern=[[1, P]], channel_multiplier=-1).then_inc(s_const, 1)
            pool.wait_ge(s_const, 4)
            for j in range(P // WINDOW):
                rows = mask_lq[j * WINDOW:(j + 1) * WINDOW]
                pool.affine_select(out=rows, in_=rows, compare_op=ALU.is_ge, fill=NEG, base=0,
                                   pattern=[[0, TPB], [1, 2 * WINDOW]], channel_multiplier=-1).then_inc(s_const, 1)
                pool.wait_ge(s_const, 5 + 2 * j)
                pool.affine_select(out=rows, in_=rows, compare_op=ALU.is_ge, fill=NEG, base=WINDOW,
                                   pattern=[[0, TPB], [-1, 2 * WINDOW]], channel_multiplier=1).then_inc(s_const, 1)
                pool.wait_ge(s_const, 6 + 2 * j)
            pool.affine_select(out=mask_lk[:, :, :], in_=mask_lk[:, :, :], compare_op=ALU.is_ge, fill=NEG, base=0,
                               pattern=[[0, 2], [1, BAND]], channel_multiplier=-1).then_inc(s_const, 1)
            pool.wait_ge(s_const, 13)
            pool.affine_select(out=mask_lk[:, :, :], in_=mask_lk[:, :, :], compare_op=ALU.is_ge, fill=NEG, base=WINDOW,
                               pattern=[[0, 2], [-1, BAND]], channel_multiplier=1).then_inc(s_const, 1)
            pool.memset(mask_lq[0:WINDOW, 0, 0:WINDOW], NEG).then_inc(s_const, 1)
            pool.wait_ge(s_half, 1)
            with pool.Fori(0, B) as b:
                pool.wait_ge(s_ve, b + 1)
                pool.tensor_tensor(rstd, ve, half_neg, ALU.pow).then_inc(s_rstd, 1)
            pool.wait_ge(s_bo, 16)
            pool.wait_ge(s_gate, 2)
            pool.wait_ge(s_xn, B)
            for b in range(B):
                pool.tensor_tensor(size[:, b, :], mod_rows[:, b, 0, :], bo_sb, ALU.mult).then_inc(s_bo_added, 1)
            pool.wait_ge(s_bo_added, B)
            for b in range(B):
                xb = x_sb[:, b * TPB:(b + 1) * TPB, :]
                pool.tensor_tensor(xb, xb, size[:, b, :].unsqueeze(1).broadcast_to([P, TPB, E]),
                                   ALU.add).then_inc(s_bo_added, 1)

        @block.scalar
        def _(act):
            act.sem_inc(s_hT, 2)
            act.sem_inc(s_v, 2)
            act.dma_start(wq_sb, wqT).then_inc(s_w, 16)
            act.dma_start(wk_sb, wkT).then_inc(s_w, 16)
            act.dma_start(wv_sb, wvT).then_inc(s_w, 16)
            act.wait_ge(s_wm, 32)
            act.activation(c_exp, c_sb, ACT.Exp, scale=-1.0).then_inc(s_cexp, 1)
            for b in range(B):
                act.wait_ge(s_rows, b + 1)
                act.activation(mod_rows[:, b], psum[:, b, :].rearrange("p (j e) -> p j e", j=4),
                               ACT.Copy).then_inc(s_rowsb, 1)
            with act.Fori(0, B) as b:
                act.wait_ge(s_modb, b + 1)
                for c in range(2):
                    act.wait_ge(s_xT, b * 2 + c + 1)
                    if c == 0:
                        act.wait_ge(s_vproj, b * 2 + 2)
                    act.activation(hT[:, c * HALF:(c + 1) * HALF], psum[:, c, :], ACT.Identity,
                                   scale=mod_b[:, 1:2], bias=mod_b[:, 0:1]).then_inc(s_hT, 1)
                for w in range(2):
                    if w == 0:
                        act.wait_ge(s_stored, b * STORES + 16)
                    for c in range(2):
                        act.wait_ge(s_proj, b * 4 + w * 2 + c + 1)
                        act.activation(q_parts[:, w, 0, c * HALF:(c + 1) * HALF], psum[:, 2 + 2 * w + c, :], ACT.Copy,
                                       scale=SCALE if w == 0 else 1.0).then_inc(s_p1, 1)
                for c in range(2):
                    act.wait_ge(s_vproj, b * 2 + c + 3)
                    act.activation(v_sb[:, c * 4:(c + 1) * 4, :, 0:D],
                                   psum[:, 6 + c, :].rearrange("p (t h d) -> p t h d", t=4, h=H),
                                   ACT.Copy).then_inc(s_v, 1)

        @block.vector
        def _(dve):
            dve.sem_inc(s_rest, 4)
            dve.memset(v_sb, 1.0).then_inc(s_c, 1)
            dve.wait_ge(s_cexp, 1)
            dve.tensor_scalar(c_exp, c_exp, 1.0, None, ALU.add).then_inc(s_c, 1)
            dve.wait_ge(s_c, 2)
            dve.reciprocal(c_exp, c_exp).then_inc(s_c, 1)
            dve.wait_ge(s_c, 3)
            dve.tensor_tensor(c_silu, c_exp, c_sb, ALU.mult).then_inc(s_c, 1)
            dve.wait_ge(s_c, 4)
            dve.tensor_copy(c_bc, c_silu.unsqueeze(2).broadcast_to([P, B, P])).then_inc(s_c, 1)
            dve.wait_ge(s_cols, 1)
            dve.tensor_copy(mod_cols[:, :, :], psum[:, 4, 0:4 * B].rearrange("p (j b) -> p j b", j=4)).then_inc(s_mod, 1)
            dve.wait_ge(s_mod, 1)
            for j in (1, 3):
                dve.tensor_scalar(mod_cols[:, j, :], mod_cols[:, j, :], 1.0, None, ALU.add).then_inc(s_mod, 1)
            dve.wait_ge(s_rowsb, B)
            dve.tensor_scalar(mod_rows[:, :, 2, :], mod_rows[:, :, 2, :], 1.0, None, ALU.add).then_inc(s_mod, 1)
            n = 4
            for j in (0, 3):
                g = mod_rows[:, :, j, :]
                dve.tensor_scalar(sign, g, 0.0, 2.0, ALU.is_ge, ALU.mult).then_inc(s_mod, 1)
                dve.wait_ge(s_mod, n + 1)
                dve.tensor_scalar(sign, sign, 1.0, None, ALU.subtract).then_inc(s_mod, 1)
                dve.wait_ge(s_mod, n + 2)
                dve.tensor_tensor(size, g, sign, ALU.mult).then_inc(s_mod, 1)
                dve.wait_ge(s_mod, n + 3)
                n += 3
                dve.scalar_tensor_tensor(out=g, in0=size, scalar=0.25, in1=sign, op0=ALU.max,
                                         op1=ALU.mult).then_inc(s_gate, 1)
                dve.wait_ge(s_gate, 1 if j == 0 else 2)
            with dve.Fori(0, B) as b:
                dve.wait_ge(s_x, B * 16)
                for t in range(TPB):
                    dve.bn_stats(stats[:, t, :], x_sb[:, bass.ds(b * TPB + t, 1), :].rearrange("p o e -> p (o e)")).then_inc(s_stat, 1)
                dve.wait_ge(s_hT, b * 2 + 2)
                dve.wait_ge(s_stat, b * TPB + TPB)
                dve.tensor_copy(mod_b, mod_cols[:, 0:2, bass.ds(b, 1)].rearrange("p j o -> p (j o)")).then_inc(s_modb, 1)
                for t in range(TPB):
                    dve.bn_aggr(mv[:, t, :], stats[:, t, :]).then_inc(s_ln, 1)
                dve.wait_ge(s_ln, b * TPB + TPB)
                dve.tensor_scalar(ve, mv[:, :, 1], EPS, None, ALU.add).then_inc(s_ve, 1)
                dve.wait_ge(s_rstd, b + 1)
                for t in range(TPB):
                    n = dve.tensor_scalar(xn[:, t, :], x_sb[:, bass.ds(b * TPB + t, 1), :].rearrange("p o e -> p (o e)"),
                                          mv[:, t, 0:1], rstd[:, t:t + 1], ALU.subtract, ALU.mult)
                n.then_inc(s_xn, 1)
                for w in range(2):
                    for c in range(2):
                        n = w * 2 + c
                        cols = slice(c * HALF, (c + 1) * HALF)
                        dve.wait_ge(s_p1, b * 4 + n + 1)
                        dve.scalar_tensor_tensor(out=rest[:, w, cols], in0=psum[:, 2 + n, :],
                                                 scalar=SCALE if w == 0 else 1.0, in1=q_parts[:, w, 0, cols],
                                                 op0=ALU.mult, op1=ALU.subtract).then_inc(s_rest, 1)
                        dve.wait_ge(s_rest, b * 4 + n + 5)
                        dve.tensor_copy(q_parts[:, w, 1, cols], rest[:, w, cols]).then_inc(s_p2, 1)
                        dve.wait_ge(s_p2, b * 4 + n + 1)
                        dve.tensor_tensor(q_parts[:, w, 2, cols], rest[:, w, cols], q_parts[:, w, 1, cols],
                                          ALU.subtract).then_inc(s_parts, 1)

        @block.tensor
        def _(pe):
            pe.sem_inc(s_vproj, 2)
            pe.wait_ge(s_wm, 32)
            pe.wait_ge(s_c, 4)
            for n, j in enumerate((0, 1, 3, 4)):
                mm = pe.matmul(psum[:, 4, n * B:(n + 1) * B], wmod_sb[:, j * E:(j + 1) * E], c_silu, start=True, stop=True)
            mm.then_inc(s_cols, 1)
            pe.wait_ge(s_c, 5)
            for b in range(B):
                pe.matmul(psum[:, b, :], c_bc[:, b, :], wmod_sb[:, 2 * E:6 * E], start=True, stop=True).then_inc(s_rows, 1)
            pe.wait_ge(s_const, 1)
            pe.wait_ge(s_w, 48)
            pe.wait_ge(s_rowsb, B)
            pe.wait_ge(s_mod, 1)
            with pe.Fori(0, B) as b:
                pe.wait_ge(s_xn, b + 1)
                for c in range(2):
                    for t in range(4):
                        mm = pe.transpose(psum[:, c, t * P:(t + 1) * P], xn[:, c * 4 + t, :], ident[:, :])
                    mm.then_inc(s_xT, 1)
                for w, wt in enumerate((wq_sb, wk_sb)):
                    for c in range(2):
                        if w == 0:
                            pe.wait_ge(s_hT, b * 2 + c + 3)
                        pe.wait_ge(s_rest, b * 4 + 4)
                        pe.matmul(psum[:, 2 + 2 * w + c, :], wt, hT[:, c * HALF:(c + 1) * HALF],
                                  start=True, stop=True).then_inc(s_proj, 1)
                pe.wait_ge(s_v, b * 2 + 2)
                for c in range(2):
                    for t in range(4):
                        mm = pe.matmul(psum[:, 6 + c, t * P:(t + 1) * P], hT[:, (c * 4 + t) * P:(c * 4 + t + 1) * P],
                                       wv_sb, start=True, stop=True)
                    mm.then_inc(s_vproj, 1)



MAX_BANKS = [
    ([(0, 0, 128, 0), (4, 512, 128, 128)], (0, 8, 2)),
    ([(1, 0, 256, 0), (5, 512, 256, 256)], (1, 8, 2)),
    ([(2, 0, 384, 0)], (2, 1, 1)),
    ([(3, 0, 512, 0)], (3, 1, 1)),
    ([(4, 0, 512, 0)], (4, 1, 1)),
    ([(5, 0, 512, 0)], (5, 1, 1)),
    ([(6, 0, 512, 0)], (6, 1, 1)),
    ([(7, 0, 512, 0)], (7, 1, 1)),
    ([(6, 512, 384, 0)], (10, 1, 1)),
    ([(7, 512, 512, 0)], (11, 1, 1)),
]
G, L = 0, 1
STEPS = 2 * TPB
SCORES = 4 * 4 + 4 * 2 + TPB
RING_A = 4 * len(MAX_BANKS) + 4 + 2
RING_B = 4
RING = RING_A + RING_B


def max_steps():
    return ([("max_g", h, n) for h in range(4) for n in range(len(MAX_BANKS))] + [("turn_m", G)],
            [("max_l", h) for h in range(4)] + [("turn_m", L)])


def slot_steps(with_next):
    ahead, of_l = max_steps() if with_next else ([], [])
    turn_g = ahead[-1:]
    ahead = ahead[:-1]
    steps = []

    def more(n):
        steps.extend(ahead[:n])
        del ahead[:n]

    for kb in range(TPB):
        parts = 4 if kb < 4 else 2
        share = [8, 7, 6, 5, 4, 3, 2, 1][kb]
        for part in range(parts):
            steps.append(("score_g", kb, part))
            more(share * (part + 1) // parts - share * part // parts)
            if part == 1 and kb:
                steps.append(("weigh_g", kb - 1))
    for kt in range(TPB):
        steps.append(("score_l", kt))
        if kt == 0:
            steps += [("weigh_g", TPB - 1), ("out", G)]
        else:
            steps.append(("weigh_l", kt - 1))
        more(1)
        if kt == 2:
            steps += [("turn_o", G, 0), ("turn_o", G, 1)]
        if kt == 4:
            steps += turn_g
        if kt >= 5:
            steps += of_l[:1]
            del of_l[:1]
    steps += [("weigh_l", TPB - 1), ("out", L)]
    steps += of_l
    steps += [("turn_o", L, 0), ("turn_o", L, 1)]
    assert not ahead
    return steps


def attention(nc, sem, psum, work, attn_sb, ident, identb, mask_qk, mask_kq, mask_lq, mask_lk, q_parts_d,
              k_parts_d, v_d):
    at = [0]

    def part(n, dt=F32):
        a = work[:, at[0]:at[0] + n]
        at[0] += n
        return a

    q_rep, k_rep, v_u = [], [], []
    for u in range(NU):
        q_rep.append(part(UH * S // 2).bitcast(BF16).rearrange("p (h s) -> p h s", h=UH))
        k_rep.append(part(UH * S // 2).bitcast(BF16).rearrange("p (h s) -> p h s", h=UH))
        v_u.append(part(TPB * UH * VW).rearrange("p (t h w) -> p t h w", t=TPB, h=UH))
    probs = [part(4 * S).rearrange("p (h s) -> p h s", h=4) for _ in range(2)]
    o_sb = part(S)
    maxima = [part(4 * 12).rearrange("p (h n) -> p h n", h=4) for _ in (G, L)]
    left = [part(4 * TPB).rearrange("p (h t) -> p h t", h=4) for _ in (G, L)]
    m_parts = [part(NPART * 4 * TPB // 2).bitcast(BF16).rearrange("p (i h t) -> p i h t", i=NPART, h=4) for _ in (G, L)]
    zero = part(4 * TPB).rearrange("p (h t) -> p h t", h=4)
    m_rows = [part(P // 2).bitcast(BF16) for _ in (G, L)]
    inv = [part(16).rearrange("p (t h) -> p t h", t=4) for _ in range(2)]

    s_init = sem("attention_memory_set")
    s_load = [[sem(f"unit{u}_global_heads_in"), sem(f"unit{u}_local_heads_in")] for u in range(NU)]
    s_score, s_exp = sem("scores_ready"), sem("score_buffers_free")
    s_ring, s_ring_free = sem("ring_filled"), sem("ring_banks_free")
    s_weigh = sem("weighed")
    s_out_free = sem("outputs_copied")
    s_max = [sem("global_maxima_ready"), sem("local_maxima_ready")]
    s_pairs = sem("maxima_paired")
    s_zero = sem("zeros_made")
    s_split = sem("maxima_split_steps")
    s_mparts = [sem("global_maxima_split"), sem("local_maxima_split")]
    s_mrows = [sem("global_max_rows_ready"), sem("local_max_rows_ready")]
    s_m = [sem("global_max_rows_in"), sem("local_max_rows_in")]
    s_inv, s_attn = sem("sums_inverted"), sem("attention_written")
    LOADS = 16 * 9
    ROWS = 16 * NPART

    def over_slots(eng, slot):
        with eng.Fori(0, B - 1) as b:
            for u in range(NU):
                slot(b, u, b * NU + u, True)
        for u in range(NU):
            slot(B - 1, u, (B - 1) * NU + u, u < NU - 1)

    with nc.Block() as block:
        @block.sync
        def _(sp):
            def load(b, u, quad):
                h0, to = 4 * (u + NU * quad), slice(4 * quad, 4 * quad + 4)
                cols = bass.ds(b * S, S)

                def parts(of, i0, i1):
                    return of[h0:h0 + 4, i0:i1, :, cols].rearrange("h i d s -> (i d) h s")

                for r in range(NPART):
                    row = r * NPART * D
                    sp.dma_start(q_rep[u][row:row + NPART * D, to, :], parts(q_parts_d, 0, NPART)).then_inc(s_load[u][quad], 16)
                    cut = row + (NPART - r) * D
                    sp.dma_start(k_rep[u][row:cut, to, :], parts(k_parts_d, r, NPART)).then_inc(s_load[u][quad], 16)
                    if r:
                        sp.dma_start(k_rep[u][cut:row + NPART * D, to, :], parts(k_parts_d, 0, r)).then_inc(s_load[u][quad], 16)
                vals = v_d[bass.ds(b, 1)].rearrange("o p (t h w) -> (o p) t h w", t=TPB, h=H)
                sp.dma_start(v_u[u][:, :, to, :], vals[:, :, h0:h0 + 4, :]).then_inc(s_load[u][quad], 16)

            def rows(u, quad, unit):
                sp.wait_ge(s_mrows[quad], unit + 1)
                for i in range(NPART):
                    sp.dma_start(q_rep[u][KS + i:KS + i + 1, 4 * quad:4 * quad + 4, :],
                                 m_rows[quad][i * 4 * TPB:(i + 1) * 4 * TPB, :]).then_inc(s_m[quad], 16)

            sp.wait_ge(s_init, 3)
            for u in range(NU):
                for quad in (G, L):
                    load(0, u, quad)
            for quad in (G, L):
                rows(0, quad, 0)

            def slot(b, u, s, more):
                if not isinstance(b, int):
                    sp.wait_ge(s_weigh, s * STEPS + TPB + 2)
                    load(b + 1, u, G)
                if more:
                    rows(1 - u, G, s + 1)
                if not isinstance(b, int):
                    sp.wait_ge(s_weigh, s * STEPS + STEPS + 2)
                    load(b + 1, u, L)
                if more:
                    rows(1 - u, L, s + 1)

            over_slots(sp, slot)
            for quad in (G, L):
                sp.wait_ge(s_m[quad], B * NU * ROWS)

        @block.gpsimd
        def _(pool):
            def split(quad, unit):
                pool.wait_ge(s_max[quad], unit + 1)
                m = maxima[quad][:, :, 0:TPB]
                n = unit * 8 + quad * 4
                pool.tensor_tensor(m_parts[quad][:, 0], zero, m, ALU.subtract).then_inc(s_split, 1)
                pool.wait_ge(s_split, n + 1)
                pool.tensor_tensor(left[quad], m, m_parts[quad][:, 0], ALU.add).then_inc(s_split, 1)
                pool.wait_ge(s_split, n + 2)
                pool.tensor_tensor(m_parts[quad][:, 1], zero, left[quad], ALU.subtract).then_inc(s_split, 1)
                pool.wait_ge(s_split, n + 3)
                pool.tensor_tensor(left[quad], left[quad], m_parts[quad][:, 1], ALU.add).then_inc(s_split, 1)
                pool.wait_ge(s_split, n + 4)
                pool.tensor_tensor(m_parts[quad][:, 2], zero, left[quad], ALU.subtract).then_inc(s_mparts[quad], 1)

            pool.memset(zero, 0.0).then_inc(s_zero, 1)
            pool.wait_ge(s_zero, 1)
            with pool.Fori(0, B * NU) as unit:
                split(G, unit)
                split(L, unit)

        @block.scalar
        def _(act):
            act.sem_inc(s_exp, 2)
            act.sem_inc(s_out_free, 1)

            def slot(b, u, s, more):
                n = r = turned = 0
                for step in slot_steps(more):
                    if step[0] in ("max_g", "max_l", "turn_m", "turn_o"):
                        r += 1
                        turned = r if step[0] == "turn_o" else turned
                    elif step[0] in ("score_g", "score_l"):
                        kt = step[1] + (TPB if step[0] == "score_l" else 0)
                        to = probs[kt % 2]
                        bank = 2 * (n % 2)
                        act.wait_ge(s_score, s * SCORES + n + 1)
                        first = step[0] == "score_l" or step[2] == 0
                        if first:
                            act.wait_ge(s_weigh, s * STEPS + kt + 1)
                        if step[0] == "score_l":
                            dst = to[:, :, 0:BAND].rearrange("p (a c) q -> p a c q", a=2)
                            src = psum[:, bank:bank + 2, 0:2 * BAND].rearrange("p a (c q) -> p a c q", c=2)
                        elif step[1] < 4:
                            cols = S - step[1] * P
                            dst = to[:, step[2], 0:cols]
                            src = psum[:, bank:bank + 2, :].rearrange("p a q -> p (a q)")[:, 0:cols]
                        else:
                            cols = S - step[1] * P
                            dst = to[:, 2 * step[2]:2 * step[2] + 2, 0:cols]
                            src = psum[:, bank:bank + 2, 0:cols]
                        act.activation(dst, src, ACT.Exp).then_inc(s_exp, 1)
                        n += 1
                    elif step[0] == "out":
                        act.wait_ge(s_weigh, s * STEPS + (step[1] + 1) * TPB + 2)
                        act.wait_ge(s_ring, RING_A + s * RING + turned)
                        act.activation(o_sb, psum[:, 6:8, :].rearrange("p a q -> p (a q)"), ACT.Copy).then_inc(s_out_free, 1)

            over_slots(act, slot)

        @block.vector
        def _(dve):
            dve.memset(psum[:, 6:8, :], 0.0).then_inc(s_init, 1)
            for u in range(NU):
                dve.memset(k_rep[u][64:96, :, :], 1.0).then_inc(s_init, 1)
            dve.sem_inc(s_ring_free, 2)

            def run(step, u, s, n, pair):
                kind = step[0]
                bank = psum[:, 4 + pair]
                dve.wait_ge(s_ring, n + 1)
                if kind == "max_g":
                    _, h, i = step
                    pieces, (first, by, count) = MAX_BANKS[i]
                    cols = pieces[0][2]
                    dve.tensor_reduce(maxima[G][:, h, first:first + by * (count - 1) + 1:by],
                                      bank[:, 0:count * cols].rearrange("p (c k) -> p c k", c=count), AX.X,
                                      ALU.max).then_inc(s_ring_free, 1)
                elif kind == "max_l":
                    _, h = step
                    dve.tensor_reduce(maxima[L][:, h, 0:TPB], bank.rearrange("p (t k) -> p t k", t=TPB), AX.X,
                                      ALU.max).then_inc(s_ring_free, 1)
                elif kind == "turn_m":
                    quad = step[1]
                    if s is not None:
                        dve.wait_ge(s_m[quad], (s + 1) * ROWS)
                    dve.tensor_copy(m_rows[quad][0:96, :], bank.bitcast(BF16)[0:96, 0:P]).then_inc(s_mrows[quad], 1)
                    dve.wait_ge(s_mrows[quad], 1 if s is None else s + 2)
                    dve.sem_inc(s_ring_free, 1)
            def after(step, s, n):
                if step == ("max_g", 3, len(MAX_BANKS) - 1):
                    dve.wait_ge(s_ring_free, n + 3)
                    m = maxima[G]
                    dve.tensor_tensor(m[:, :, 4:8], m[:, :, 4:8], m[:, :, 8:12], ALU.max).then_inc(s_max[G], 1)
                elif step == ("max_l", 3):
                    dve.wait_ge(s_ring_free, n + 3)
                    dve.sem_inc(s_max[L], 1)

            n = 0
            for step in sum(max_steps(), []):
                run(step, None, None, n, n % 2)
                after(step, None, n)
                n += 1

            def slot(b, u, s, more):
                n = 0
                for step in slot_steps(more):
                    if step[0] in ("max_g", "max_l", "turn_m"):
                        run(step, u, s, RING_A + s * RING + n, n % 2)
                        after(step, s, RING_A + s * RING + n)
                        n += 1
                    elif step[0] == "turn_o":
                        _, quad, c = step
                        h0 = 4 * (u + NU * quad)
                        bank = psum[:, 4 + n % 2].rearrange("p (t h w) -> p t h w", t=4, h=4)
                        k = s * 4 + quad * 2 + c
                        dve.wait_ge(s_ring, RING_A + s * RING + n + 1)
                        dve.reciprocal(inv[c], bank[:, :, :, D]).then_inc(s_inv, 1)
                        dve.wait_ge(s_inv, k + 1)
                        dve.tensor_tensor(
                            attn_sb[:, bass.ds(b * TPB + 4 * c, 4), h0 * D:(h0 + 4) * D].rearrange("p t (h d) -> p t h d", h=4),
                            bank[:, :, :, 0:D], inv[c].unsqueeze(3).broadcast_to([P, 4, 4, D]),
                            ALU.mult).then_inc(s_ring_free, 1)
                        n += 1

            over_slots(dve, slot)

        @block.tensor
        def _(pe):
            def ring_bank(n, pair):
                pe.wait_ge(s_ring_free, n + 1)
                return psum[:, 4 + pair]

            def run(step, u, batch, unit, n, pair):
                kind = step[0]
                if step == ("max_g", 0, 0):
                    pe.wait_ge(s_load[u][G], (batch + 1) * LOADS)
                if step == ("max_l", 0):
                    pe.wait_ge(s_load[u][L], (batch + 1) * LOADS)
                if kind == "turn_m":
                    quad = step[1]
                    pe.wait_ge(s_mparts[quad], unit + 1)
                    bank = ring_bank(n, pair)
                    pe.transpose(bank.bitcast(BF16)[0:96, 0:P], m_parts[quad].rearrange("p i h t -> p (i h t)"),
                                 identb[:, :]).then_inc(s_ring, 1)
                    return
                bank = ring_bank(n, pair)
                if kind == "max_g":
                    _, h, i = step
                    for qt, k0, cols, to in MAX_BANKS[i][0]:
                        last = k0 + cols == (qt + 1) * P
                        mm = pe.matmul(bank[:, to:to + cols], q_rep[u][0:KS, h, qt * P:(qt + 1) * P],
                                       k_rep[u][0:KS, h, k0:k0 + cols], start=True, stop=not last)
                        if last:
                            mm = pe.matmul(bank[:, to + cols - P:to + cols], identb[:, :], mask_qk[:, :],
                                           start=False, stop=True)
                else:
                    _, h = step
                    pe.matmul(bank, identb[:, :], mask_lq[:, :, :].rearrange("p t k -> p (t k)"), start=True, stop=False,
                              skip_group_check=True)
                    for t in range(TPB):
                        for j in range(P // WINDOW):
                            q0 = t * P + j * WINDOW
                            k0 = max(q0 - WINDOW, 0)
                            c0 = t * 2 * WINDOW + k0 - (q0 - WINDOW)
                            cols = q0 + WINDOW - k0
                            mm = pe.matmul(bank[j * WINDOW:(j + 1) * WINDOW, c0:c0 + cols],
                                           q_rep[u][0:KS, 4 + h, q0:q0 + WINDOW], k_rep[u][0:KS, 4 + h, k0:k0 + cols],
                                           start=False, stop=True, skip_group_check=True)
                mm.then_inc(s_ring, 1)

            pe.sem_inc(s_weigh, 2)
            pe.wait_ge(s_init, 3)
            n = 0
            for step in sum(max_steps(), []):
                run(step, 0, 0, 0, n, n % 2)
                n += 1

            def slot(b, u, s, more):
                n = r = 0
                for step in slot_steps(more):
                    kind = step[0]
                    if kind == "score_g":
                        _, kb, i = step
                        if kb == 0 and i == 0:
                            pe.wait_ge(s_m[G], (s + 1) * ROWS)
                        pe.wait_ge(s_exp, s * SCORES + n + 1)
                        cols = S - kb * P
                        for h in ([i] if kb < 4 else [2 * i, 2 * i + 1]):
                            for c0 in range(0, cols, HALF):
                                bank = 2 * (n % 2) + (c0 // HALF if kb < 4 else h % 2)
                                w = min(HALF, cols - c0)
                                mm = pe.matmul(psum[:, bank, 0:w], k_rep[u][0:KM, h, kb * P:(kb + 1) * P],
                                               q_rep[u][0:KM, h, kb * P + c0:kb * P + c0 + w],
                                               start=True, stop=c0 > 0)
                                if c0 == 0:
                                    mm = pe.matmul(psum[:, bank, 0:P], identb[:, :], mask_kq[:, :], start=False, stop=True)
                        mm.then_inc(s_score, 1)
                        n += 1
                    elif kind == "score_l":
                        kt = step[1]
                        if kt == 0:
                            pe.wait_ge(s_m[L], (s + 1) * ROWS)
                        pe.wait_ge(s_exp, s * SCORES + n + 1)
                        w = min(BAND, S - kt * P)
                        for a in range(2):
                            bank = 2 * (n % 2) + a
                            pe.matmul(psum[:, bank, 0:2 * BAND], identb[:, :],
                                      mask_lk[:, :, :].rearrange("p c q -> p (c q)"), start=True, stop=False,
                                      skip_group_check=True)
                            for c in range(2):
                                h = 4 + 2 * a + c
                                mm = pe.matmul(psum[:, bank, c * BAND:c * BAND + w], k_rep[u][0:KM, h, kt * P:(kt + 1) * P],
                                               q_rep[u][0:KM, h, kt * P:kt * P + w], start=False, stop=True,
                                               skip_group_check=True)
                        mm.then_inc(s_score, 1)
                        n += 1
                    elif kind == "weigh_g":
                        kb = step[1]
                        done = (4 * (kb + 1) if kb < 4 else 16 + 2 * (kb - 3))
                        pe.wait_ge(s_exp, s * SCORES + done + 2)
                        if kb == 0:
                            pe.wait_ge(s_out_free, s * 2 + 1)
                        for half in range(2):
                            q0 = max(kb * P, half * HALF)
                            w = (half + 1) * HALF - q0
                            if w <= 0:
                                continue
                            for h in range(4):
                                mm = pe.matmul(psum[32 * h:32 * h + VW, 6 + half, q0 - half * HALF:HALF], v_u[u][:, kb, h, :],
                                               probs[kb % 2][:, h, q0 - kb * P:q0 - kb * P + w], start=kb == 0,
                                               stop=kb == (3 if half == 0 else 7), skip_group_check=True)
                        mm.then_inc(s_weigh, 1)
                    elif kind == "weigh_l":
                        kt = step[1]
                        pe.wait_ge(s_exp, s * SCORES + 24 + kt + 1 + 2)
                        if kt == 0:
                            pe.wait_ge(s_out_free, s * 2 + 2)
                        end = min(kt * P + BAND, S)
                        for half in range(2):
                            q0, q1 = max(kt * P, half * HALF), min(end, (half + 1) * HALF)
                            if q1 <= q0:
                                continue
                            first = kt == 0 or (half == 1 and kt == 3)
                            for h in range(4):
                                mm = pe.matmul(psum[32 * h:32 * h + VW, 6 + half, q0 - half * HALF:q1 - half * HALF],
                                               v_u[u][:, kt, 4 + h, :], probs[kt % 2][:, h, q0 - kt * P:q1 - kt * P],
                                               start=first, stop=True, skip_group_check=True)
                        mm.then_inc(s_weigh, 1)
                    elif kind == "turn_o":
                        _, quad, c = step
                        pe.wait_ge(s_out_free, s * 2 + quad + 2)
                        bank = ring_bank(RING_A + s * RING + r, r % 2)
                        for t in range(4):
                            mm = pe.transpose(bank[:, t * P:(t + 1) * P], o_sb[:, (4 * c + t) * P:(4 * c + t + 1) * P], ident[:, :])
                        mm.then_inc(s_ring, 1)
                        r += 1
                    elif kind in ("max_g", "max_l", "turn_m"):
                        run(step, 1 - u, b + u, s + 1, RING_A + s * RING + r, r % 2)
                        r += 1

            over_slots(pe, slot)



def feed_forward(nc, sem, psum, work, x_sb, attn_sb, ident, mod_cols, mod_rows, woT, wrT, gate_up, down, wgT,
                 wuT, wdT, sorted_d, expert_d, out):
    at = [0]

    def part(n, dt=F32):
        a = work[:, at[0]:at[0] + n]
        at[0] += n
        return a

    wo_sb, wr_sb = part(E), part(NE)
    wg_sb, wu_sb = part(F), part(F)
    wd_sb = part(2 * E).rearrange("p (c e) -> p c e", c=2)
    w_all = part(NE * WE)
    stage, attnT, xn, h2T, tmp = part(HALF), part(HALF), part(HALF), part(HALF), part(HALF)
    silu = part(2 * HALF).rearrange("p (c s) -> p c s", c=2)
    act_s = part(2 * HALF).rearrange("p (c s) -> p c s", c=2)
    stats = part(4 * 6).rearrange("p (t s) -> p t s", t=4)
    mv = part(4 * 2).rearrange("p (t s) -> p t s", t=4)
    half_neg, ve, rstd, mod_b = part(4), part(4), part(4), part(2)
    x2 = part(HALF).rearrange("p (t e) -> p t e", t=4)
    h2m, cb_row = part(HALF), part(E)
    logits = part(NT * NE).rearrange("p (t e) -> p t e", t=NT)
    blank_at = at[0]
    blank = part(ET * RW).rearrange("p (r e) -> p r e", r=ET)
    rows_sb = part(NT * RW).rearrange("p (t e) -> p t e", t=NT)
    top, gate_of, best, pos_f, pos = part(NT), part(NT), part(NT), part(NT), part(NT).bitcast(I32)
    pick = part(NT * NE).rearrange("p (t e) -> p t e", t=NT)
    pick_b = part(NT * NE // 2).bitcast(BF16).rearrange("p (t e) -> p t e", t=NT)
    lower = part(NE)
    steps_of = part(NT)
    tri16 = part(NE * NE).rearrange("p (e f) -> p e f", e=NE)
    before = part(P // 2).bitcast(BF16)
    ones = part(P // 2).bitcast(BF16)
    slots = part(ET)
    count, tiles, ends, starts = part(NE), part(NE), part(NE), part(NE)
    cmp = part(ET * NE)
    expert_f = part(ET)
    expert = part(ET).bitcast(I32)
    behind = at[0]
    at[0] = blank_at
    h_in = [part(RW) for _ in range(8)]
    h_inT = [part(P) for _ in range(4)]
    w_tile = [part(WE) for _ in range(4)]
    silu_e = [part(2 * P) for _ in range(2)]
    act_e = [part(2 * P) for _ in range(2)]
    y_out = [part(P) for _ in range(4)]
    assert at[0] <= blank_at + ET * RW <= behind

    dense(nc, sem, psum, x_sb, attn_sb, ident, mod_cols, mod_rows, woT, wrT, gate_up, down, wgT, wuT, wdT, sorted_d,
          wo_sb, wr_sb, wg_sb, wu_sb, wd_sb, w_all, stage, attnT, xn, h2T, tmp, silu, act_s, stats, mv,
          half_neg, ve, rstd, mod_b, logits, blank, x2, h2m, cb_row)
    route(nc, sem, psum, attn_sb, rows_sb, sorted_d, logits, top, gate_of, best, pos_f, pos, pick, pick_b, lower, steps_of,
          tri16, before, ones, slots, count, tiles, ends, starts, cmp, expert_f, expert)
    experts(nc, sem, psum, ident, sorted_d, expert_d, w_all, expert, h_in, h_inT, w_tile, silu_e, act_e, y_out)
    combine(nc, sem, x_sb, attn_sb, mod_rows, expert_d, out)


def dense(nc, sem, psum, x_sb, attn_sb, ident, mod_cols, mod_rows, woT, wrT, gate_up, down, wgT, wuT, wdT, sorted_d,
          wo_sb, wr_sb, wg_sb, wu_sb, wd_sb, w_all, stage, attnT, xn, h2T, tmp, silu, act_s, stats, mv,
          half_neg, ve, rstd, mod_b, logits, blank, x2, h2m, cb_row):
    s_w, s_ew = sem("dense_weights_in"), sem("expert_weights_in")
    s_zero, s_zeroed = sem("dense_zeros_made"), sem("sorted_rows_zeroed")
    s_stage, s_aT, s_attnT, s_y = sem("attn_staged"), sem("attn_turned"), sem("attnT_ready"), sem("attn_projected")
    s_gated, s_x2 = sem("attn_gated"), sem("x2_ready")
    s_stat, s_aggr, s_ve, s_rstd, s_xn = (sem("stats2_done"), sem("aggr2_done"), sem("ve2_done"), sem("rstd2_done"),
                                          sem("xn2_done"))
    s_modb = sem("mod2_copied")
    s_xT, s_h2T, s_h2m, s_h2 = sem("xn2_turned"), sem("h2T_ready"), sem("h2_scaled"), sem("h2_ready")
    s_log, s_logs = sem("logits_summed"), sem("logits_copied")
    s_gate, s_up, s_silu, s_act = sem("gate_ready"), sem("up_ready"), sem("silu_ready"), sem("act_ready")
    s_dn, s_dng, s_x3 = sem("shared_ready"), sem("shared_gated"), sem("x3_ready")

    with nc.Block() as block:
        @block.sync
        def _(sp):
            sp.dma_start(wo_sb, woT).then_inc(s_w, 16)
            sp.dma_start(wr_sb, wrT).then_inc(s_w, 16)
            sp.dma_start(wg_sb, wgT).then_inc(s_w, 16)
            sp.dma_start(wu_sb, wuT).then_inc(s_w, 16)
            sp.dma_start(wd_sb, wdT.rearrange("(c p) e -> p c e", p=P)).then_inc(s_w, 16)
            w_e = w_all.rearrange("p (e w) -> p e w", e=NE)
            sp.dma_start(w_e[:, :, 0:2 * F], gate_up.rearrange("e h f -> h e f")).then_inc(s_ew, 16)
            for f in range(2):
                sp.dma_start(w_e[:, :, 2 * F + f * E:2 * F + (f + 1) * E],
                             down[:, f * P:(f + 1) * P, :].rearrange("e p h -> p e h")).then_inc(s_ew, 16)
            sp.wait_ge(s_zero, 3)
            for n in range(ET // 8):
                sp.dma_start(sorted_d[n * 8 * P:(n + 1) * 8 * P, :].rearrange("(r p) e -> p r e", p=P),
                             blank[:, n * 8:(n + 1) * 8, :]).then_inc(s_zeroed, 16)
            sp.wait_ge(s_ew, 48)
            sp.wait_ge(s_zeroed, 16 * (ET // 8))

        @block.gpsimd
        def _(pool):
            pool.memset(blank[:, :, 0:E], 0.0).then_inc(s_zero, 1)
            pool.iota(blank[:, :, E:E + 1].bitcast(I32), pattern=[[P, ET], [0, 1]], base=NT * P,
                      channel_multiplier=1).then_inc(s_zero, 1)
            pool.memset(half_neg, -0.5).then_inc(s_zero, 1)
            pool.wait_ge(s_zero, 3)
            with pool.Fori(0, B) as b:
                for c in range(2):
                    n = b * 2 + c
                    pool.wait_ge(s_ve, n + 1)
                    pool.tensor_tensor(rstd, ve, half_neg, ALU.pow).then_inc(s_rstd, 1)
                    pool.wait_ge(s_xn, n + 1)
                    pool.tensor_tensor(h2m.rearrange("p (t e) -> p t e", t=4), xn.rearrange("p (t e) -> p t e", t=4),
                                       cb_row.unsqueeze(1).broadcast_to([P, 4, E]), ALU.mult).then_inc(s_h2m, 1)

        @block.scalar
        def _(act):
            act.sem_inc(s_h2T, 1)
            with act.Fori(0, B) as b:
                for c in range(2):
                    n = b * 2 + c
                    act.activation(stage.rearrange("p (t e) -> p t e", t=4), attn_sb[:, bass.ds(b * TPB + 4 * c, 4), :],
                                   ACT.Copy).then_inc(s_stage, 1)
                    act.wait_ge(s_aT, n + 1)
                    act.activation(attnT, psum[:, 0, :], ACT.Copy).then_inc(s_attnT, 1)
                    act.wait_ge(s_xT, n + 1)
                    act.wait_ge(s_modb, b * 2 + 1)
                    act.activation(h2T, psum[:, 2, :], ACT.Identity, scale=mod_b[:, 1:2], bias=mod_b[:, 0:1])\
                        .then_inc(s_h2T, 1)
                    act.wait_ge(s_gate, n + 1)
                    act.wait_ge(s_act, n + 1)
                    act.activation(silu, psum[:, 4:6, :], ACT.Silu).then_inc(s_silu, 1)

        @block.vector
        def _(dve):
            dve.sem_inc(s_act, 1)
            dve.sem_inc(s_dng, 1)
            with dve.Fori(0, B) as b:
                for c in range(2):
                    n = b * 2 + c
                    x4 = x_sb[:, bass.ds(b * TPB + 4 * c, 4), :]
                    tmp4 = tmp.rearrange("p (t e) -> p t e", t=4)

                    def row(j):
                        return mod_rows[:, bass.ds(b, 1), j, :].broadcast_to([P, 4, E])

                    if c == 0:
                        dve.wait_ge(s_h2T, n + 1)
                        dve.tensor_copy(mod_b, mod_cols[:, 2:4, bass.ds(b, 1)].rearrange("p j o -> p (j o)")).then_inc(s_modb, 1)
                        dve.tensor_copy(cb_row, mod_rows[:, bass.ds(b, 1), 2, :].rearrange("p o e -> p (o e)")).then_inc(s_modb, 1)
                    dve.wait_ge(s_y, n + 1)
                    dve.tensor_tensor(tmp4, psum[:, 1, :].rearrange("p (t e) -> p t e", t=4), row(0), ALU.mult).then_inc(s_gated, 1)
                    dve.wait_ge(s_gated, n + 1)
                    dve.tensor_tensor(x2, x4, tmp4, ALU.add).then_inc(s_x2, 1)
                    dve.wait_ge(s_x2, n + 1)
                    for t in range(4):
                        dve.bn_stats(stats[:, t, :], x2[:, t, :]).then_inc(s_stat, 1)
                    dve.wait_ge(s_stat, n * 4 + 4)
                    dve.tensor_copy(ve, stats[:, :, 0]).then_inc(s_aggr, 1)
                    for t in range(4):
                        dve.bn_aggr(mv[:, t, :], stats[:, t, :]).then_inc(s_aggr, 1)
                    dve.wait_ge(s_aggr, n * 5 + 5)
                    dve.tensor_scalar(ve, mv[:, :, 1], EPS, None, ALU.add).then_inc(s_ve, 1)
                    dve.wait_ge(s_rstd, n + 1)
                    for t in range(4):
                        st = dve.tensor_scalar(xn[:, t * E:(t + 1) * E],
                                               x2[:, t, :], mv[:, t, 0:1], rstd[:, t:t + 1], ALU.subtract, ALU.mult)
                    st.then_inc(s_xn, 1)
                    dve.wait_ge(s_h2m, n + 1)
                    dve.tensor_tensor(attn_sb[:, bass.ds(b * TPB + 4 * c, 4), :], h2m.rearrange("p (t e) -> p t e", t=4),
                                      row(1), ALU.add).then_inc(s_h2, 1)
                    dve.wait_ge(s_log, n + 1)
                    dve.tensor_copy(logits[:, bass.ds(b * TPB + 4 * c, 4), :],
                                    psum[:, 3, 0:4 * NE].rearrange("p (t e) -> p t e", t=4)).then_inc(s_logs, 1)
                    dve.wait_ge(s_up, n + 1)
                    dve.wait_ge(s_silu, n + 1)
                    dve.tensor_tensor(act_s, psum[:, 6:8, :], silu, ALU.mult).then_inc(s_act, 1)
                    dve.wait_ge(s_dn, n + 1)
                    dve.tensor_tensor(tmp4, psum[:, 0, :].rearrange("p (t e) -> p t e", t=4), row(3), ALU.mult).then_inc(s_dng, 1)
                    dve.wait_ge(s_dng, n + 2)
                    dve.tensor_tensor(x4, x2, tmp4, ALU.add).then_inc(s_x3, 1)
                    dve.wait_ge(s_x3, n + 1)

        @block.tensor
        def _(pe):
            pe.wait_ge(s_w, 80)
            with pe.Fori(0, B) as b:
                for c in range(2):
                    n = b * 2 + c
                    tile = [slice(t * P, (t + 1) * P) for t in range(4)]
                    pe.wait_ge(s_stage, n + 1)
                    pe.wait_ge(s_dng, n + 1)
                    for t in range(4):
                        mm = pe.transpose(psum[:, 0, tile[t]], stage[:, tile[t]], ident[:, :])
                    mm.then_inc(s_aT, 1)
                    pe.wait_ge(s_attnT, n + 1)
                    for t in range(4):
                        mm = pe.matmul(psum[:, 1, tile[t]], attnT[:, tile[t]], wo_sb, start=True, stop=True)
                    mm.then_inc(s_y, 1)
                    pe.wait_ge(s_xn, n + 1)
                    for t in range(4):
                        mm = pe.transpose(psum[:, 2, tile[t]], xn[:, tile[t]], ident[:, :])
                    mm.then_inc(s_xT, 1)
                    pe.wait_ge(s_h2T, n + 2)
                    for t in range(4):
                        mm = pe.matmul(psum[:, 3, t * NE:(t + 1) * NE], h2T[:, tile[t]], wr_sb, start=True, stop=True)
                    mm.then_inc(s_log, 1)
                    for f in range(2):
                        mm = pe.matmul(psum[:, 4 + f, :], wg_sb[:, f * P:(f + 1) * P], h2T, start=True, stop=True)
                    mm.then_inc(s_gate, 1)
                    for f in range(2):
                        mm = pe.matmul(psum[:, 6 + f, :], wu_sb[:, f * P:(f + 1) * P], h2T, start=True, stop=True)
                    mm.then_inc(s_up, 1)
                    pe.wait_ge(s_act, n + 2)
                    for t in range(4):
                        for f in range(2):
                            mm = pe.matmul(psum[:, 0, tile[t]], act_s[:, f, tile[t]], wd_sb[:, f, :], start=f == 0, stop=f == 1)
                    mm.then_inc(s_dn, 1)


def route(nc, sem, psum, attn_sb, rows_sb, sorted_d, logits, top, gate_of, best, pos_f, pos, pick, pick_b, lower, steps_of,
          tri16, before, ones, slots, count, tiles, ends, starts, cmp, expert_f, expert):
    s_c, s_v = sem("route_constants"), sem("route_steps")
    s_top, s_sig, s_pick = sem("top_logit_ready"), sem("gates_ready"), sem("pick_ready")
    s_places, s_counts = sem("places_summed"), sem("counts_summed")
    s_scaled, s_pos, s_scat = sem("rows_scaled"), sem("places_ready"), sem("rows_sorted")

    with nc.Block() as block:
        @block.gpsimd
        def _(pool):
            small = dict(allow_small_or_imprecise_dtypes=True)
            pool.iota(lower, pattern=[[-1, NE]], base=NE, channel_multiplier=0, **small).then_inc(s_c, 1)
            pool.iota(steps_of, pattern=[[P, NT]], base=0, channel_multiplier=0, **small).then_inc(s_c, 1)
            pool.iota(slots, pattern=[[1, ET]], base=0, channel_multiplier=0, **small).then_inc(s_c, 1)
            pool.memset(tri16, 1.0).then_inc(s_c, 1)
            pool.memset(before, 1.0).then_inc(s_c, 1)
            pool.memset(ones, 1.0).then_inc(s_c, 1)
            pool.wait_ge(s_c, 6)
            pool.affine_select(out=tri16, in_=tri16, compare_op=ALU.is_ge, fill=0.0, base=0,
                               pattern=[[1, NE], [-1, NE]], channel_multiplier=0).then_inc(s_c, 1)
            pool.affine_select(out=before, in_=before, compare_op=ALU.is_gt, fill=0.0, base=0,
                               pattern=[[1, P]], channel_multiplier=-1).then_inc(s_c, 1)
            pool.iota(rows_sb[:, :, E:E + 1].bitcast(I32), pattern=[[P, NT], [0, 1]], base=0,
                      channel_multiplier=1).then_inc(s_c, 1)
            pool.wait_ge(s_c, 9)
            pool.wait_ge(s_pos, 1)
            for t in range(NT):
                if t % TPB == 0:
                    pool.wait_ge(s_scaled, t // TPB + 1)
                pool.indirect_dma_start(sorted_d[:, :], bass.IndirectOffsetOnAxis(ap=pos[:, t:t + 1], axis=0),
                                        rows_sb[:, t, :], None).then_inc(s_scat, 16)
            pool.wait_ge(s_scat, 16 * NT)

        @block.scalar
        def _(act):
            act.wait_ge(s_top, 1)
            act.activation(gate_of, top, ACT.Sigmoid).then_inc(s_sig, 1)

        @block.vector
        def _(dve):
            done = [0]

            def then(ins):
                done[0] += 1
                ins.then_inc(s_v, 1)
                dve.wait_ge(s_v, done[0])

            shape = [P, NT, NE]
            dve.tensor_reduce(top, logits, AX.X, ALU.max).then_inc(s_top, 1)
            dve.wait_ge(s_top, 1)
            then(dve.tensor_tensor(pick, logits, top.unsqueeze(2).broadcast_to(shape), ALU.is_equal))
            dve.wait_ge(s_c, 8)
            then(dve.tensor_tensor(pick, pick, lower.unsqueeze(1).broadcast_to(shape), ALU.mult))
            then(dve.tensor_reduce(best, pick, AX.X, ALU.max))
            then(dve.tensor_tensor(pick, lower.unsqueeze(1).broadcast_to(shape), best.unsqueeze(2).broadcast_to(shape),
                                   ALU.is_equal))
            dve.tensor_copy(pick_b, pick).then_inc(s_pick, 1)
            dve.wait_ge(s_sig, 1)
            for b in range(B):
                rows = attn_sb[:, b * TPB:(b + 1) * TPB, :]
                dve.tensor_tensor(rows_sb[:, b * TPB:(b + 1) * TPB, 0:E], rows, gate_of[:, b * TPB:(b + 1) * TPB].unsqueeze(2).broadcast_to([P, TPB, E]),
                                  ALU.mult).then_inc(s_scaled, 1)
            dve.wait_ge(s_counts, 1)
            then(dve.tensor_reduce(count, psum[:, 1, :].rearrange("p (t e) -> p e t", t=NT), AX.X, ALU.add))
            cmp_n = cmp[:, 0:NE * NT].rearrange("p (e n) -> p e n", e=NE)
            then(dve.tensor_tensor(cmp_n, count.unsqueeze(2).broadcast_to([P, NE, NT]),
                                   steps_of.unsqueeze(1).broadcast_to([P, NE, NT]), ALU.is_gt))
            then(dve.tensor_reduce(tiles, cmp_n, AX.X, ALU.add))
            cmp_e = cmp[:, 0:NE * NE].rearrange("p (e f) -> p e f", e=NE)
            then(dve.tensor_tensor(cmp_e, tri16, tiles.unsqueeze(1).broadcast_to([P, NE, NE]), ALU.mult))
            then(dve.tensor_reduce(ends, cmp_e, AX.X, ALU.add))
            then(dve.tensor_tensor(starts, ends, tiles, ALU.subtract))
            then(dve.tensor_scalar(starts, starts, float(P), None, ALU.mult))
            dve.wait_ge(s_places, 1)
            placed = cmp[:, 0:NT * NE].rearrange("p (t e) -> p t e", t=NT)
            then(dve.tensor_tensor(placed, psum[:, 0, :].rearrange("p (t e) -> p t e", t=NT),
                                   starts.unsqueeze(1).broadcast_to(shape), ALU.add))
            then(dve.tensor_tensor(placed, placed, pick, ALU.mult))
            then(dve.tensor_reduce(pos_f, placed, AX.X, ALU.add))
            dve.tensor_copy(pos, pos_f).then_inc(s_pos, 1)
            cmp_s = cmp.rearrange("p (s e) -> p s e", s=ET)
            then(dve.tensor_tensor(cmp_s, slots.unsqueeze(2).broadcast_to([P, ET, NE]),
                                   ends.unsqueeze(1).broadcast_to([P, ET, NE]), ALU.is_ge))
            then(dve.tensor_reduce(expert_f, cmp_s, AX.X, ALU.add))
            then(dve.tensor_scalar(expert_f, expert_f, float(NE - 1), None, ALU.min))
            then(dve.tensor_copy(expert, expert_f))

        @block.tensor
        def _(pe):
            pe.wait_ge(s_c, 8)
            pe.wait_ge(s_pick, 1)
            flat = pick_b.rearrange("p t e -> p (t e)")
            pe.matmul(psum[:, 1, :], ones, flat, start=True, stop=True).then_inc(s_counts, 1)
            pe.matmul(psum[:, 0, :], before, flat, start=True, stop=False)
            for t in range(NT - 1):
                mm = pe.matmul(psum[:, 0, (t + 1) * NE:], ones, pick_b[:, t:t + 1, :].broadcast_to([P, NT - 1 - t, NE]),
                               start=False, stop=t == NT - 2)
            mm.then_inc(s_places, 1)


def experts(nc, sem, psum, ident, sorted_d, expert_d, w_all, expert, h_in, h_inT, w_tile, silu_e, act_e, y_out):
    s_in = [sem(f"rows{i}_in") for i in range(8)]
    s_turn, s_hT, s_w = sem("rows_turned"), sem("rowsT_ready"), sem("expert_weights_copied")
    s_gu, s_silu, s_act = sem("expert_gate_up_ready"), sem("expert_silu_ready"), sem("expert_act_ready")
    s_y, s_yout = sem("expert_rows_ready"), sem("expert_rows_copied")
    s_told = sem("store_begun")
    s_back = [sem(f"expert_rows{i}_stored") for i in range(4)]
    LOOPS = ET // 8 - 1

    def over_tiles(eng, step):
        for c in range(4):
            step(0, c)
        with eng.Fori(0, LOOPS) as i:
            for c in range(4, 12):
                step(i, c)
        for c in range(4, 8):
            step(LOOPS, c)

    def wait(eng, s, i, per, more):
        if not isinstance(i, int) or per * i + more > 0:
            eng.wait_ge(s, i * per + more)

    def exists(i, c):
        return not isinstance(i, int) or i * 8 + c < ET

    with nc.Block() as block:
        @block.sync
        def _(sp):
            def load(i, c):
                sp.dma_start(h_in[c % 8], sorted_d[bass.ds(i * 8 * P + c * P, P), :]).then_inc(s_in[c % 8], 16)

            for c in range(8):
                load(0, c)

            with sp.Fori(0, LOOPS) as i:
                for c in range(8):
                    sp.wait_ge(s_back[c % 4], i * 32 + (c // 4) * 16 + 16)
                    load(i, c + 8)

        @block.gpsimd
        def _(pool):
            def step(i, c):
                wait(pool, s_yout, i, 8, c + 1)
                pool.sem_inc(s_told, 1)
                pool.indirect_dma_start(expert_d[:, :],
                                        bass.IndirectOffsetOnAxis(ap=h_in[c % 8][:, E:E + 1].bitcast(I32), axis=0),
                                        y_out[c % 4], None).then_inc(s_back[c % 4], 16)

            over_tiles(pool, step)
            for s in s_back:
                pool.wait_ge(s, 16 * ET // 4)

        @block.scalar
        def _(act):
            def turn(i, c):
                if exists(i, c):
                    wait(act, s_turn, i, 8, c + 1)
                    wait(act, s_gu, i, 8, c - 3)
                    act.activation(h_inT[c % 4], psum[:, c % 2, 0:P], ACT.Copy).then_inc(s_hT, 1)

            def silu(i, c):
                if exists(i, c):
                    wait(act, s_gu, i, 8, c + 1)
                    wait(act, s_act, i, 8, c - 1)
                    act.activation(silu_e[c % 2], psum[:, 2 + c % 2, 0:2 * P], ACT.Silu).then_inc(s_silu, 1)

            def copy_out(i, c):
                wait(act, s_y, i, 8, c + 1)
                wait(act, s_back[c % 4], i, 32, (c // 4) * 16)
                act.activation(y_out[c % 4], psum[:, 4 + c % 2, 0:P], ACT.Copy).then_inc(s_yout, 1)

            def step(i, c):
                turn(i, c + 3)
                silu(i, c + 1)
                copy_out(i, c)

            for c in range(3):
                turn(0, c)
            silu(0, 0)
            over_tiles(act, step)

        @block.vector
        def _(dve):
            def copy_weights(i, c):
                if exists(i, c):
                    e = dve.value_load(expert[0:1, bass.ds(i * 8 + c, 1)], min_val=0, max_val=NE - 1)
                    wait(dve, s_y, i, 8, c - 3)
                    dve.tensor_copy(w_tile[c % 4], w_all[:, bass.ds(e * WE, WE)]).then_inc(s_w, 1)

            def mult(i, c):
                if exists(i, c):
                    wait(dve, s_silu, i, 8, c + 1)
                    wait(dve, s_y, i, 8, c - 1)
                    dve.tensor_tensor(act_e[c % 2], psum[:, 2 + c % 2, 2 * P:4 * P], silu_e[c % 2], ALU.mult).then_inc(s_act, 1)

            def step(i, c):
                copy_weights(i, c + 3)
                mult(i, c + 1)

            for c in range(3):
                copy_weights(0, c)
            mult(0, 0)
            over_tiles(dve, step)

        @block.tensor
        def _(pe):
            def turn(i, c):
                if exists(i, c):
                    wait(pe, s_in[c % 8], i, 16, (c // 8) * 16 + 16)
                    wait(pe, s_hT, i, 8, c - 1)
                    pe.transpose(psum[:, c % 2, 0:P], h_in[c % 8][:, 0:E], ident[:, :]).then_inc(s_turn, 1)

            def gate_up(i, c):
                if exists(i, c):
                    wait(pe, s_hT, i, 8, c + 1)
                    wait(pe, s_w, i, 8, c + 1)
                    wait(pe, s_act, i, 8, c - 1)
                    for f in range(4):
                        mm = pe.matmul(psum[:, 2 + c % 2, f * P:(f + 1) * P], w_tile[c % 4][:, f * P:(f + 1) * P],
                                       h_inT[c % 4], start=True, stop=True)
                    mm.then_inc(s_gu, 1)

            def down(i, c):
                wait(pe, s_act, i, 8, c + 1)
                wait(pe, s_yout, i, 8, c - 1)
                for f in range(2):
                    mm = pe.matmul(psum[:, 4 + c % 2, 0:P], act_e[c % 2][:, f * P:(f + 1) * P],
                                   w_tile[c % 4][:, 2 * F + f * E:2 * F + (f + 1) * E], start=f == 0, stop=f == 1)
                mm.then_inc(s_y, 1)

            def step(i, c):
                turn(i, c + 3)
                gate_up(i, c + 1)
                down(i, c)

            for c in range(3):
                turn(0, c)
            gate_up(0, 0)
            over_tiles(pe, step)


def combine(nc, sem, x_sb, attn_sb, mod_rows, expert_d, out):
    s_got = [sem(f"expert_rows_back{g}") for g in range(B)]
    s_gated, s_sum, s_out = sem("expert_rows_gated"), sem("result_ready"), sem("result_out")
    out_v = out.rearrange("b (t p) e -> p b t e", p=P)
    expert_v = expert_d[0:NT * P, :].rearrange("(b t p) e -> p b t e", b=B, p=P)

    with nc.Block() as block:
        @block.sync
        def _(sp):
            for b in range(B):
                sp.dma_start(attn_sb[:, b * TPB:(b + 1) * TPB, :], expert_v[:, b]).then_inc(s_got[b], 16)
            for b in range(B):
                sp.wait_ge(s_sum, b + 1)
                sp.dma_start(out_v[:, b], x_sb[:, b * TPB:(b + 1) * TPB, :]).then_inc(s_out, 16)
            sp.wait_ge(s_out, 16 * B)

        @block.vector
        def _(dve):
            for b in range(B):
                y = attn_sb[:, b * TPB:(b + 1) * TPB, :]
                x8 = x_sb[:, b * TPB:(b + 1) * TPB, :]
                dve.wait_ge(s_got[b], 16)
                dve.tensor_tensor(y, y, mod_rows[:, b:b + 1, 3, :].broadcast_to([P, TPB, E]), ALU.mult).then_inc(s_gated, 1)
                dve.wait_ge(s_gated, b + 1)
                dve.tensor_tensor(x8, x8, y, ALU.add).then_inc(s_sum, 1)


def kernel(L0_attn_hidden_states, L0_attn_Wq, L0_attn_Wk, L0_attn_Wv, L0_attn_Wo, L0_attn_bo, L0_ffn_w_router,
           L0_ffn_gate_up_proj, L0_ffn_down_proj, L0_ffn_w_gate, L0_ffn_w_up, L0_ffn_w_down, L0_c, L0_wmod):
    import numpy as np
    import concourse.bacc as bacc
    from concourse import mybir as mb
    from concourse.bass_utils import run_bass_kernel_spmd as run

    given = [
        ("x", L0_attn_hidden_states), ("wqT", np.transpose(L0_attn_Wq)), ("wkT", np.transpose(L0_attn_Wk)),
        ("wvT", np.transpose(L0_attn_Wv)), ("woT", np.transpose(L0_attn_Wo)), ("bo", L0_attn_bo),
        ("wrT", np.transpose(L0_ffn_w_router)), ("gate_up", L0_ffn_gate_up_proj), ("down", L0_ffn_down_proj),
        ("wgT", np.transpose(L0_ffn_w_gate)), ("wuT", np.transpose(L0_ffn_w_up)), ("wdT", np.transpose(L0_ffn_w_down)),
        ("cT", np.transpose(L0_c)), ("wmod", L0_wmod),
    ]
    nc = bacc.Bacc("TRN2", target_bir_lowering=False, num_devices=1)
    arrays, args = {}, []
    for name, a in given:
        a = np.ascontiguousarray(a)
        arrays[f"{name}_dram"] = a
        args.append(nc.dram_tensor(f"{name}_dram", a.shape, mb.dt.from_np(a.dtype), kind="ExternalInput").ap())
    out = nc.dram_tensor("out_dram", (B, S, E), F32, kind="ExternalOutput").ap()
    adaln_kernel(nc, *args, out)
    r = run(nc, [arrays], core_ids=[0])
    return r.results[0]["out_dram"]
```

```python
from contextlib import ExitStack

import concourse.bass as bass
from concourse import mybir

F32 = mybir.dt.float32
BF16 = mybir.dt.bfloat16
I32 = mybir.dt.int32
ALU = mybir.AluOpType
ACT = mybir.ActivationFunctionType
AX = mybir.AxisListType

P = 128
B, S, E = 4, 1024, 128
TPB = S // P
NT = B * TPB
H, D, WINDOW = 16, 8, 32
SCALE = D ** -0.5
NEG = -1e30
EPS = 1e-5
NE, F = 16, 256
NPART = 3
KS = NPART * NPART * D
KM = KS + NPART
VW = D + 1
UH = 8
NU = 2
UNIT = UH * S + TPB * UH * VW
BAND = P + WINDOW
ET = NT + NE
WE = 2 * F + 2 * E
REGION = B * S + P
RW = E + 1
ONES = 1 + 0x3F80 / 2 ** 23
HALF = 512


def adaln_kernel(nc, x, wqT, wkT, wvT, woT, bo, wrT, gate_up, down, wgT, wuT, wdT, cT, wmod, out):
    ctx = ExitStack()
    with ctx:
        def sb(name, shape, dt=F32):
            return ctx.enter_context(nc.sbuf_tensor(name, shape, dt))

        def sem(name):
            return ctx.enter_context(nc.semaphore(name))

        psum = ctx.enter_context(nc.psum_tensor("psum", [P, 8, HALF], F32))
        q_parts_d = nc.dram_tensor("q_parts_d", [H, NPART, D, B * S], BF16, kind="Internal").ap()
        k_parts_d = nc.dram_tensor("k_parts_d", [H, NPART, D, B * S], BF16, kind="Internal").ap()
        v_d = nc.dram_tensor("v_d", [B, P, TPB * H * VW], F32, kind="Internal").ap()

        x_sb = sb("x_sb", [P, NT, E])
        ident = sb("ident", [P, P])
        identb = sb("identb", [P, P], BF16)
        mask_qk = sb("mask_qk", [P, P], BF16)
        mask_kq = sb("mask_kq", [P, P], BF16)
        mask_lq = sb("mask_lq", [P, TPB, 2 * WINDOW], BF16)
        mask_lk = sb("mask_lk", [P, 2, BAND], BF16)
        mod_cols = sb("mod_cols", [P, 4, B])
        mod_rows = sb("mod_rows", [P, B, 4, E])
        attn_sb = sb("attn_sb", [P, NT, E])
        dense_w = dict(wo=sb("wo", [P, E]), wr=sb("wr", [P, NE]), wg=sb("wg", [P, F]), wu=sb("wu", [P, F]),
                       wd=sb("wd", [P, 2, E]), wo_gated=sb("wo_gated", [P, B, E]),
                       wd_gated=sb("wd_gated", [P, B, 2, E]), blank=sb("blank", [P, 2 * NE, RW]))
        bo_sb = sb("bo_sb", [P, E])
        work = sb("work", [P, 29000])

        sorted_d = nc.dram_tensor("sorted_d", [NE * REGION + NE * P, RW], F32, kind="Internal").ap()
        expert_d = nc.dram_tensor("expert_d", [(NT + 2 * NE) * P, E], F32, kind="Internal").ap()
        s_setup_stored = setup(nc, sem, psum, work, x, x_sb, wqT, wkT, wvT, bo, bo_sb, cT, wmod, ident, identb,
                               mask_qk, mask_kq, mask_lq, mask_lk, mod_cols, mod_rows, q_parts_d, k_parts_d, v_d)
        attention(nc, sem, psum, work, attn_sb, ident, identb, mask_qk, mask_kq, mask_lq, mask_lk, q_parts_d,
                  k_parts_d, v_d, s_setup_stored, x_sb, bo_sb, mod_rows, dense_w, woT, wrT, wgT, wuT, wdT, sorted_d)
        feed_forward(nc, sem, psum, work, x_sb, attn_sb, ident, mod_cols, mod_rows, dense_w, gate_up, down,
                     sorted_d, expert_d, out)


def q_of(work, u):
    return work[:, u * UNIT:u * UNIT + UH * S // 2].bitcast(BF16)


def k_of(work, u):
    return work[:, u * UNIT + UH * S // 2:u * UNIT + UH * S].bitcast(BF16)


def setup(nc, sem, psum, work, x, x_sb, wqT, wkT, wvT, bo, bo_sb, cT, wmod, ident, identb, mask_qk, mask_kq,
          mask_lq, mask_lk, mod_cols, mod_rows, q_parts_d, k_parts_d, v_d):
    at = [UNIT * NU]

    def part(n, dt=F32):
        a = work[:, at[0]:at[0] + n]
        at[0] += n
        return a

    q_parts = part(2 * NPART * S // 2).bitcast(BF16).rearrange("p (w i s) -> p w i s", w=2, i=NPART)
    v_sb = part(TPB * H * VW).rearrange("p (t h w) -> p t h w", t=TPB, h=H)
    wq_sb, wk_sb, wv_sb = part(E), part(E), part(E)
    wmod_sb = part(6 * E)
    c_sb, c_exp, c_silu = part(B), part(B), part(B)
    c_bc = part(B * P).rearrange("p (b m) -> p b m", b=B)
    stats = part(TPB * 6).rearrange("p (t s) -> p t s", t=TPB)
    mv = part(TPB * 2).rearrange("p (t s) -> p t s", t=TPB)
    half_neg = part(TPB)
    ve = part(TPB)
    rstd = part(TPB)
    xn = part(TPB * E).rearrange("p (t e) -> p t e", t=TPB)
    hT = part(S)
    mod_b = part(2)
    rest = part(2 * S).rearrange("p (w s) -> p w s", w=2)
    ones_of = [k_of(work, u) for u in range(NU)]

    s_wm, s_w, s_x0, s_x, s_bo = (sem("modulation_weights_in"), sem("projection_weights_in"), sem("first_x_in"),
                                  sem("other_x_in"), sem("bo_in"))
    s_const, s_zero = sem("constants_made"), sem("constants_zeroed")
    s_ones = [sem("even_rows_of_ones_set"), sem("odd_rows_of_ones_set")]
    s_cexp, s_c, s_cols, s_rows, s_rowsb = (sem("c_exp_done"), sem("c_steps"), sem("mod_cols_summed"),
                                            sem("mod_rows_summed"), sem("mod_rows_copied"))
    s_mod = sem("mod_steps")
    s_ln, s_stat, s_ve, s_rstd, s_xn = sem("ln_steps"), sem("stats_done"), sem("ve_done"), sem("rstd_done"), sem("xn_done")
    s_xT, s_hT, s_modb = sem("x_transposed"), sem("hT_done"), sem("mod_b_copied")
    s_proj, s_p1, s_rest, s_p2, s_parts = (sem("projected"), sem("first_part_done"), sem("rest_done"),
                                           sem("second_part_done"),
                                           [sem("q_parts_done"), sem("k_parts_done")])
    s_vproj, s_v = sem("v_projected"), sem("v_copied")
    s_stored = [sem("q_parts_stored"), sem("k_parts_stored")]
    s_vstored = sem("v_stored")
    s_half = sem("constants_half")

    def set_ones(eng, u):
        eng.memset(ones_of[u].bitcast(F32)[64:96, :], ONES).then_inc(s_ones[u], 1)

    def halves(w):
        return [(w * 2 + c, slice(c * HALF, (c + 1) * HALF)) for c in range(2)]

    def over_batches(eng, step):
        with eng.Fori(0, B - 1) as b:
            step(b)
        step(B - 1)

    def follows(b):
        return not isinstance(b, int) or b < B - 1

    with nc.Block() as block:
        @block.sync
        def _(sp):
            for s in (*s_stored, s_vstored):
                sp.sem_inc(s, 16)
            xv = x.rearrange("b (t p) e -> b p t e", p=P)
            sp.dma_start(x_sb[:, 0:TPB, :], xv[0]).then_inc(s_x0, 16)
            sp.dma_start(c_sb, cT).then_inc(s_wm, 16)
            sp.dma_start(wmod_sb, wmod).then_inc(s_wm, 16)
            for b in range(1, B):
                sp.dma_start(x_sb[:, b * TPB:(b + 1) * TPB, :], xv[b]).then_inc(s_x, 16)
            with sp.Fori(0, B) as b:
                cols = bass.ds(b * S, S)
                for w, parts_d in enumerate((q_parts_d, k_parts_d)):
                    sp.wait_ge(s_parts[w], b * 2 + 2)
                    for i in range(NPART):
                        sp.dma_start(parts_d[:, i, :, cols], q_parts[:, w, i]).then_inc(s_stored[w], 16)
                sp.wait_ge(s_v, b * 2 + 4)
                sp.dma_start(v_d[bass.ds(b, 1)].rearrange("o p n -> (o p) n"),
                             v_sb.rearrange("p t h w -> p (t h w)")).then_inc(s_vstored, 16)

        @block.gpsimd
        def _(pool):
            pool.dma_start(bo_sb[:, :], bo.partition_broadcast(P)).then_inc(s_bo, 16)
            set_ones(pool, 0)
            pool.wait_ge(s_ones[0], 1)
            pool.memset(half_neg, -0.5).then_inc(s_half, 1)
            pool.memset(ident[:, :], 0.0).then_inc(s_zero, 1)
            pool.wait_ge(s_zero, 1)
            pool.affine_select(out=ident[:, :], in_=ident[:, :], compare_op=ALU.not_equal, fill=1.0, base=0,
                               pattern=[[-1, P]], channel_multiplier=1).then_inc(s_const, 1)
            pool.wait_ge(s_half, 1)

            def norm(b):
                pool.wait_ge(s_ve, b + 1)
                pool.tensor_tensor(rstd, ve, half_neg, ALU.pow).then_inc(s_rstd, 1)

            norm(0)
            pool.wait_ge(s_rstd, 1)
            pool.memset(identb[:, :], 0.0).then_inc(s_zero, 1)
            pool.memset(mask_qk[:, :], 0.0).then_inc(s_zero, 1)
            pool.memset(mask_kq[:, :], 0.0).then_inc(s_zero, 1)
            pool.memset(mask_lq[:, :, :], 0.0).then_inc(s_zero, 1)
            pool.memset(mask_lk[:, :, :], 0.0).then_inc(s_zero, 1)
            pool.wait_ge(s_zero, 6)
            pool.affine_select(out=identb[:, :], in_=identb[:, :], compare_op=ALU.not_equal, fill=1.0, base=0,
                               pattern=[[-1, P]], channel_multiplier=1).then_inc(s_const, 1)
            pool.affine_select(out=mask_qk[:, :], in_=mask_qk[:, :], compare_op=ALU.is_ge, fill=NEG, base=0,
                               pattern=[[-1, P]], channel_multiplier=1).then_inc(s_const, 1)
            pool.affine_select(out=mask_kq[:, :], in_=mask_kq[:, :], compare_op=ALU.is_ge, fill=NEG, base=0,
                               pattern=[[1, P]], channel_multiplier=-1).then_inc(s_const, 1)
            pool.wait_ge(s_const, 4)
            for j in range(P // WINDOW):
                rows = mask_lq[j * WINDOW:(j + 1) * WINDOW]
                pool.affine_select(out=rows, in_=rows, compare_op=ALU.is_ge, fill=NEG, base=0,
                                   pattern=[[0, TPB], [1, 2 * WINDOW]], channel_multiplier=-1).then_inc(s_const, 1)
                pool.wait_ge(s_const, 5 + 2 * j)
                pool.affine_select(out=rows, in_=rows, compare_op=ALU.is_ge, fill=NEG, base=WINDOW,
                                   pattern=[[0, TPB], [-1, 2 * WINDOW]], channel_multiplier=1).then_inc(s_const, 1)
                pool.wait_ge(s_const, 6 + 2 * j)
            pool.affine_select(out=mask_lk[:, :, :], in_=mask_lk[:, :, :], compare_op=ALU.is_ge, fill=NEG, base=0,
                               pattern=[[0, 2], [1, BAND]], channel_multiplier=-1).then_inc(s_const, 1)
            pool.wait_ge(s_const, 13)
            pool.affine_select(out=mask_lk[:, :, :], in_=mask_lk[:, :, :], compare_op=ALU.is_ge, fill=NEG, base=WINDOW,
                               pattern=[[0, 2], [-1, BAND]], channel_multiplier=1).then_inc(s_const, 1)
            pool.memset(mask_lq[0:WINDOW, 0, 0:WINDOW], NEG).then_inc(s_const, 1)
            pool.wait_ge(s_const, 14)

            def step(b):
                if follows(b):
                    norm(b + 1)
                for n, cols in halves(1):
                    pool.wait_ge(s_p2, b * 4 + n + 1)
                    pool.tensor_tensor(q_parts[:, 1, 2, cols], rest[:, 1, cols], q_parts[:, 1, 1, cols],
                                       ALU.subtract).then_inc(s_parts[1], 1)

            over_batches(pool, step)
            pool.wait_ge(s_bo, 16)

        @block.scalar
        def _(act):
            act.sem_inc(s_v, 2)
            act.dma_start(wq_sb, wqT).then_inc(s_w, 16)
            act.dma_start(wk_sb, wkT).then_inc(s_w, 16)
            act.dma_start(wv_sb, wvT).then_inc(s_w, 16)
            act.wait_ge(s_wm, 32)
            act.activation(c_exp, c_sb, ACT.Exp, scale=-1.0).then_inc(s_cexp, 1)

            def modulate(b):
                act.wait_ge(s_modb, b + 1)
                if not isinstance(b, int) or b > 0:
                    act.wait_ge(s_vproj, b * 2)
                for c in range(2):
                    act.wait_ge(s_xT, b * 2 + c + 1)
                    act.activation(hT[:, c * HALF:(c + 1) * HALF], psum[:, c, :], ACT.Identity,
                                   scale=mod_b[:, 1:2], bias=mod_b[:, 0:1]).then_inc(s_hT, 1)

            modulate(0)

            def step(b):
                def first(w):
                    act.wait_ge(s_stored[w], b * 16 * NPART + 16)
                    for n, cols in halves(w):
                        act.wait_ge(s_proj, b * 4 + n + 1)
                        act.activation(q_parts[:, w, 0, cols], psum[:, 2 + n, :], ACT.Copy,
                                       scale=SCALE if w == 0 else 1.0).then_inc(s_p1, 1)

                def second(w):
                    for n, cols in halves(w):
                        act.wait_ge(s_rest, b * 4 + n + 5)
                        act.activation(q_parts[:, w, 1, cols], rest[:, w, cols], ACT.Copy).then_inc(s_p2, 1)

                first(0)
                second(0)
                first(1)
                act.wait_ge(s_vstored, b * 16 + 16)
                for c in range(2):
                    act.wait_ge(s_vproj, b * 2 + c + 1)
                    act.activation(v_sb[:, c * 4:(c + 1) * 4, :, 0:D],
                                   psum[:, 6 + c, :].rearrange("p (t h d) -> p t h d", t=4, h=H),
                                   ACT.Copy).then_inc(s_v, 1)
                if follows(b):
                    modulate(b + 1)
                second(1)

            over_batches(act, step)
            for b in range(B):
                act.wait_ge(s_rows, b + 1)
                act.activation(mod_rows[:, b], psum[:, b % 2, :].rearrange("p (j e) -> p j e", j=4),
                               ACT.Copy).then_inc(s_rowsb, 1)

        @block.vector
        def _(dve):
            dve.sem_inc(s_rest, 4)
            set_ones(dve, 1)

            def statistics(b):
                for t in range(TPB):
                    dve.bn_stats(stats[:, t, :], x_sb[:, bass.ds(b * TPB + t, 1), :].rearrange("p o e -> p (o e)"))\
                        .then_inc(s_stat, 1)
                dve.wait_ge(s_stat, b * TPB + TPB)
                dve.tensor_copy(ve, stats[:, :, 0]).then_inc(s_ln, 1)
                for t in range(TPB):
                    dve.bn_aggr(mv[:, t, :], stats[:, t, :]).then_inc(s_ln, 1)
                dve.wait_ge(s_ln, b * (TPB + 1) + TPB + 1)
                dve.tensor_scalar(ve, mv[:, :, 1], EPS, None, ALU.add).then_inc(s_ve, 1)

            def norm(b):
                dve.wait_ge(s_rstd, b + 1)
                if not isinstance(b, int) or b > 0:
                    dve.wait_ge(s_xT, b * 2)
                for t in range(TPB):
                    n = dve.tensor_scalar(xn[:, t, :], x_sb[:, bass.ds(b * TPB + t, 1), :].rearrange("p o e -> p (o e)"),
                                          mv[:, t, 0:1], rstd[:, t:t + 1], ALU.subtract, ALU.mult)
                n.then_inc(s_xn, 1)

            def copy_mod(b):
                dve.tensor_copy(mod_b, mod_cols[:, 0:2, bass.ds(b, 1)].rearrange("p j o -> p (j o)")).then_inc(s_modb, 1)

            dve.wait_ge(s_x0, 16)
            statistics(0)
            dve.wait_ge(s_cexp, 1)
            dve.tensor_scalar(c_exp, c_exp, 1.0, None, ALU.add).then_inc(s_c, 1)
            dve.wait_ge(s_c, 1)
            dve.reciprocal(c_exp, c_exp).then_inc(s_c, 1)
            dve.wait_ge(s_c, 2)
            dve.tensor_tensor(c_silu, c_exp, c_sb, ALU.mult).then_inc(s_c, 1)
            dve.wait_ge(s_c, 3)
            dve.tensor_copy(c_bc, c_silu.unsqueeze(2).broadcast_to([P, B, P])).then_inc(s_c, 1)
            dve.wait_ge(s_cols, 1)
            dve.tensor_copy(mod_cols[:, :, :], psum[:, 4, 0:4 * B].rearrange("p (j b) -> p j b", j=4)).then_inc(s_mod, 1)
            dve.wait_ge(s_mod, 1)
            for j in (1, 3):
                dve.tensor_scalar(mod_cols[:, j, :], mod_cols[:, j, :], 1.0, None, ALU.add).then_inc(s_mod, 1)
            dve.wait_ge(s_mod, 3)
            copy_mod(0)
            norm(0)
            dve.memset(v_sb[:, :, :, D:VW], 1.0)
            dve.wait_ge(s_x, 16 * (B - 1))

            def step(b):
                def rest_of(n, w, cols):
                    dve.wait_ge(s_p1, b * 4 + n + 1)
                    if w == 1 and (not isinstance(b, int) or b > 0):
                        dve.wait_ge(s_parts[1], b * 2)
                    dve.scalar_tensor_tensor(out=rest[:, w, cols], in0=psum[:, 2 + n, :],
                                             scalar=SCALE if w == 0 else 1.0, in1=q_parts[:, w, 0, cols],
                                             op0=ALU.mult, op1=ALU.subtract).then_inc(s_rest, 1)

                def third(n, cols):
                    dve.wait_ge(s_p2, b * 4 + n + 1)
                    dve.tensor_tensor(q_parts[:, 0, 2, cols], rest[:, 0, cols], q_parts[:, 0, 1, cols],
                                      ALU.subtract).then_inc(s_parts[0], 1)

                if follows(b):
                    statistics(b + 1)
                    dve.wait_ge(s_hT, b * 2 + 2)
                    copy_mod(b + 1)
                for n, cols in halves(0):
                    rest_of(n, 0, cols)
                if follows(b):
                    norm(b + 1)
                for n, cols in halves(0):
                    third(n, cols)
                for n, cols in halves(1):
                    rest_of(n, 1, cols)

            over_batches(dve, step)
            dve.wait_ge(s_rowsb, B)
            dve.tensor_scalar(mod_rows[:, :, 2, :], mod_rows[:, :, 2, :], 1.0, None, ALU.add).then_inc(s_mod, 1)

        @block.tensor
        def _(pe):
            pe.wait_ge(s_wm, 32)
            pe.wait_ge(s_c, 3)
            for n, j in enumerate((0, 1, 3, 4)):
                mm = pe.matmul(psum[:, 4, n * B:(n + 1) * B], wmod_sb[:, j * E:(j + 1) * E], c_silu, start=True, stop=True)
            mm.then_inc(s_cols, 1)

            def turn(b):
                pe.wait_ge(s_xn, b + 1)
                for c in range(2):
                    for t in range(4):
                        mm = pe.transpose(psum[:, c, t * P:(t + 1) * P], xn[:, c * 4 + t, :], ident[:, :])
                    mm.then_inc(s_xT, 1)

            pe.wait_ge(s_const, 1)
            turn(0)
            pe.wait_ge(s_w, 48)
            pe.wait_ge(s_mod, 1)

            def step(b):
                for w, wt in enumerate((wq_sb, wk_sb)):
                    for c in range(2):
                        if w == 0:
                            pe.wait_ge(s_hT, b * 2 + c + 1)
                        pe.wait_ge(s_rest, b * 4 + 2 * w + c + 1)
                        pe.matmul(psum[:, 2 + 2 * w + c, :], wt, hT[:, c * HALF:(c + 1) * HALF],
                                  start=True, stop=True).then_inc(s_proj, 1)
                pe.wait_ge(s_v, b * 2 + 2)
                for c in range(2):
                    for t in range(4):
                        mm = pe.matmul(psum[:, 6 + c, t * P:(t + 1) * P], hT[:, (c * 4 + t) * P:(c * 4 + t + 1) * P],
                                       wv_sb, start=True, stop=True)
                    mm.then_inc(s_vproj, 1)
                if follows(b):
                    turn(b + 1)

            over_batches(pe, step)
            pe.wait_ge(s_c, 4)
            pe.wait_ge(s_hT, 2 * B)
            for b in range(B):
                if b > 1:
                    pe.wait_ge(s_rowsb, b - 1)
                pe.matmul(psum[:, b % 2, :], c_bc[:, b, :], wmod_sb[:, 2 * E:6 * E], start=True, stop=True).then_inc(s_rows, 1)

    return [(s, B * 16 * NPART + 16) for s in s_stored] + [(s_vstored, B * 16 + 16)]


MAX_BANKS = [
    ([(0, 0, 128, 0), (4, 512, 128, 128)], (0, 8, 2)),
    ([(1, 0, 256, 0), (5, 512, 256, 256)], (1, 8, 2)),
    ([(2, 0, 384, 0)], (2, 1, 1)),
    ([(3, 0, 512, 0)], (3, 1, 1)),
    ([(4, 0, 512, 0)], (4, 1, 1)),
    ([(5, 0, 512, 0)], (5, 1, 1)),
    ([(6, 0, 512, 0)], (6, 1, 1)),
    ([(7, 0, 512, 0)], (7, 1, 1)),
    ([(6, 512, 384, 0)], (10, 1, 1)),
    ([(7, 512, 512, 0)], (11, 1, 1)),
]
G, L = 0, 1
STEPS = 2 * TPB
SCORES = 4 * 4 + 4 * 2 + TPB
MAXIMA_G = [("max_g", h, n) for h in range(4) for n in range(len(MAX_BANKS))]
MAXIMA_L = [("max_l", h) for h in range(4)]
FIRST = MAXIMA_G[:16] + MAXIMA_L[:1] + MAXIMA_G[16:] + MAXIMA_L[1:3] + [("turn_m", G)] + MAXIMA_L[3:]
RING_A = len(FIRST)
RING = RING_A + 1 + 4

FOLLOW = (1, 2, 1, 2, 1, 1, 0, 0, 2, 2, 0, 2, 0, 1, 1, 1, 1, 0, 2, 1, 1, 1, 1, 0,
          2, 1, 0, 2, 0, 1, 1, 0, 1, 0, 1, 1, 0, 1, 2, 0, 1, 1, 0, 2)


def slot_steps(with_next):
    steps = []
    for kb in range(TPB):
        for part in range(4 if kb < 4 else 2):
            steps.append(("score_g", kb, part))
            if part == 1 and kb:
                steps += [("weigh_g", kb - 1, half) for half in range(0 if kb <= 4 else 1, 2)]
    for kt in range(TPB):
        steps.append(("score_l", kt))
        if kt == 0:
            steps += [("weigh_g", TPB - 1, 1), ("out", G)]
        else:
            steps.append(("weigh_l", kt - 1))
        if kt == 4:
            steps += [("turn_o", G, 0), ("turn_o", G, 1)]
    last = [("weigh_l", TPB - 1), ("out", L), ("turn_o", L, 0), ("turn_o", L, 1)]
    if not with_next:
        return steps[:6] + [("turn_m", L)] + steps[6:] + last

    ahead = MAXIMA_G[:8] + [("turn_m", L)] + MAXIMA_G[8:]
    mixed = []
    for step, count in zip(steps, FOLLOW + (0,) * len(steps)):
        mixed += [step] + ahead[:count]
        ahead = ahead[count:]
        if step == ("weigh_l", 5):
            mixed.append(("turn_m", G))
    assert not ahead
    return mixed + MAXIMA_L[:2] + last[:2] + MAXIMA_L[2:] + last[2:]


def attention(nc, sem, psum, work, attn_sb, ident, identb, mask_qk, mask_kq, mask_lq, mask_lk, q_parts_d,
              k_parts_d, v_d, s_setup_stored, x_sb, bo_sb, mod_rows, dense_w, woT, wrT, wgT, wuT, wdT, sorted_d):
    at = [0]

    def part(n, dt=F32):
        a = work[:, at[0]:at[0] + n]
        at[0] += n
        return a

    q_rep, k_rep, v_u = [], [], []
    for u in range(NU):
        q_rep.append(q_of(work, u).rearrange("p (h s) -> p h s", h=UH))
        k_rep.append(k_of(work, u).rearrange("p (h s) -> p h s", h=UH))
        part(UH * S)
        v_u.append(part(TPB * UH * VW).rearrange("p (t h w) -> p t h w", t=TPB, h=UH))
    probs = [part(4 * S).rearrange("p (h s) -> p h s", h=4) for _ in range(2)]
    o_sb = part(S)
    maxima = [part(4 * 12).rearrange("p (h n) -> p h n", h=4) for _ in (G, L)]
    left = [part(4 * TPB).rearrange("p (h t) -> p h t", h=4) for _ in (G, L)]
    m_parts = [part(NPART * 4 * TPB // 2).bitcast(BF16).rearrange("p (i h t) -> p i h t", i=NPART, h=4) for _ in (G, L)]
    zero = part(4 * TPB).rearrange("p (h t) -> p h t", h=4)
    m_rows = [part(P // 2).bitcast(BF16) for _ in (G, L)]
    inv = [part(16).rearrange("p (t h) -> p t h", t=4) for _ in range(2)]

    sign = part(B * E).rearrange("p (b m) -> p b m", b=B)
    size = part(B * E).rearrange("p (b m) -> p b m", b=B)

    s_init = sem("attention_memory_set")
    s_gates = sem("gate_steps")
    s_load = [[sem(f"unit{u}_global_heads_in"), sem(f"unit{u}_local_heads_in")] for u in range(NU)]
    s_score, s_exp = sem("scores_ready"), sem("score_buffers_free")
    s_ring, s_ring_free = sem("ring_filled"), sem("ring_banks_free")
    s_weigh = sem("weighed")
    s_out_free = sem("outputs_copied")
    s_max = [sem("global_maxima_ready"), sem("local_maxima_ready")]
    s_zero = sem("zeros_made")
    s_split = sem("maxima_split_steps")
    s_mparts = [sem("global_maxima_split"), sem("local_maxima_split")]
    s_mrows = [sem("global_max_rows_ready"), sem("local_max_rows_ready")]
    s_m = [sem("global_max_rows_in"), sem("local_max_rows_in")]
    s_inv = sem("sums_inverted")
    s_dense_w, s_dense_steps, s_blank = sem("dense_weights_in"), sem("dense_weights_gated"), sem("blank_rows_out")
    LOADS = 16 * 9
    ROWS = 16 * NPART

    def first_bank(n):
        back = RING_A - 1 - n
        return (4, 5, 0, 1, 2, 3)[back % 6]

    def ring_bank(n):
        return 4 + (RING_A + n) % 2

    def over_slots(eng, slot):
        with eng.Fori(0, B - 1) as b:
            for u in range(NU):
                slot(b, u, b * NU + u, True)
        for u in range(NU):
            slot(B - 1, u, (B - 1) * NU + u, u < NU - 1)

    with nc.Block() as block:
        @block.sync
        def _(sp):
            def load(b, u, quad):
                h0, to = 4 * (u + NU * quad), slice(4 * quad, 4 * quad + 4)
                cols = bass.ds(b * S, S)

                def parts(of, i0, i1):
                    return of[h0:h0 + 4, i0:i1, :, cols].rearrange("h i d s -> (i d) h s")

                for r in range(NPART):
                    row = r * NPART * D
                    sp.dma_start(q_rep[u][row:row + NPART * D, to, :],
                                 parts(q_parts_d, 0, NPART)).then_inc(s_load[u][quad], 16)
                    cut = row + (NPART - r) * D
                    sp.dma_start(k_rep[u][row:cut, to, :], parts(k_parts_d, r, NPART)).then_inc(s_load[u][quad], 16)
                    if r:
                        sp.dma_start(k_rep[u][cut:row + NPART * D, to, :],
                                     parts(k_parts_d, 0, r)).then_inc(s_load[u][quad], 16)
                vals = v_d[bass.ds(b, 1)].rearrange("o p (t h w) -> (o p) t h w", t=TPB, h=H)
                sp.dma_start(v_u[u][:, :, to, :], vals[:, :, h0:h0 + 4, :]).then_inc(s_load[u][quad], 16)

            def rows(u, quad, unit):
                sp.wait_ge(s_mrows[quad], unit + 1)
                for i in range(NPART):
                    sp.dma_start(q_rep[u][KS + i:KS + i + 1, 4 * quad:4 * quad + 4, :],
                                 m_rows[quad][i * 4 * TPB:(i + 1) * 4 * TPB, :]).then_inc(s_m[quad], 16)

            sp.sem_inc(s_m[L], 16)
            load(0, 0, G)
            load(0, 0, L)
            for s, value in s_setup_stored:
                sp.wait_ge(s, value)
            for name, w in (("wo", woT), ("wr", wrT), ("wg", wgT), ("wu", wuT)):
                sp.dma_start(dense_w[name][:, :], w).then_inc(s_dense_w, 16)
            sp.dma_start(dense_w["wd"][:, :, :], wdT.rearrange("(c p) e -> p c e", p=P)).then_inc(s_dense_w, 16)
            load(0, 1, G)
            rows(0, G, 0)
            load(0, 1, L)
            sp.wait_ge(s_zero, 3)
            sp.dma_start(sorted_d[NE * REGION:, :].rearrange("(r p) e -> p r e", p=P),
                         dense_w["blank"][:, NE:2 * NE, :]).then_inc(s_blank, 16)

            def slot(b, u, s, more):
                rows(u, L, s)
                if not isinstance(b, int):
                    sp.wait_ge(s_weigh, s * STEPS + TPB + 2)
                    load(b + 1, u, G)
                if more:
                    rows(1 - u, G, s + 1)
                if not isinstance(b, int):
                    sp.wait_ge(s_weigh, s * STEPS + STEPS + 2)
                    load(b + 1, u, L)

            over_slots(sp, slot)
            sp.wait_ge(s_blank, 16)
            for quad in (G, L):
                sp.wait_ge(s_m[quad], B * NU * ROWS + 16 * quad)

        @block.gpsimd
        def _(pool):
            def split(quad, unit):
                pool.wait_ge(s_max[quad], unit + 1)
                m = maxima[quad][:, :, 0:TPB]
                n = unit * 8 + quad * 4
                pool.tensor_tensor(m_parts[quad][:, 0], zero, m, ALU.subtract).then_inc(s_split, 1)
                pool.wait_ge(s_split, n + 1)
                pool.tensor_tensor(left[quad], m, m_parts[quad][:, 0], ALU.add).then_inc(s_split, 1)
                pool.wait_ge(s_split, n + 2)
                pool.tensor_tensor(m_parts[quad][:, 1], zero, left[quad], ALU.subtract).then_inc(s_split, 1)
                pool.wait_ge(s_split, n + 3)
                pool.tensor_tensor(left[quad], left[quad], m_parts[quad][:, 1], ALU.add).then_inc(s_split, 1)
                pool.wait_ge(s_split, n + 4)
                pool.tensor_tensor(m_parts[quad][:, 2], zero, left[quad], ALU.subtract).then_inc(s_mparts[quad], 1)

            pool.memset(zero, 0.0).then_inc(s_zero, 1)
            pool.memset(dense_w["blank"][:, :, 0:E], 0.0).then_inc(s_zero, 1)
            pool.iota(dense_w["blank"][:, :, E:E + 1].bitcast(I32), pattern=[[P, 2 * NE], [0, 1]], base=NT * P,
                      channel_multiplier=1).then_inc(s_zero, 1)
            pool.wait_ge(s_zero, 3)
            for j in (0, 3):
                g = mod_rows[:, :, j, :]
                for i, (out, a, b, op) in enumerate(((sign, g, 0.0, ALU.is_ge), (sign, sign, 2.0, ALU.mult),
                                                     (sign, sign, 1.0, ALU.subtract), (size, g, sign, ALU.mult),
                                                     (size, size, 0.25, ALU.max), (g, size, sign, ALU.mult))):
                    if isinstance(b, float):
                        pool.tensor_scalar(out, a, b, None, op).then_inc(s_gates, 1)
                    else:
                        pool.tensor_tensor(out, a, b, op).then_inc(s_gates, 1)
                    pool.wait_ge(s_gates, (0 if j == 0 else 6) + i + 1)
            for b in range(B):
                pool.tensor_tensor(size[:, b, :], mod_rows[:, b, 0, :], bo_sb[:, :], ALU.mult).then_inc(s_gates, 1)
            pool.wait_ge(s_gates, 12 + B)
            split(G, 0)
            split(L, 0)

            def slot(b, u, s, more):
                for step in slot_steps(more):
                    if step == MAXIMA_G[-1]:
                        split(G, s + 1)
                    elif step == MAXIMA_L[-1]:
                        split(L, s + 1)

            over_slots(pool, slot)
            for b in range(B):
                xb = x_sb[:, b * TPB:(b + 1) * TPB, :]
                pool.tensor_tensor(xb, xb, size[:, b, :].unsqueeze(1).broadcast_to([P, TPB, E]),
                                   ALU.add).then_inc(s_gates, 1)
            pool.wait_ge(s_dense_w, 80)
            for b in range(B):
                pool.tensor_tensor(dense_w["wo_gated"][:, b], dense_w["wo"][:, :], mod_rows[:, b, 0, :],
                                   ALU.mult).then_inc(s_dense_steps, 1)
                pool.tensor_tensor(dense_w["wd_gated"][:, b], dense_w["wd"][:, :, :],
                                   mod_rows[:, b, 3:4, :].broadcast_to([P, 2, E]), ALU.mult).then_inc(s_dense_steps, 1)

        @block.scalar
        def _(act):
            act.sem_inc(s_exp, 2)
            act.sem_inc(s_out_free, 1)

            def slot(b, u, s, more):
                n = r = turned = 0
                for step in slot_steps(more):
                    if step[0] in ("max_g", "max_l", "turn_m", "turn_o"):
                        r += 1
                        turned = r if step[0] == "turn_o" else turned
                    elif step[0] in ("score_g", "score_l"):
                        kt = step[1] + (TPB if step[0] == "score_l" else 0)
                        to = probs[kt % 2]
                        bank = 2 * (n % 2)
                        act.wait_ge(s_score, s * SCORES + n + 1)
                        first = step[0] == "score_l" or step[2] == 0
                        if first:
                            act.wait_ge(s_weigh, s * STEPS + kt + 1)
                        if step[0] == "score_l":
                            dst = to[:, :, 0:BAND].rearrange("p (a c) q -> p a c q", a=2)
                            src = psum[:, bank:bank + 2, 0:2 * BAND].rearrange("p a (c q) -> p a c q", c=2)
                        elif step[1] < 4:
                            cols = S - step[1] * P
                            dst = to[:, step[2], 0:cols]
                            src = psum[:, bank:bank + 2, :].rearrange("p a q -> p (a q)")[:, 0:cols]
                        else:
                            cols = S - step[1] * P
                            dst = to[:, 2 * step[2]:2 * step[2] + 2, 0:cols]
                            src = psum[:, bank:bank + 2, 0:cols]
                        act.activation(dst, src, ACT.Exp).then_inc(s_exp, 1)
                        n += 1
                    elif step[0] == "out":
                        act.wait_ge(s_weigh, s * STEPS + (step[1] + 1) * TPB + 2)
                        act.wait_ge(s_ring, RING_A + s * RING + turned)
                        act.activation(o_sb, psum[:, 6:8, :].rearrange("p a q -> p (a q)"),
                                       ACT.Copy).then_inc(s_out_free, 1)

            over_slots(act, slot)

        @block.vector
        def _(dve):
            dve.memset(psum[:, 6:8, :], 0.0).then_inc(s_init, 1)
            dve.sem_inc(s_ring_free, 2)

            def run(step, s, n, place):
                kind = step[0]
                bank = psum[:, place]
                dve.wait_ge(s_ring, n + 1)
                if kind == "max_g":
                    _, h, i = step
                    pieces, (first, by, count) = MAX_BANKS[i]
                    cols = pieces[0][2]
                    dve.tensor_reduce(maxima[G][:, h, first:first + by * (count - 1) + 1:by],
                                      bank[:, 0:count * cols].rearrange("p (c k) -> p c k", c=count), AX.X,
                                      ALU.max).then_inc(s_ring_free, 1)
                elif kind == "max_l":
                    _, h = step
                    dve.tensor_reduce(maxima[L][:, h, 0:TPB], bank.rearrange("p (t k) -> p t k", t=TPB), AX.X,
                                      ALU.max).then_inc(s_ring_free, 1)
                elif kind == "turn_m":
                    quad = step[1]
                    if s is not None:
                        dve.wait_ge(s_m[quad], (s + 1) * ROWS if quad == G else s * ROWS + 16)
                    dve.tensor_copy(m_rows[quad][0:96, :], bank.bitcast(BF16)[0:96, 0:P]).then_inc(s_mrows[quad], 1)
                    dve.wait_ge(s_mrows[quad], 1 if s is None else s + 2 - quad)
                    dve.sem_inc(s_ring_free, 1)

            def after(step, n):
                if step == ("max_g", 3, len(MAX_BANKS) - 1):
                    dve.wait_ge(s_ring_free, n + 3)
                    m = maxima[G]
                    dve.tensor_tensor(m[:, :, 4:8], m[:, :, 4:8], m[:, :, 8:12], ALU.max).then_inc(s_max[G], 1)
                elif step == ("max_l", 3):
                    dve.wait_ge(s_ring_free, n + 3)
                    dve.sem_inc(s_max[L], 1)

            assert RING_A % 2
            for n, step in enumerate(FIRST):
                run(step, None, n, first_bank(n))
                after(step, n)

            def slot(b, u, s, more):
                n = 0
                for step in slot_steps(more):
                    if step[0] in ("max_g", "max_l", "turn_m"):
                        run(step, s, RING_A + s * RING + n, ring_bank(n))
                        after(step, RING_A + s * RING + n)
                        n += 1
                    elif step[0] == "turn_o":
                        _, quad, c = step
                        h0 = 4 * (u + NU * quad)
                        bank = psum[:, ring_bank(n)].rearrange("p (t h w) -> p t h w", t=4, h=4)
                        k = s * 4 + quad * 2 + c
                        dve.wait_ge(s_ring, RING_A + s * RING + n + 1)
                        dve.reciprocal(inv[c], bank[:, :, :, D]).then_inc(s_inv, 1)
                        dve.wait_ge(s_inv, k + 1)
                        dve.tensor_tensor(
                            attn_sb[:, bass.ds(b * TPB + 4 * c, 4), h0 * D:(h0 + 4) * D].rearrange("p t (h d) -> p t h d", h=4),
                            bank[:, :, :, 0:D], inv[c].unsqueeze(3).broadcast_to([P, 4, 4, D]),
                            ALU.mult).then_inc(s_ring_free, 1)
                        n += 1

            over_slots(dve, slot)

        @block.tensor
        def _(pe):
            def free_bank(n, place):
                if not isinstance(n, int) or n >= RING_A:
                    pe.wait_ge(s_ring_free, n + 1)
                elif n >= 6:
                    pe.wait_ge(s_ring_free, n - 3)
                return psum[:, place]

            def run(step, u, batch, unit, n, place):
                kind = step[0]
                if step == ("max_g", 0, 0):
                    pe.wait_ge(s_load[u][G], (batch + 1) * LOADS)
                if step == ("max_l", 0):
                    pe.wait_ge(s_load[u][L], (batch + 1) * LOADS)
                if kind == "turn_m":
                    quad = step[1]
                    pe.wait_ge(s_mparts[quad], unit + 1)
                    bank = free_bank(n, place)
                    pe.transpose(bank.bitcast(BF16)[0:96, 0:P], m_parts[quad].rearrange("p i h t -> p (i h t)"),
                                 identb[:, :]).then_inc(s_ring, 1)
                    return
                bank = free_bank(n, place)
                if kind == "max_g":
                    _, h, i = step
                    for qt, k0, cols, to in MAX_BANKS[i][0]:
                        last = k0 + cols == (qt + 1) * P
                        mm = pe.matmul(bank[:, to:to + cols], q_rep[u][0:KS, h, qt * P:(qt + 1) * P],
                                       k_rep[u][0:KS, h, k0:k0 + cols], start=True, stop=not last)
                        if last:
                            mm = pe.matmul(bank[:, to + cols - P:to + cols], identb[:, :], mask_qk[:, :],
                                           start=False, stop=True)
                else:
                    _, h = step
                    pe.matmul(bank, identb[:, :], mask_lq[:, :, :].rearrange("p t k -> p (t k)"), start=True, stop=False,
                              skip_group_check=True)
                    for t in range(TPB):
                        for j in range(P // WINDOW):
                            q0 = t * P + j * WINDOW
                            k0 = max(q0 - WINDOW, 0)
                            c0 = t * 2 * WINDOW + k0 - (q0 - WINDOW)
                            cols = q0 + WINDOW - k0
                            mm = pe.matmul(bank[j * WINDOW:(j + 1) * WINDOW, c0:c0 + cols],
                                           q_rep[u][0:KS, 4 + h, q0:q0 + WINDOW], k_rep[u][0:KS, 4 + h, k0:k0 + cols],
                                           start=False, stop=True, skip_group_check=True)
                mm.then_inc(s_ring, 1)

            pe.sem_inc(s_weigh, 2)
            pe.wait_ge(s_init, 1)
            for n, step in enumerate(FIRST):
                run(step, 0, 0, 0, n, first_bank(n))

            def slot(b, u, s, more):
                n = r = 0
                for step in slot_steps(more):
                    kind = step[0]
                    if kind == "score_g":
                        _, kb, i = step
                        if kb == 0 and i == 0:
                            pe.wait_ge(s_m[G], (s + 1) * ROWS)
                        pe.wait_ge(s_exp, s * SCORES + n + 1)
                        cols = S - kb * P
                        for h in ([i] if kb < 4 else [2 * i, 2 * i + 1]):
                            for c0 in range(0, cols, HALF):
                                bank = 2 * (n % 2) + (c0 // HALF if kb < 4 else h % 2)
                                w = min(HALF, cols - c0)
                                mm = pe.matmul(psum[:, bank, 0:w], k_rep[u][0:KM, h, kb * P:(kb + 1) * P],
                                               q_rep[u][0:KM, h, kb * P + c0:kb * P + c0 + w],
                                               start=True, stop=c0 > 0)
                                if c0 == 0:
                                    mm = pe.matmul(psum[:, bank, 0:P], identb[:, :], mask_kq[:, :], start=False, stop=True)
                        mm.then_inc(s_score, 1)
                        n += 1
                    elif kind == "score_l":
                        kt = step[1]
                        if kt == 0:
                            pe.wait_ge(s_m[L], (s + 1) * ROWS + 16)
                        pe.wait_ge(s_exp, s * SCORES + n + 1)
                        w = min(BAND, S - kt * P)
                        for a in range(2):
                            bank = 2 * (n % 2) + a
                            pe.matmul(psum[:, bank, 0:2 * BAND], identb[:, :],
                                      mask_lk[:, :, :].rearrange("p c q -> p (c q)"), start=True, stop=False,
                                      skip_group_check=True)
                            for c in range(2):
                                h = 4 + 2 * a + c
                                mm = pe.matmul(psum[:, bank, c * BAND:c * BAND + w], k_rep[u][0:KM, h, kt * P:(kt + 1) * P],
                                               q_rep[u][0:KM, h, kt * P:kt * P + w], start=False, stop=True,
                                               skip_group_check=True)
                        mm.then_inc(s_score, 1)
                        n += 1
                    elif kind == "weigh_g":
                        _, kb, half = step
                        done = (4 * (kb + 1) if kb < 4 else 16 + 2 * (kb - 3))
                        pe.wait_ge(s_exp, s * SCORES + done + 2)
                        if kb == 0 and half == 0:
                            pe.wait_ge(s_out_free, s * 2 + 1)
                        q0 = max(kb * P, half * HALF)
                        w = (half + 1) * HALF - q0
                        for h in range(4):
                            mm = pe.matmul(psum[32 * h:32 * h + VW, 6 + half, q0 - half * HALF:HALF], v_u[u][:, kb, h, :],
                                           probs[kb % 2][:, h, q0 - kb * P:q0 - kb * P + w], start=kb == 0,
                                           stop=kb == (3 if half == 0 else 7), skip_group_check=True)
                        if half == 1:
                            mm.then_inc(s_weigh, 1)
                    elif kind == "weigh_l":
                        kt = step[1]
                        pe.wait_ge(s_exp, s * SCORES + 24 + kt + 1 + 2)
                        if kt == 0:
                            pe.wait_ge(s_out_free, s * 2 + 2)
                        end = min(kt * P + BAND, S)
                        for half in range(2):
                            q0, q1 = max(kt * P, half * HALF), min(end, (half + 1) * HALF)
                            if q1 <= q0:
                                continue
                            first = kt == 0 or (half == 1 and kt == 3)
                            for h in range(4):
                                mm = pe.matmul(psum[32 * h:32 * h + VW, 6 + half, q0 - half * HALF:q1 - half * HALF],
                                               v_u[u][:, kt, 4 + h, :], probs[kt % 2][:, h, q0 - kt * P:q1 - kt * P],
                                               start=first, stop=True, skip_group_check=True)
                        mm.then_inc(s_weigh, 1)
                    elif kind == "turn_o":
                        _, quad, c = step
                        pe.wait_ge(s_out_free, s * 2 + quad + 2)
                        bank = free_bank(RING_A + s * RING + r, ring_bank(r))
                        for t in range(4):
                            mm = pe.transpose(bank[:, t * P:(t + 1) * P],
                                              o_sb[:, (4 * c + t) * P:(4 * c + t + 1) * P], ident[:, :])
                        mm.then_inc(s_ring, 1)
                        r += 1
                    elif kind in ("max_g", "max_l", "turn_m"):
                        ahead = step != ("turn_m", L)
                        run(step, 1 - u if ahead else u, b + u if ahead else b, s + 1 if ahead else s,
                            RING_A + s * RING + r, ring_bank(r))
                        r += 1

            over_slots(pe, slot)


def feed_forward(nc, sem, psum, work, x_sb, attn_sb, ident, mod_cols, mod_rows, dense_w, gate_up, down,
                 sorted_d, expert_d, out):
    at = [0]

    def part(n, dt=F32):
        a = work[:, at[0]:at[0] + n]
        at[0] += n
        return a

    w_all = part(NE * WE)
    table_rows = part(2 * P)[0:1, :].bitcast(I32)
    expert, tile_row = table_rows[:, 0:ET], table_rows[:, P:P + ET]
    behind = at[0]
    dense(nc, sem, psum, x_sb, attn_sb, ident, mod_cols, mod_rows, dense_w, gate_up, down, sorted_d, w_all,
          table_rows, part)
    at[0] = behind
    experts(nc, sem, psum, ident, sorted_d, expert_d, w_all, expert, tile_row, part)
    combine(nc, sem, x_sb, attn_sb, mod_rows, expert_d, out)


def dense(nc, sem, psum, x_sb, attn_sb, ident, mod_cols, mod_rows, dense_w, gate_up, down, sorted_d, w_all,
          table_rows, part):
    wr, wg, wu = dense_w["wr"][:, :], dense_w["wg"][:, :], dense_w["wu"][:, :]
    wo_gated, wd_gated = dense_w["wo_gated"], dense_w["wd_gated"]
    stage, attnT, xn, h2T = part(HALF), part(HALF), part(HALF), part(HALF)
    silu = part(2 * HALF).rearrange("p (c s) -> p c s", c=2)
    act_s = part(2 * HALF).rearrange("p (c s) -> p c s", c=2)
    stats = part(4 * 6).rearrange("p (t s) -> p t s", t=4)
    mv = part(4 * 2).rearrange("p (t s) -> p t s", t=4)
    half_neg, ve, rstd, mod_b = part(4), part(4), part(4), part(2)
    h2m, cb_row = part(HALF), part(E)
    top, gate_of, best, pos_f = part(4), part(4), part(4), part(4)
    pos = [part(4).bitcast(I32) for _ in range(2)]
    pick = part(4 * NE).rearrange("p (t e) -> p t e", t=4)
    placed = part(4 * NE).rearrange("p (t e) -> p t e", t=4)
    pick_b = part(4 * NE // 2).bitcast(BF16).rearrange("p (t e) -> p t e", t=4)
    lower, added = part(NE), part(NE)
    before, ones = part(P // 2).bitcast(BF16), part(P // 2).bitcast(BF16)
    token = part(NT)
    rows = [part(4 * RW).rearrange("p (t e) -> p t e", t=4) for _ in range(2)]

    free_row, free_i, first_row, steps_of = part(NE), part(NE).bitcast(I32), part(NE), part(NT)
    tri16 = part(NE * NE).rearrange("p (e f) -> p e f", e=NE)
    count, tiles, ends = part(NE), part(NE), part(NE)
    cmp = part(NE * NT)
    slot, passed = part(1), part(NE)
    expert_f, start_f, row_f = part(1), part(1), part(1)

    s_ew = sem("expert_weights_in")
    s_tc, s_t, s_freed, s_tail = sem("table_constants"), sem("table_steps"), sem("free_rows_ready"), sem("tails_blank")
    s_columns, s_turned = sem("table_columns_ready"), sem("table_columns_turned")
    s_c = sem("dense_constants_made")
    s_stage, s_aT, s_attnT, s_y = sem("attn_staged"), sem("attn_turned"), sem("attnT_ready"), sem("attn_projected")
    s_x2 = sem("x2_ready")
    s_stat, s_aggr, s_ve, s_rstd, s_xn = (sem("stats2_done"), sem("aggr2_done"), sem("ve2_done"), sem("rstd2_done"),
                                          sem("xn2_done"))
    s_modb, s_row = sem("mod2_copied"), sem("scale_row_copied")
    s_xT, s_h2T, s_h2m, s_h2 = sem("xn2_turned"), sem("h2T_ready"), sem("h2_scaled"), sem("h2_ready")
    s_log = sem("logits_summed")
    s_gate, s_up, s_silu, s_act = sem("gate_ready"), sem("up_ready"), sem("silu_ready"), sem("act_ready")
    s_dn, s_x3 = sem("shared_ready"), sem("x3_ready")
    s_r, s_top, s_sig, s_pick, s_rank = (sem("route_steps"), sem("top_logit_ready"), sem("gates_ready"),
                                         sem("pick_ready"), sem("ranks_summed"))
    s_rows, s_pos, s_free = sem("rows_scaled"), sem("places_ready"), sem("row_buffers_free")
    s_begun = sem("sorting_begun")
    s_scat = [sem("even_rows_sorted"), sem("odd_rows_sorted")]
    HALVES = 2 * B
    tile = [slice(t * P, (t + 1) * P) for t in range(4)]
    shape = [P, 4, NE]

    def half(b, c, more=0):
        return b * 2 + c + more, b + (c + more) // 2, (c + more) % 2

    def tiles_of(t, b, c):
        return t[:, bass.ds(b * TPB + 4 * c, 4), :]

    def exists(b, c, more):
        return not isinstance(b, int) or b * 2 + c + more < HALVES

    def over_halves(eng, step):
        with eng.Fori(0, B - 1) as b:
            for c in range(2):
                step(b, c)
        for c in range(2):
            step(B - 1, c)

    def blank_tails(eng, first):
        eng.wait_ge(s_freed, 1)
        for e in range(first, NE, 2):
            row = eng.value_load(free_i[0:1, e:e + 1], min_val=0, max_val=NE * REGION - P)
            eng.dma_start(sorted_d[bass.ds(row, P), :], dense_w["blank"][:, e, :]).then_inc(s_tail, 16)

    with nc.Block() as block:
        @block.sync
        def _(sp):
            w_e = w_all.rearrange("p (e w) -> p e w", e=NE)
            sp.dma_start(w_e[:, :, 0:2 * F], gate_up.rearrange("e h f -> h e f")).then_inc(s_ew, 16)
            for f in range(2):
                sp.dma_start(w_e[:, :, 2 * F + f * E:2 * F + (f + 1) * E],
                             down[:, f * P:(f + 1) * P, :].rearrange("e p h -> p e h")).then_inc(s_ew, 16)
            blank_tails(sp, 0)
            sp.wait_ge(s_ew, 48)
            sp.wait_ge(s_tail, 16 * NE)

        @block.gpsimd
        def _(pool):
            small = dict(allow_small_or_imprecise_dtypes=True)
            pool.memset(half_neg, -0.5).then_inc(s_c, 1)
            pool.iota(lower, pattern=[[-1, NE]], base=NE, channel_multiplier=0, **small).then_inc(s_c, 1)
            pool.iota(free_row, pattern=[[REGION, NE]], base=0, channel_multiplier=0, **small).then_inc(s_c, 1)
            pool.iota(token.bitcast(I32), pattern=[[P, NT]], base=0, channel_multiplier=1).then_inc(s_c, 1)
            pool.memset(before, 1.0).then_inc(s_c, 1)
            pool.memset(ones, 1.0).then_inc(s_c, 1)
            pool.wait_ge(s_c, 6)
            pool.affine_select(out=before, in_=before, compare_op=ALU.is_gt, fill=0.0, base=0,
                               pattern=[[1, P]], channel_multiplier=-1).then_inc(s_c, 1)

            def norm(b, c, more):
                n, _, _ = half(b, c, more)
                pool.wait_ge(s_ve, n + 1)
                pool.tensor_tensor(rstd, ve, half_neg, ALU.pow).then_inc(s_rstd, 1)

            def scale(b, c, more):
                n, _, _ = half(b, c, more)
                pool.wait_ge(s_xn, n + 1)
                pool.tensor_tensor(h2m.rearrange("p (t e) -> p t e", t=4), xn.rearrange("p (t e) -> p t e", t=4),
                                   cb_row.unsqueeze(1).broadcast_to([P, 4, E]), ALU.mult).then_inc(s_h2m, 1)

            for c in range(2):
                norm(0, c, 0)
                if c == 1:
                    pool.wait_ge(s_h2, 1)
                scale(0, c, 0)
            pool.iota(first_row, pattern=[[REGION, NE]], base=0, channel_multiplier=0, **small).then_inc(s_tc, 1)
            pool.iota(steps_of, pattern=[[P, NT]], base=0, channel_multiplier=0, **small).then_inc(s_tc, 1)
            pool.iota(slot, pattern=[[0, 1]], base=0, channel_multiplier=1, **small).then_inc(s_tc, 1)
            pool.memset(tri16, 1.0).then_inc(s_tc, 1)
            pool.wait_ge(s_tc, 4)
            pool.affine_select(out=tri16, in_=tri16, compare_op=ALU.is_ge, fill=0.0, base=0,
                               pattern=[[1, NE], [-1, NE]], channel_multiplier=0).then_inc(s_tc, 1)

            def step(b, c):
                n, _, _ = half(b, c)
                if exists(b, c, 2):
                    norm(b, c, 2)
                if exists(b, c, 2):
                    pool.wait_ge(s_h2, n + 2)
                    scale(b, c, 2)
                pool.wait_ge(s_pos, n + 1)
                pool.sem_inc(s_begun, 1)
                for t in range(4):
                    pool.indirect_dma_start(sorted_d[:, :], bass.IndirectOffsetOnAxis(ap=pos[c][:, t:t + 1], axis=0),
                                            rows[c][:, t, :], None).then_inc(s_scat[c], 16)
                pool.wait_ge(s_scat[c], b * 64 + 64)
                pool.sem_inc(s_free, 1)

            over_halves(pool, step)

        @block.scalar
        def _(act):
            def copy_attn(b, c, more):
                n, b2, c2 = half(b, c, more)
                if not isinstance(n, int) or n > 0:
                    act.wait_ge(s_aT, n)
                act.activation(stage.rearrange("p (t e) -> p t e", t=4), tiles_of(attn_sb, b2, c2),
                               ACT.Copy).then_inc(s_stage, 1)

            def copy_attnT(b, c, more):
                n, _, _ = half(b, c, more)
                act.wait_ge(s_aT, n + 1)
                if not isinstance(n, int) or n > 0:
                    act.wait_ge(s_y, n)
                act.activation(attnT, psum[:, 0, :], ACT.Copy).then_inc(s_attnT, 1)

            def gates(b, c):
                n, _, _ = half(b, c)
                act.wait_ge(s_top, n + 1)
                act.wait_ge(s_rows, n + 1)
                act.activation(gate_of, top, ACT.Sigmoid).then_inc(s_sig, 1)

            def modulate(b, c, more):
                n, b2, _ = half(b, c, more)
                act.wait_ge(s_xT, n + 1)
                act.wait_ge(s_modb, b2 + 1)
                if not isinstance(n, int) or n > 0:
                    act.wait_ge(s_up, n)
                act.activation(h2T, psum[:, 2, :], ACT.Identity, scale=mod_b[:, 1:2], bias=mod_b[:, 0:1])\
                    .then_inc(s_h2T, 1)

            for c in range(2):
                copy_attn(0, c, 0)
                copy_attnT(0, c, 0)
            modulate(0, 0, 0)
            act.sem_inc(s_silu, 1)

            def step(b, c):
                n, _, _ = half(b, c)
                if exists(b, c, 2):
                    copy_attn(b, c, 2)
                if not exists(b, c, 1):
                    gates(b, c)
                act.wait_ge(s_gate, n + 1)
                act.wait_ge(s_act, n + 1)
                act.activation(silu, psum[:, 4:6, :], ACT.Silu).then_inc(s_silu, 1)
                if exists(b, c, 2):
                    copy_attnT(b, c, 2)
                if exists(b, c, 1):
                    gates(b, c)
                if exists(b, c, 1):
                    modulate(b, c, 1)

            over_halves(act, step)
            blank_tails(act, 1)

        @block.vector
        def _(dve):
            dve.sem_inc(s_act, 1)
            dve.sem_inc(s_rows, 1)
            dve.sem_inc(s_free, 2)
            dve.sem_inc(s_r, 1)
            dve.wait_ge(s_c, 4)

            def copy_mod(b):
                dve.tensor_copy(mod_b, mod_cols[:, 2:4, bass.ds(b, 1)].rearrange("p j o -> p (j o)")).then_inc(s_modb, 1)

            def copy_row(b):
                dve.tensor_copy(cb_row, mod_rows[:, bass.ds(b, 1), 2, :].rearrange("p o e -> p (o e)")).then_inc(s_row, 1)

            def residual(b, c, more):
                n, b2, c2 = half(b, c, more)
                x4 = tiles_of(x_sb, b2, c2)
                dve.wait_ge(s_y, n + 1)
                dve.tensor_tensor(x4, psum[:, 1, :].rearrange("p (t e) -> p t e", t=4), x4, ALU.add).then_inc(s_x2, 1)
                dve.wait_ge(s_x2, n + 1)
                dve.tensor_copy(ve, half_neg).then_inc(s_aggr, 1)
                for t in range(4):
                    dve.bn_stats(stats[:, t, :], x_sb[:, bass.ds(b2 * TPB + 4 * c2 + t, 1), :].rearrange("p o e -> p (o e)"))\
                        .then_inc(s_stat, 1)
                dve.wait_ge(s_stat, n * 4 + 4)
                dve.tensor_copy(ve, stats[:, :, 0]).then_inc(s_aggr, 1)
                for t in range(4):
                    dve.bn_aggr(mv[:, t, :], stats[:, t, :]).then_inc(s_aggr, 1)
                dve.wait_ge(s_aggr, n * 6 + 6)
                dve.tensor_scalar(ve, mv[:, :, 1], EPS, None, ALU.add).then_inc(s_ve, 1)

            def norm(b, c, more):
                n, b2, c2 = half(b, c, more)
                dve.wait_ge(s_rstd, n + 1)
                if not isinstance(n, int) or n > 0:
                    dve.wait_ge(s_xT, n)
                    dve.wait_ge(s_h2m, n)
                for t in range(4):
                    st = dve.tensor_scalar(xn[:, t * E:(t + 1) * E],
                                           x_sb[:, bass.ds(b2 * TPB + 4 * c2 + t, 1), :].rearrange("p o e -> p (o e)"),
                                           mv[:, t, 0:1], rstd[:, t:t + 1], ALU.subtract, ALU.mult)
                st.then_inc(s_xn, 1)

            def make_h2(b, c, more):
                n, b2, c2 = half(b, c, more)
                dve.wait_ge(s_h2m, n + 1)
                dve.tensor_tensor(tiles_of(attn_sb, b2, c2), h2m.rearrange("p (t e) -> p t e", t=4),
                                  mod_rows[:, bass.ds(b2, 1), 1, :].broadcast_to([P, 4, E]), ALU.add).then_inc(s_h2, 1)

            copy_mod(0)
            copy_row(0)
            residual(0, 0, 0)
            norm(0, 0, 0)
            residual(0, 1, 0)
            make_h2(0, 0, 0)
            norm(0, 1, 0)

            def step(b, c):
                n, _, _ = half(b, c)
                done = [n * 9 + 1]

                def then(ins):
                    done[0] = done[0] + 1
                    ins.then_inc(s_r, 1)
                    dve.wait_ge(s_r, done[0])

                def place_rows(b, c):
                    dve.wait_ge(s_sig, n + 1)
                    dve.wait_ge(s_free, n + 1)
                    dve.tensor_tensor(rows[c][:, :, 0:E], tiles_of(attn_sb, b, c),
                                      gate_of.unsqueeze(2).broadcast_to([P, 4, E]), ALU.mult).then_inc(s_rows, 1)
                    dve.tensor_copy(rows[c][:, :, E:E + 1].bitcast(I32),
                                    token[:, bass.ds(b * TPB + 4 * c, 4)].unsqueeze(2).bitcast(I32))
                    dve.wait_ge(s_rank, n + 1)
                    then(dve.tensor_tensor(placed, psum[:, 2, 4 * NE:8 * NE].rearrange("p (t e) -> p t e", t=4),
                                           free_row.unsqueeze(1).broadcast_to(shape), ALU.add))
                    then(dve.tensor_tensor(placed, placed, pick, ALU.mult))
                    then(dve.tensor_reduce(pos_f, placed, AX.X, ALU.add))
                    dve.tensor_copy(pos[c], pos_f).then_inc(s_pos, 1)
                    then(dve.tensor_reduce(added, psum[:, 2, 8 * NE:12 * NE].rearrange("p (t e) -> p e t", t=4), AX.X, ALU.add))
                    then(dve.tensor_tensor(free_row, free_row, added, ALU.add))

                logits = psum[:, 3, 0:4 * NE].rearrange("p (t e) -> p t e", t=4)
                low = lower.unsqueeze(1).broadcast_to(shape)
                dve.wait_ge(s_log, n + 1)
                dve.tensor_reduce(top, logits, AX.X, ALU.max).then_inc(s_top, 1)
                dve.wait_ge(s_top, n + 1)
                then(dve.tensor_tensor(pick, logits, top.unsqueeze(2).broadcast_to(shape), ALU.is_equal))
                then(dve.tensor_tensor(pick, pick, low, ALU.mult))
                then(dve.tensor_reduce(best, pick, AX.X, ALU.max))
                then(dve.tensor_tensor(pick, low, best.unsqueeze(2).broadcast_to(shape), ALU.is_equal))
                dve.tensor_copy(pick_b, pick).then_inc(s_pick, 1)
                if exists(b, c, 1):
                    make_h2(b, c, 1)
                else:
                    place_rows(b, c)
                    dve.tensor_copy(free_i, free_row).then_inc(s_freed, 1)
                dve.wait_ge(s_up, n + 1)
                dve.wait_ge(s_silu, n + 2)
                dve.tensor_tensor(act_s, psum[:, 6:8, :], silu, ALU.mult).then_inc(s_act, 1)
                if c == 1 and exists(b, c, 1):
                    dve.wait_ge(s_h2T, n + 1)
                    copy_mod(b + 1)
                if c == 0 and exists(b, c, 2):
                    dve.wait_ge(s_h2m, n + 2)
                    copy_row(b + 1)
                if exists(b, c, 2):
                    residual(b, c, 2)
                if exists(b, c, 1):
                    place_rows(b, c)
                x4 = tiles_of(x_sb, b, c)
                dve.wait_ge(s_dn, n + 1)
                dve.tensor_tensor(x4, psum[:, 0, :].rearrange("p (t e) -> p t e", t=4), x4, ALU.add).then_inc(s_x3, 1)
                if exists(b, c, 2):
                    norm(b, c, 2)

            over_halves(dve, step)
            tabled = [0]

            def table(ins):
                tabled[0] += 1
                ins.then_inc(s_t, 1)
                dve.wait_ge(s_t, tabled[0])

            dve.wait_ge(s_tc, 5)
            table(dve.tensor_tensor(count, free_row, first_row, ALU.subtract))
            cmp_n = cmp[:, 0:NE * NT].rearrange("p (e n) -> p e n", e=NE)
            table(dve.tensor_tensor(cmp_n, count.unsqueeze(2).broadcast_to([P, NE, NT]),
                                   steps_of.unsqueeze(1).broadcast_to([P, NE, NT]), ALU.is_gt))
            table(dve.tensor_reduce(tiles, cmp_n, AX.X, ALU.add))
            cmp_e = cmp[:, 0:NE * NE].rearrange("p (e f) -> p e f", e=NE)
            table(dve.tensor_tensor(cmp_e, tri16, tiles.unsqueeze(1).broadcast_to([P, NE, NE]), ALU.mult))
            table(dve.tensor_reduce(ends, cmp_e, AX.X, ALU.add))
            table(dve.tensor_scalar(passed, ends, slot, None, ALU.is_le))
            table(dve.tensor_reduce(expert_f, passed, AX.X, ALU.add))
            table(dve.tensor_tensor(passed, passed, ends, ALU.mult))
            table(dve.tensor_reduce(start_f, passed, AX.X, ALU.max))
            table(dve.tensor_scalar(start_f, start_f, slot, -float(P), ALU.subtract, ALU.mult))
            table(dve.scalar_tensor_tensor(out=row_f, in0=expert_f, scalar=float(REGION), in1=start_f, op0=ALU.mult,
                                           op1=ALU.add))
            dve.tensor_scalar(expert_f, expert_f, float(NE - 1), None, ALU.min).then_inc(s_columns, 1)
            dve.wait_ge(s_turned, 1)
            dve.tensor_copy(table_rows, psum[0:1, 3, 0:2 * P]).then_inc(s_t, 1)

        @block.tensor
        def _(pe):
            def turn_attn(b, c, more):
                n, _, _ = half(b, c, more)
                pe.wait_ge(s_stage, n + 1)
                if more == 2:
                    pe.wait_ge(s_x3, b * 2 + c + 1)
                elif c == 1:
                    pe.wait_ge(s_attnT, 1)
                for t in range(4):
                    mm = pe.transpose(psum[:, 0, tile[t]], stage[:, tile[t]], ident[:, :])
                mm.then_inc(s_aT, 1)

            def project(b, c, more):
                n, b2, _ = half(b, c, more)
                pe.wait_ge(s_attnT, n + 1)
                if not isinstance(n, int) or n > 0:
                    pe.wait_ge(s_x2, n)
                for t in range(4):
                    mm = pe.matmul(psum[:, 1, tile[t]], attnT[:, tile[t]],
                                   wo_gated[:, bass.ds(b2, 1), :].rearrange("p o e -> p (o e)"), start=True, stop=True)
                mm.then_inc(s_y, 1)

            def turn_norm(b, c, more):
                n, _, _ = half(b, c, more)
                pe.wait_ge(s_xn, n + 1)
                if not isinstance(n, int) or n > 0:
                    pe.wait_ge(s_h2T, n)
                    pe.wait_ge(s_r, n * 9 - 8)
                for t in range(4):
                    mm = pe.transpose(psum[:, 2, tile[t]], xn[:, tile[t]], ident[:, :])
                mm.then_inc(s_xT, 1)

            for c in range(2):
                turn_attn(0, c, 0)
                project(0, c, 0)
            turn_norm(0, 0, 0)
            pe.wait_ge(s_c, 7)
            pe.sem_inc(s_x3, 1)

            def rank(b, c):
                n, _, _ = half(b, c)
                pe.wait_ge(s_pick, n + 1)
                if exists(b, c, 1):
                    pe.wait_ge(s_h2T, n + 2)
                flat = pick_b.rearrange("p t e -> p (t e)")
                pe.matmul(psum[:, 2, 8 * NE:12 * NE], ones, flat, start=True, stop=True)
                pe.matmul(psum[:, 2, 4 * NE:8 * NE], before, flat, start=True, stop=False)
                for t in range(3):
                    mm = pe.matmul(psum[:, 2, (5 + t) * NE:8 * NE], ones, pick_b[:, t:t + 1, :].broadcast_to([P, 3 - t, NE]),
                                   start=False, stop=t == 2)
                mm.then_inc(s_rank, 1)

            def step(b, c):
                n, _, _ = half(b, c)
                pe.wait_ge(s_h2T, n + 1)
                for t in range(4):
                    mm = pe.matmul(psum[:, 3, t * NE:(t + 1) * NE], h2T[:, tile[t]], wr, start=True, stop=True)
                mm.then_inc(s_log, 1)
                pe.wait_ge(s_silu, n + 1)
                for f in range(2):
                    mm = pe.matmul(psum[:, 4 + f, :], wg[:, f * P:(f + 1) * P], h2T, start=True, stop=True)
                mm.then_inc(s_gate, 1)
                if exists(b, c, 2):
                    turn_attn(b, c, 2)
                if not exists(b, c, 1):
                    rank(b, c)
                pe.wait_ge(s_act, n + 1)
                for f in range(2):
                    mm = pe.matmul(psum[:, 6 + f, :], wu[:, f * P:(f + 1) * P], h2T, start=True, stop=True)
                mm.then_inc(s_up, 1)
                if exists(b, c, 1):
                    turn_norm(b, c, 1)
                if exists(b, c, 2):
                    project(b, c, 2)
                if exists(b, c, 1):
                    rank(b, c)
                pe.wait_ge(s_act, n + 2)
                if not exists(b, c, 2):
                    pe.wait_ge(s_x3, b * 2 + c + 1)
                for t in range(4):
                    for f in range(2):
                        mm = pe.matmul(psum[:, 0, tile[t]], act_s[:, f, tile[t]],
                                       wd_gated[:, bass.ds(b, 1), f, :].rearrange("p o e -> p (o e)"),
                                       start=f == 0, stop=f == 1)
                mm.then_inc(s_dn, 1)

            over_halves(pe, step)
            pe.wait_ge(s_columns, 1)
            for n, column in enumerate((expert_f, row_f)):
                mm = pe.matmul(psum[0:1, 3, n * P:(n + 1) * P], column, ident[:, :], start=True, stop=True)
            mm.then_inc(s_turned, 1)


def experts(nc, sem, psum, ident, sorted_d, expert_d, w_all, expert, tile_row, part):
    s_in = [sem(f"rows{i}_in") for i in range(8)]
    s_turn, s_hT, s_w = sem("rows_turned"), sem("rowsT_ready"), sem("expert_weights_copied")
    s_gu, s_silu, s_act = sem("expert_gate_up_ready"), sem("expert_silu_ready"), sem("expert_act_ready")
    s_y, s_yout = sem("expert_rows_ready"), sem("expert_rows_copied")
    h_in = [part(RW) for _ in range(8)]
    h_inT = [part(P) for _ in range(4)]
    w_tile = [part(WE) for _ in range(4)]
    silu_e = [part(2 * P) for _ in range(2)]
    act_e = [part(2 * P) for _ in range(2)]
    y_out = [part(P) for _ in range(4)]
    s_told = sem("store_begun")
    s_back = [sem(f"expert_rows{i}_stored") for i in range(4)]
    LOOPS = ET // 8 - 1

    def over_tiles(eng, step):
        for c in range(4):
            step(0, c)
        with eng.Fori(0, LOOPS) as i:
            for c in range(4, 12):
                step(i, c)
        for c in range(4, 8):
            step(LOOPS, c)

    def wait(eng, s, i, per, more):
        if not isinstance(i, int) or per * i + more > 0:
            eng.wait_ge(s, i * per + more)

    def exists(i, c):
        return not isinstance(i, int) or i * 8 + c < ET

    with nc.Block() as block:
        @block.sync
        def _(sp):
            def load(i, c):
                row = sp.value_load(tile_row[0:1, bass.ds(i * 8 + c, 1)], min_val=0, max_val=NE * REGION + NE * P - P)
                sp.dma_start(h_in[c % 8], sorted_d[bass.ds(row, P), :]).then_inc(s_in[c % 8], 16)

            for c in range(8):
                load(0, c)

            with sp.Fori(0, LOOPS) as i:
                for c in range(8):
                    sp.wait_ge(s_back[c % 4], i * 32 + (c // 4) * 16 + 16)
                    load(i, c + 8)

        @block.gpsimd
        def _(pool):
            def step(i, c):
                wait(pool, s_yout, i, 8, c + 1)
                pool.sem_inc(s_told, 1)
                pool.indirect_dma_start(expert_d[:, :],
                                        bass.IndirectOffsetOnAxis(ap=h_in[c % 8][:, E:E + 1].bitcast(I32), axis=0),
                                        y_out[c % 4], None).then_inc(s_back[c % 4], 16)

            over_tiles(pool, step)
            for s in s_back:
                pool.wait_ge(s, 16 * ET // 4)

        @block.scalar
        def _(act):
            def turn(i, c):
                if exists(i, c):
                    wait(act, s_turn, i, 8, c + 1)
                    wait(act, s_gu, i, 8, c - 3)
                    act.activation(h_inT[c % 4], psum[:, c % 2, 0:P], ACT.Copy).then_inc(s_hT, 1)

            def silu(i, c):
                if exists(i, c):
                    wait(act, s_gu, i, 8, c + 1)
                    wait(act, s_act, i, 8, c - 1)
                    act.activation(silu_e[c % 2], psum[:, 2 + c % 2, 0:2 * P], ACT.Silu).then_inc(s_silu, 1)

            def copy_out(i, c):
                wait(act, s_y, i, 8, c + 1)
                wait(act, s_back[c % 4], i, 32, (c // 4) * 16)
                act.activation(y_out[c % 4], psum[:, 4 + c % 2, 0:P], ACT.Copy).then_inc(s_yout, 1)

            def step(i, c):
                turn(i, c + 3)
                silu(i, c + 1)
                copy_out(i, c)

            for c in range(3):
                turn(0, c)
            silu(0, 0)
            over_tiles(act, step)

        @block.vector
        def _(dve):
            def copy_weights(i, c):
                if exists(i, c):
                    e = dve.value_load(expert[0:1, bass.ds(i * 8 + c, 1)], min_val=0, max_val=NE - 1)
                    wait(dve, s_y, i, 8, c - 3)
                    dve.tensor_copy(w_tile[c % 4], w_all[:, bass.ds(e * WE, WE)]).then_inc(s_w, 1)

            def mult(i, c):
                if exists(i, c):
                    wait(dve, s_silu, i, 8, c + 1)
                    wait(dve, s_y, i, 8, c - 1)
                    dve.tensor_tensor(act_e[c % 2], psum[:, 2 + c % 2, 2 * P:4 * P], silu_e[c % 2], ALU.mult).then_inc(s_act, 1)

            def step(i, c):
                copy_weights(i, c + 3)
                mult(i, c + 1)

            for c in range(3):
                copy_weights(0, c)
            mult(0, 0)
            over_tiles(dve, step)

        @block.tensor
        def _(pe):
            def turn(i, c):
                if exists(i, c):
                    wait(pe, s_in[c % 8], i, 16, (c // 8) * 16 + 16)
                    wait(pe, s_hT, i, 8, c - 1)
                    pe.transpose(psum[:, c % 2, 0:P], h_in[c % 8][:, 0:E], ident[:, :]).then_inc(s_turn, 1)

            def gate_up(i, c):
                if exists(i, c):
                    wait(pe, s_hT, i, 8, c + 1)
                    wait(pe, s_w, i, 8, c + 1)
                    wait(pe, s_act, i, 8, c - 1)
                    for f in range(4):
                        mm = pe.matmul(psum[:, 2 + c % 2, f * P:(f + 1) * P], w_tile[c % 4][:, f * P:(f + 1) * P],
                                       h_inT[c % 4], start=True, stop=True)
                    mm.then_inc(s_gu, 1)

            def down(i, c):
                wait(pe, s_act, i, 8, c + 1)
                wait(pe, s_yout, i, 8, c - 1)
                for f in range(2):
                    mm = pe.matmul(psum[:, 4 + c % 2, 0:P], act_e[c % 2][:, f * P:(f + 1) * P],
                                   w_tile[c % 4][:, 2 * F + f * E:2 * F + (f + 1) * E], start=f == 0, stop=f == 1)
                mm.then_inc(s_y, 1)

            def step(i, c):
                turn(i, c + 3)
                gate_up(i, c + 1)
                down(i, c)

            for c in range(3):
                turn(0, c)
            gate_up(0, 0)
            over_tiles(pe, step)


def combine(nc, sem, x_sb, attn_sb, mod_rows, expert_d, out):
    HALVES = 2 * B
    s_got = [sem(f"expert_rows_back{g}") for g in range(HALVES)]
    s_gated = [sem(f"expert_rows_gated{g}") for g in range(HALVES)]
    s_sum, s_out = sem("result_ready"), sem("result_out")
    out_v = out.rearrange("b (c t p) e -> p (b c) t e", c=2, p=P)
    expert_v = expert_d[0:NT * P, :].rearrange("(g t p) e -> p g t e", g=HALVES, p=P)

    def tiles_of(t, g):
        return t[:, 4 * g:4 * g + 4, :]

    def gate(eng, g):
        y = tiles_of(attn_sb, g)
        eng.wait_ge(s_got[g], 16)
        eng.tensor_tensor(y, y, mod_rows[:, g // 2:g // 2 + 1, 3, :].broadcast_to([P, 4, E]), ALU.mult).then_inc(s_gated[g], 1)

    with nc.Block() as block:
        @block.sync
        def _(sp):
            for g in range(0, HALVES, 2):
                sp.dma_start(tiles_of(attn_sb, g), expert_v[:, g]).then_inc(s_got[g], 16)
            for g in range(HALVES):
                sp.wait_ge(s_sum, g + 1)
                sp.dma_start(out_v[:, g], tiles_of(x_sb, g)).then_inc(s_out, 16)
            sp.wait_ge(s_out, 16 * HALVES)

        @block.scalar
        def _(act):
            for g in range(1, HALVES, 2):
                act.dma_start(tiles_of(attn_sb, g), expert_v[:, g]).then_inc(s_got[g], 16)

        @block.gpsimd
        def _(pool):
            for g in range(1, HALVES, 2):
                gate(pool, g)

        @block.vector
        def _(dve):
            for g in range(HALVES):
                if g % 2 == 0:
                    gate(dve, g)
                dve.wait_ge(s_gated[g], 1)
                dve.tensor_tensor(tiles_of(x_sb, g), tiles_of(x_sb, g), tiles_of(attn_sb, g), ALU.add).then_inc(s_sum, 1)


def kernel(L0_attn_hidden_states, L0_attn_Wq, L0_attn_Wk, L0_attn_Wv, L0_attn_Wo, L0_attn_bo, L0_ffn_w_router,
           L0_ffn_gate_up_proj, L0_ffn_down_proj, L0_ffn_w_gate, L0_ffn_w_up, L0_ffn_w_down, L0_c, L0_wmod):
    import numpy as np
    import concourse.bacc as bacc
    from concourse import mybir as mb
    from concourse.bass_utils import run_bass_kernel_spmd as run

    given = [
        ("x", L0_attn_hidden_states), ("wqT", np.transpose(L0_attn_Wq)), ("wkT", np.transpose(L0_attn_Wk)),
        ("wvT", np.transpose(L0_attn_Wv)), ("woT", np.transpose(L0_attn_Wo)), ("bo", L0_attn_bo),
        ("wrT", np.transpose(L0_ffn_w_router)), ("gate_up", L0_ffn_gate_up_proj), ("down", L0_ffn_down_proj),
        ("wgT", np.transpose(L0_ffn_w_gate)), ("wuT", np.transpose(L0_ffn_w_up)), ("wdT", np.transpose(L0_ffn_w_down)),
        ("cT", np.transpose(L0_c)), ("wmod", L0_wmod),
    ]
    nc = bacc.Bacc("TRN2", target_bir_lowering=False, num_devices=1)
    arrays, args = {}, []
    for name, a in given:
        a = np.ascontiguousarray(a)
        arrays[f"{name}_dram"] = a
        args.append(nc.dram_tensor(f"{name}_dram", a.shape, mb.dt.from_np(a.dtype), kind="ExternalInput").ap())
    out = nc.dram_tensor("out_dram", (B, S, E), F32, kind="ExternalOutput").ap()
    adaln_kernel(nc, *args, out)
    r = run(nc, [arrays], core_ids=[0])
    return r.results[0]["out_dram"]
```
